# Optimizing a Trainium2 kernel written in Bass

```python
import numpy as np
import jax
import jax.numpy as jnp

def _softmax(x, axis=-1):
    return jax.nn.softmax(x, axis=axis)

def _gelu(x):
    return jax.nn.gelu(x, approximate=True)

def _silu(x):
    return jax.nn.silu(x)

def _sigmoid(x):
    return jax.nn.sigmoid(x)

def _layernorm(x, axis=-1, eps=1e-05):
    m = jnp.mean(x, axis=axis, keepdims=True)
    v = jnp.var(x, axis=axis, keepdims=True)
    return (x - m) / jnp.sqrt(v + eps)

def _scatter_add(tgt, idx, src, axis=0):
    return tgt.at[idx].add(src)

def _segment_sum(src, seg, n):
    return jax.ops.segment_sum(src, seg, n)
kernel_name = 'mk_lm_tower_d2_tok_ids768_r4_334291'

def setup_inputs(seed: int=0):
    np.random.seed(seed)
    _w = jnp.asarray

    def _rec_inputs():
        import jax
        import jax.numpy as jnp
        _rk = jax.random.key(seed)
        x = jax.random.randint(jax.random.fold_in(_rk, 1), (2, 1024), 0, 127999, jnp.int32)
        return x
    x = _rec_inputs()

    def _L0_tok_setup():
        import jax, jax.numpy as jnp
        import numpy as np
        import math
        VOCAB = 32000
        BASIN_DIM = 64
        D_MODEL = 192
        EPS = 1e-08
        key = jax.random.key(seed)
        k1, k2, k3, k4 = jax.random.split(key, 4)
        token_ids = jax.random.randint(k1, (8, 1024), 0, VOCAB, dtype=jnp.int32)
        coords = jax.random.normal(k2, (VOCAB, BASIN_DIM), dtype=jnp.float32)
        coords = coords / jnp.linalg.norm(coords, axis=-1, keepdims=True)
        coords = coords * (math.sqrt(BASIN_DIM) / 5.0)
        coords = coords + jax.random.normal(k3, coords.shape, dtype=jnp.float32) * 0.01
        w = jax.random.normal(k4, (D_MODEL, BASIN_DIM), dtype=jnp.float32)
        q, _ = jnp.linalg.qr(w)
        proj_w = q * 0.1
        norm_w = jnp.ones((D_MODEL,), dtype=jnp.float32)
        return {'token_ids': token_ids, 'basin_coords': coords, 'proj_w': proj_w, 'norm_w': norm_w}
    _L0_tok_all = _L0_tok_setup()
    _L0_tok_in = {k: v for k, v in _L0_tok_all.items() if k in ('basin_coords', 'proj_w', 'norm_w')}
    del _L0_tok_all

    def _L0_attn_setup():
        import jax, jax.numpy as jnp
        import numpy as np
        B, S, D, H = (16, 256, 192, 12)
        HD = D // H
        key = jax.random.key(seed)
        ks = jax.random.split(key, 9)
        std = 0.02
        x = jax.random.normal(ks[0], (B, S, D), dtype=jnp.float32)
        Wq = std * jax.random.truncated_normal(ks[1], -2.0, 2.0, (D, H, HD), dtype=jnp.float32)
        Wk = std * jax.random.truncated_normal(ks[2], -2.0, 2.0, (D, H, HD), dtype=jnp.float32)
        Wv = std * jax.random.truncated_normal(ks[3], -2.0, 2.0, (D, H, HD), dtype=jnp.float32)
        Wo = std * jax.random.truncated_normal(ks[4], -2.0, 2.0, (H, HD, D), dtype=jnp.float32)
        bq = jnp.zeros((H, HD), dtype=jnp.float32)
        bk = jnp.zeros((H, HD), dtype=jnp.float32)
        bv = jnp.zeros((H, HD), dtype=jnp.float32)
        bo = jnp.zeros((D,), dtype=jnp.float32)
        return {'x': x, 'Wq': Wq, 'bq': bq, 'Wk': Wk, 'bk': bk, 'Wv': Wv, 'bv': bv, 'Wo': Wo, 'bo': bo}
    _L0_attn_all = _L0_attn_setup()
    _L0_attn_in = {k: v for k, v in _L0_attn_all.items() if k in ('Wq', 'bq', 'Wk', 'bk', 'Wv', 'bv', 'Wo', 'bo')}
    del _L0_attn_all

    def _L0_ffn_setup():
        import jax, jax.numpy as jnp
        import numpy as np
        B, S, D, F, E = (4, 512, 192, 768, 8)
        key = jax.random.key(seed)
        ks = jax.random.split(key, 5)
        return {'x': jax.random.normal(ks[0], (B, S, D), dtype=jnp.float32), 'Ws': jax.random.normal(ks[1], (D, E), dtype=jnp.float32) * 0.02, 'bs': jnp.zeros((E,), dtype=jnp.float32), 'W1': jax.random.normal(ks[2], (E, D, F), dtype=jnp.float32) * 0.02, 'b1': jnp.zeros((E, F), dtype=jnp.float32), 'W2': jax.random.normal(ks[3], (E, F, D), dtype=jnp.float32) * 0.02, 'b2': jnp.zeros((E, D), dtype=jnp.float32)}
    _L0_ffn_all = _L0_ffn_setup()
    _L0_ffn_in = {k: v for k, v in _L0_ffn_all.items() if k in ('Ws', 'bs', 'W1', 'b1', 'W2', 'b2')}
    del _L0_ffn_all

    def _L1_attn_setup():
        import jax, jax.numpy as jnp
        import numpy as np
        from jax import lax
        D_MODEL = 192
        D_STATE = 16
        D_CONV = 4
        EXPAND = 2
        D_INNER = EXPAND * D_MODEL
        N = D_STATE // 2
        B_SZ = 8
        SEQ_L = 1024
        key = jax.random.key(seed)
        ks = jax.random.split(key, 8)
        s = 0.02
        return {'x': jax.random.normal(ks[0], (B_SZ, SEQ_L, D_MODEL), jnp.float32), 'W_in': jax.random.normal(ks[1], (D_MODEL, 2 * D_INNER), jnp.float32) * s, 'b_in': jnp.zeros((2 * D_INNER,), jnp.float32), 'conv_w': jax.random.normal(ks[2], (D_INNER, 1, D_CONV), jnp.float32) * s, 'conv_b': jnp.zeros((D_INNER,), jnp.float32), 'W_x': jax.random.normal(ks[3], (D_INNER, 2 * D_STATE), jnp.float32) * s, 'b_x': jnp.zeros((2 * D_STATE,), jnp.float32), 'W_dt': jax.random.normal(ks[4], (D_INNER, D_INNER), jnp.float32) * s, 'b_dt': jnp.zeros((D_INNER,), jnp.float32), 'W_out': jax.random.normal(ks[5], (D_INNER, D_MODEL), jnp.float32) * s, 'b_out': jnp.zeros((D_MODEL,), jnp.float32)}
    _L1_attn_all = _L1_attn_setup()
    _L1_attn_in = {k: v for k, v in _L1_attn_all.items() if k in ('W_in', 'b_in', 'conv_w', 'conv_b', 'W_x', 'b_x', 'W_dt', 'b_dt', 'W_out', 'b_out')}
    del _L1_attn_all

    def _L1_ffn_setup():
        import jax, jax.numpy as jnp
        import numpy as np
        E = 192
        H = 12
        D = E // H
        HID = 768
        NEXP = 4
        TOPK = 2
        EPS = 1e-05

        def _ln(x, g, b):
            m = jnp.mean(x, axis=-1, keepdims=True)
            v = jnp.mean(jnp.square(x - m), axis=-1, keepdims=True)
            return (x - m) * jax.lax.rsqrt(v + EPS) * g + b
        key = jax.random.key(seed)
        ks = jax.random.split(key, 10)
        s = 0.02
        return {'x': jax.random.normal(ks[0], (8, 256, E), jnp.float32), 'ln1_g': jnp.ones((E,), jnp.float32), 'ln1_b': jnp.zeros((E,), jnp.float32), 'in_w': jax.random.normal(ks[1], (3 * E, E), jnp.float32) * s, 'in_b': jnp.zeros((3 * E,), jnp.float32), 'out_w': jax.random.normal(ks[2], (E, E), jnp.float32) * s, 'out_b': jnp.zeros((E,), jnp.float32), 'mlp_w1': jax.random.normal(ks[3], (E, HID), jnp.float32) * s, 'mlp_b1': jnp.zeros((HID,), jnp.float32), 'mlp_w2': jax.random.normal(ks[4], (HID, E), jnp.float32) * s, 'mlp_b2': jnp.zeros((E,), jnp.float32), 'ln2_g': jnp.ones((E,), jnp.float32), 'ln2_b': jnp.zeros((E,), jnp.float32), 'gate_w': jax.random.normal(ks[5], (NEXP, E), jnp.float32) * s, 'gate_b': jnp.zeros((NEXP,), jnp.float32), 'exp_w1': jax.random.normal(ks[6], (NEXP, E, HID), jnp.float32) * s, 'exp_b1': jnp.zeros((NEXP, HID), jnp.float32), 'exp_w2': jax.random.normal(ks[7], (NEXP, HID, E), jnp.float32) * s, 'exp_b2': jnp.zeros((NEXP, E), jnp.float32)}
    _L1_ffn_all = _L1_ffn_setup()
    _L1_ffn_in = {k: v for k, v in _L1_ffn_all.items() if k in ('ln1_g', 'ln1_b', 'in_w', 'in_b', 'out_w', 'out_b', 'mlp_w1', 'mlp_b1', 'mlp_w2', 'mlp_b2', 'ln2_g', 'ln2_b', 'gate_w', 'gate_b', 'exp_w1', 'exp_b1', 'exp_w2', 'exp_b2')}
    del _L1_ffn_all
    return {'x': x, 'L0_tok_basin_coords': _L0_tok_in['basin_coords'], 'L0_tok_proj_w': _L0_tok_in['proj_w'], 'L0_tok_norm_w': _L0_tok_in['norm_w'], 'L0_attn_Wq': _L0_attn_in['Wq'], 'L0_attn_bq': _L0_attn_in['bq'], 'L0_attn_Wk': _L0_attn_in['Wk'], 'L0_attn_bk': _L0_attn_in['bk'], 'L0_attn_Wv': _L0_attn_in['Wv'], 'L0_attn_bv': _L0_attn_in['bv'], 'L0_attn_Wo': _L0_attn_in['Wo'], 'L0_attn_bo': _L0_attn_in['bo'], 'L0_ffn_Ws': _L0_ffn_in['Ws'], 'L0_ffn_bs': _L0_ffn_in['bs'], 'L0_ffn_W1': _L0_ffn_in['W1'], 'L0_ffn_b1': _L0_ffn_in['b1'], 'L0_ffn_W2': _L0_ffn_in['W2'], 'L0_ffn_b2': _L0_ffn_in['b2'], 'L1_attn_W_in': _L1_attn_in['W_in'], 'L1_attn_b_in': _L1_attn_in['b_in'], 'L1_attn_conv_w': _L1_attn_in['conv_w'], 'L1_attn_conv_b': _L1_attn_in['conv_b'], 'L1_attn_W_x': _L1_attn_in['W_x'], 'L1_attn_b_x': _L1_attn_in['b_x'], 'L1_attn_W_dt': _L1_attn_in['W_dt'], 'L1_attn_b_dt': _L1_attn_in['b_dt'], 'L1_attn_W_out': _L1_attn_in['W_out'], 'L1_attn_b_out': _L1_attn_in['b_out'], 'L1_ffn_ln1_g': _L1_ffn_in['ln1_g'], 'L1_ffn_ln1_b': _L1_ffn_in['ln1_b'], 'L1_ffn_in_w': _L1_ffn_in['in_w'], 'L1_ffn_in_b': _L1_ffn_in['in_b'], 'L1_ffn_out_w': _L1_ffn_in['out_w'], 'L1_ffn_out_b': _L1_ffn_in['out_b'], 'L1_ffn_mlp_w1': _L1_ffn_in['mlp_w1'], 'L1_ffn_mlp_b1': _L1_ffn_in['mlp_b1'], 'L1_ffn_mlp_w2': _L1_ffn_in['mlp_w2'], 'L1_ffn_mlp_b2': _L1_ffn_in['mlp_b2'], 'L1_ffn_ln2_g': _L1_ffn_in['ln2_g'], 'L1_ffn_ln2_b': _L1_ffn_in['ln2_b'], 'L1_ffn_gate_w': _L1_ffn_in['gate_w'], 'L1_ffn_gate_b': _L1_ffn_in['gate_b'], 'L1_ffn_exp_w1': _L1_ffn_in['exp_w1'], 'L1_ffn_exp_b1': _L1_ffn_in['exp_b1'], 'L1_ffn_exp_w2': _L1_ffn_in['exp_w2'], 'L1_ffn_exp_b2': _L1_ffn_in['exp_b2']}

def reference(x, L0_tok_basin_coords, L0_tok_proj_w, L0_tok_norm_w, L0_attn_Wq, L0_attn_bq, L0_attn_Wk, L0_attn_bk, L0_attn_Wv, L0_attn_bv, L0_attn_Wo, L0_attn_bo, L0_ffn_Ws, L0_ffn_bs, L0_ffn_W1, L0_ffn_b1, L0_ffn_W2, L0_ffn_b2, L1_attn_W_in, L1_attn_b_in, L1_attn_conv_w, L1_attn_conv_b, L1_attn_W_x, L1_attn_b_x, L1_attn_W_dt, L1_attn_b_dt, L1_attn_W_out, L1_attn_b_out, L1_ffn_ln1_g, L1_ffn_ln1_b, L1_ffn_in_w, L1_ffn_in_b, L1_ffn_out_w, L1_ffn_out_b, L1_ffn_mlp_w1, L1_ffn_mlp_b1, L1_ffn_mlp_w2, L1_ffn_mlp_b2, L1_ffn_ln2_g, L1_ffn_ln2_b, L1_ffn_gate_w, L1_ffn_gate_b, L1_ffn_exp_w1, L1_ffn_exp_b1, L1_ffn_exp_w2, L1_ffn_exp_b2):
    import jax
    import jax.numpy as jnp

    def _L0_tok_ref(token_ids, basin_coords, proj_w, norm_w):
        import jax, jax.numpy as jnp
        import numpy as np
        import math
        VOCAB = 32000
        BASIN_DIM = 64
        D_MODEL = 192
        EPS = 1e-08
        basin = basin_coords[token_ids]
        emb = jnp.einsum('bsk,dk->bsd', basin, proj_w)
        x_f = emb.astype(jnp.float32)
        rms = jnp.sqrt(jnp.mean(x_f * x_f, axis=-1, keepdims=True) + EPS)
        y = (x_f / rms).astype(emb.dtype)
        return y * norm_w

    def _L0_attn_ref(x, Wq, bq, Wk, bk, Wv, bv, Wo, bo):
        import jax, jax.numpy as jnp
        import numpy as np
        B, S, D, H = (16, 256, 192, 12)
        HD = D // H
        q = jnp.einsum('bsd,dhe->bshe', x, Wq) + bq
        k = jnp.einsum('bsd,dhe->bshe', x, Wk) + bk
        v = jnp.einsum('bsd,dhe->bshe', x, Wv) + bv
        scale = 1.0 / jnp.sqrt(jnp.float32(HD))
        z = jnp.einsum('bqhd,bkhd->bhqk', q * scale, k)
        a = jax.nn.softmax(z, axis=-1)
        o = jnp.einsum('bhqk,bkhd->bqhd', a, v)
        return jnp.einsum('bqhd,hde->bqe', o, Wo) + bo

    def _L0_ffn_ref(x, Ws, bs, W1, b1, W2, b2):
        import jax, jax.numpy as jnp
        import numpy as np
        B, S, D, F, E = (4, 512, 192, 768, 8)
        b, s, d = x.shape
        xt = x.reshape(-1, d)
        logits = xt @ Ws + bs
        probs = jax.nn.softmax(logits, axis=-1)
        routes = jnp.argmax(probs, axis=-1)
        prob_max = jnp.max(probs, axis=-1)
        h = jax.nn.gelu(jnp.einsum('td,edf->etf', xt, W1) + b1[:, None, :], approximate=False)
        y = jnp.einsum('etf,efd->etd', h, W2) + b2[:, None, :]
        out = jnp.take_along_axis(y, routes[None, :, None], axis=0)[0]
        out = out * prob_max[:, None]
        return out.reshape(b, s, d)

    def _L1_attn_ref(x, W_in, b_in, conv_w, conv_b, W_x, b_x, W_dt, b_dt, W_out, b_out):
        import jax, jax.numpy as jnp
        import numpy as np
        from jax import lax
        D_MODEL = 192
        D_STATE = 16
        D_CONV = 4
        EXPAND = 2
        D_INNER = EXPAND * D_MODEL
        N = D_STATE // 2
        B_SZ = 8
        SEQ_L = 1024
        B, L, _ = x.shape
        xz = x @ W_in + b_in
        xc, z = jnp.split(xz, 2, axis=-1)
        xt = jnp.transpose(xc, (0, 2, 1))
        xt = lax.conv_general_dilated(xt, conv_w, window_strides=(1,), padding=((D_CONV - 1, 0),), dimension_numbers=('NCH', 'OIH', 'NCH'), feature_group_count=D_INNER)
        xt = xt + conv_b[None, :, None]
        xc = jax.nn.silu(jnp.transpose(xt, (0, 2, 1)))
        delta = jax.nn.softplus(xc @ W_dt + b_dt)[..., :N]
        BC = (xc @ W_x + b_x)[..., D_STATE:]
        Bm, Cm = (BC[..., :N], BC[..., N:])
        decay = jnp.exp(-delta)
        xn = xc[..., :N]

        def step(h, ins):
            d_t, B_t, C_t, x_t = ins
            h = h * d_t[:, None, :] + B_t[:, None, :] * x_t[:, :, None]
            y = jnp.einsum('bj,bij->bi', C_t, h)
            return (h, y)
        tm = lambda a: jnp.transpose(a, (1, 0, 2))
        h0 = jnp.zeros((B, N, N), x.dtype)
        _, ys = lax.scan(step, h0, (tm(decay), tm(Bm), tm(Cm), tm(xn)))
        ys = jnp.transpose(ys, (1, 0, 2))
        ssm_out = jnp.pad(ys, ((0, 0), (0, 0), (0, D_INNER - N)))
        out = ssm_out * jax.nn.silu(z) @ W_out + b_out
        return out

    def _L1_ffn_ref(x, ln1_g, ln1_b, in_w, in_b, out_w, out_b, mlp_w1, mlp_b1, mlp_w2, mlp_b2, ln2_g, ln2_b, gate_w, gate_b, exp_w1, exp_b1, exp_w2, exp_b2):
        import jax, jax.numpy as jnp
        import numpy as np
        E = 192
        H = 12
        D = E // H
        HID = 768
        NEXP = 4
        TOPK = 2
        EPS = 1e-05

        def _ln(x, g, b):
            m = jnp.mean(x, axis=-1, keepdims=True)
            v = jnp.mean(jnp.square(x - m), axis=-1, keepdims=True)
            return (x - m) * jax.lax.rsqrt(v + EPS) * g + b
        B, N, _ = x.shape
        h = _ln(x, ln1_g, ln1_b)
        qkv = h @ in_w.T + in_b
        q, k, v = jnp.split(qkv, 3, axis=-1)
        q = q.reshape(B, N, H, D)
        k = k.reshape(B, N, H, D)
        v = v.reshape(B, N, H, D)
        scores = jnp.einsum('bqhd,bkhd->bhqk', q, k) / jnp.sqrt(jnp.float32(D))
        attn = jax.nn.softmax(scores, axis=-1)
        ctx = jnp.einsum('bhqk,bkhd->bqhd', attn, v).reshape(B, N, E)
        x = x + ctx @ out_w.T + out_b
        x = x + jax.nn.gelu(x @ mlp_w1 + mlp_b1, approximate=False) @ mlp_w2 + mlp_b2
        xm = _ln(x, ln2_g, ln2_b)
        logits = xm @ gate_w.T + gate_b
        topv, topi = jax.lax.top_k(logits, TOPK)
        gates = jax.nn.softmax(topv, axis=-1)
        onehot = jax.nn.one_hot(topi, NEXP, dtype=x.dtype)
        comb = jnp.einsum('bnk,bnke->bne', gates, onehot)
        moe_out = jnp.zeros_like(x)
        for e in range(NEXP):
            he = jax.nn.gelu(xm @ exp_w1[e] + exp_b1[e], approximate=False)
            oe = he @ exp_w2[e] + exp_b2[e]
            moe_out = moe_out + comb[..., e:e + 1] * oe
        return x + moe_out
    h = _L0_tok_ref(x, L0_tok_basin_coords, L0_tok_proj_w, L0_tok_norm_w)
    h = h + _L0_attn_ref(_layernorm(h, axis=-1), L0_attn_Wq, L0_attn_bq, L0_attn_Wk, L0_attn_bk, L0_attn_Wv, L0_attn_bv, L0_attn_Wo, L0_attn_bo)
    h = h + _L0_ffn_ref(_layernorm(h, axis=-1), L0_ffn_Ws, L0_ffn_bs, L0_ffn_W1, L0_ffn_b1, L0_ffn_W2, L0_ffn_b2)
    h = h + _L1_attn_ref(_layernorm(h, axis=-1), L1_attn_W_in, L1_attn_b_in, L1_attn_conv_w, L1_attn_conv_b, L1_attn_W_x, L1_attn_b_x, L1_attn_W_dt, L1_attn_b_dt, L1_attn_W_out, L1_attn_b_out)
    h = h + _L1_ffn_ref(_layernorm(h, axis=-1), L1_ffn_ln1_g, L1_ffn_ln1_b, L1_ffn_in_w, L1_ffn_in_b, L1_ffn_out_w, L1_ffn_out_b, L1_ffn_mlp_w1, L1_ffn_mlp_b1, L1_ffn_mlp_w2, L1_ffn_mlp_b2, L1_ffn_ln2_g, L1_ffn_ln2_b, L1_ffn_gate_w, L1_ffn_gate_b, L1_ffn_exp_w1, L1_ffn_exp_b1, L1_ffn_exp_w2, L1_ffn_exp_b2)
    return h

_drawn_inputs = setup_inputs


def setup_inputs(seed=0):
    import zlib

    import numpy as np

    out = dict(_drawn_inputs(seed))
    spreads = {'L0_tok_norm_w': (1.0, 0.2),
     'L0_attn_bq': (0.0, 0.8),
     'L0_attn_bk': (0.0, 2.0),
     'L0_attn_bv': (0.0, 0.33),
     'L0_attn_bo': (0.0, 0.1),
     'L0_ffn_bs': (0.0, 0.8),
     'L0_ffn_b1': (0.0, 0.8),
     'L0_ffn_b2': (0.0, 0.427),
     'L1_attn_b_in': (0.0, 0.8),
     'L1_attn_conv_b': (0.0, 0.8),
     'L1_attn_b_x': (0.0, 0.8),
     'L1_attn_b_dt': (0.0, 0.8),
     'L1_attn_b_out': (0.0, 0.8),
     'L1_ffn_ln1_g': (1.0, 0.6),
     'L1_ffn_ln1_b': (0.0, 2.0),
     'L1_ffn_in_b': (0.0, 2.0),
     'L1_ffn_out_b': (0.0, 0.8),
     'L1_ffn_mlp_b1': (0.0, 2.0),
     'L1_ffn_mlp_b2': (0.0, 0.8),
     'L1_ffn_ln2_g': (1.0, 0.6),
     'L1_ffn_ln2_b': (0.0, 2.0),
     'L1_ffn_gate_b': (0.0, 2.0),
     'L1_ffn_exp_b1': (0.0, 2.0),
     'L1_ffn_exp_b2': (0.0, 0.8)}
    factors = {'L0_attn_Wq': 8.0,
     'L0_attn_Wk': 8.0,
     'L0_ffn_Ws': 4.968,
     'L0_ffn_W1': 3.986,
     'L0_ffn_W2': 3.76,
     'L1_attn_W_in': 8.0,
     'L1_attn_conv_w': 8.0,
     'L1_attn_W_x': 8.0,
     'L1_attn_W_dt': 8.0,
     'L1_attn_W_out': 8.0,
     'L1_ffn_in_w': 8.0,
     'L1_ffn_out_w': 8.0,
     'L1_ffn_mlp_w1': 8.0,
     'L1_ffn_mlp_w2': 8.0,
     'L1_ffn_gate_w': 8.0,
     'L1_ffn_exp_w1': 8.0,
     'L1_ffn_exp_w2': 8.0}
    for name, (base, spread) in spreads.items():
        noise = np.random.default_rng([zlib.crc32(name.encode()), seed]).standard_normal(out[name].shape)
        drawn = base * np.exp(spread * noise) if base else spread * noise
        out[name] = jnp.asarray(drawn.astype(out[name].dtype))
    for name, factor in factors.items():
        out[name] = (out[name] * factor).astype(out[name].dtype)
    return out
```

```python
from contextlib import ExitStack

import concourse.bass as bass
from concourse import mybir

F32 = mybir.dt.float32
BF16 = mybir.dt.bfloat16
F16 = mybir.dt.float16
I32 = mybir.dt.int32
ALU = mybir.AluOpType
ACT = mybir.ActivationFunctionType
AX = mybir.AxisListType.X

P = 128
B, S, D = 2, 1024, 192
T = B * S
DC, DH = 2, 96
G = 512
NG = T // G
NB = T // P
VOCAB, BASIN = 32000, 64
HEADS, HD = 12, 16
NH = B * HEADS
TERMS = 6
KA = TERMS * HD
KM = KA + 3
FF, FC = 768, 6
E0, E1 = 8, 4
DI, IC = 384, 3
NS = 8

C96 = {}
for _n in ("bq0", "bk0", "ln1_g", "ln1_b", "bq1", "bk1", "ln2_g", "ln2_b"):
    C96[_n] = 2 * len(C96)
N96 = 2 * len(C96)
C128 = {"b_in": 0, "conv_b": 3, "conv_w": 6, "mlp_b1": 18}
N128 = 24
ROW = {"bv0": 0, "bv1": D, "bo0": 2 * D, "bo1": 3 * D, "b_out": 4 * D, "mlp_b2": 5 * D, "norm_w": 6 * D, "bs": 7 * D, "gb": 7 * D + E0}
NROW = 7 * D + E0 + E1

RECURRING = [
    "b2_added", "b2_weighted", "bo_added", "cxT_ready", "cx_turned", "exp_done", "exp_router", "gates", "gates_rows",
    "gates_turned", "kq_0", "kq_1", "kq_2", "kq_3", "ln_done", "ln_dve", "ln_root", "ln_scaled", "ln_turned",
    "ln_var", "lo_d", "lo_p", "logits", "max_part", "max_split", "max_taken", "max_turned", "mlp_added",
    "mlp_b2_added", "mlp_down", "mlp_gcol", "mlp_gelu", "mlp_up", "mlp_w0", "mlp_w1", "mrow_0", "mrow_1", "mrow_2",
    "mrow_3", "norm_done", "norm_dve", "norm_hi", "o_evac", "o_turned", "pv_done", "qk_evac", "qk_hi", "qk_lo",
    "qk_mid", "qk_projected", "qk_rest", "qk_stored", "router_dve", "shifted", "sk_done", "sq_done", "v_evac", "v_hi",
    "v_lo", "v_projected", "vs_ready", "vs_zeroed", "wo_added", "wo_projected",
]

STOP = None


class Chain:

    def __init__(self, eng, sem, base=0):
        self.eng, self.sem, self.base, self.n = eng, sem, base, 0

    def __call__(self, ins):
        self.n += 1
        ins.then_inc(self.sem, 1)
        self.eng.wait_ge(self.sem, self.base + self.n)


def build(nc, A, out, stop):
    ctx = ExitStack()
    with ctx:
        def sb(name, shape, dt):
            return ctx.enter_context(nc.sbuf_tensor(name, shape, dt))

        sems = {}

        def sem(name):
            if name not in sems:
                sems[name] = ctx.enter_context(nc.semaphore(name))
            return sems[name]

        for name in RECURRING:
            sem(name)
        numbers = [sems[name].num for name in RECURRING]
        assert numbers == list(range(numbers[0], numbers[0] + len(numbers)))

        def clear(k):
            def wait(eng):
                eng.wait_ge(sem("cleared"), k)
            return dict(sp=lambda e: e.sem_clear(range(numbers[0], numbers[-1] + 1)).then_inc(sem("cleared"), 1),
                        pe=wait, act=wait, dve=wait, pool=wait)

        def dram(name, shape, dt):
            return nc.dram_tensor(name, shape, dt, kind="Internal").ap()

        ps = [ctx.enter_context(nc.psum_tensor(f"bank{i}", [P, 512], F32)) for i in range(0)]
        PS = ctx.enter_context(nc.psum_tensor("PS", [P, 8, 512], F32))
        H = sb("H", [P, NB, D], F32)
        XN = sb("XN", [DH, DC, T], F32)
        c96 = sb("c96", [DH, N96], F32)
        c128 = sb("c128", [P, N128], F32)
        rows = sb("rows", [P, NROW], F32)
        ident = sb("ident", [P, P], F32)
        epsc = sb("epsc", [P, 2], F32)
        projT = sb("projT", [BASIN, D], F32)
        wqkv = [sb(f"wqkv{l}", [DH, DC, 3 * D], F32) for l in range(2)]
        wo = [sb(f"wo{l}", [DH, DC, D], F32) for l in range(2)]
        wr = [sb(f"wr{l}", [DH, DC, E], F32) for l, E in enumerate((E0, E1))]
        b2 = [sb(f"b2{l}", [E, D], F32) for l, E in enumerate((E0, E1))]
        order = sb("order", [P, E0], F32)
        w_in = sb("w_in", [DH, DC, DI + NS], F32)
        w_x = sb("w_x", [P, IC, 72], F32)
        b_x = sb("b_x", [72, 1], F32)
        b_z = sb("b_z", [NS, 1], F32)
        w_out = sb("w_out", [NS, D], F32)
        ssum = sb("ssum", [P, 2, NS], F32)
        ARENA = 38048
        arena = sb("arena", [P, ARENA], F32)
        cur = [0]

        def at(shape, dt, reset=None):
            if reset is not None:
                cur[0] = reset
            n = 1
            for s in shape[1:]:
                n *= s
            words = n if dt in (F32, I32) else (n + 1) // 2
            o = cur[0]
            cur[0] += words
            assert cur[0] <= ARENA, (cur[0], ARENA)
            v = arena[0:shape[0], o:o + words]
            if dt != F32:
                v = v.bitcast(dt)
            if len(shape) > 2:
                names = "abcdef"[:len(shape) - 1]
                v = v.rearrange(f"p ({' '.join(names)}) -> p {' '.join(names)}", **{k: s for k, s in zip(names, shape[1:])})
            return v

        idx_in = at([P, NB], I32, 0)
        idx_f = at([P, NB], F32)
        idx_w = at([P, NB], F32)
        idx = at([P, NB], I32)
        emb = at([P, NB, BASIN], F32)
        embT = at([BASIN, T], F32)
        sq_e = at([P, D], F32)
        ms_e = at([P, NB], F32)
        rr_e = at([P, NB], F32)
        XT = at([P, NB, D], F32, 0)
        ST = at([P, NB, 6], F32)
        MV = at([P, NB, 2], F32)
        RS = at([P, NB], F32)
        RI = at([P, NB], F32)
        VC = at([P, NH, 8, 2, HD], BF16, 0)
        VS = at([P, 2, 8, 2, P], BF16)
        KQ = [[at([KM, S], BF16) for _ in range(4)] for _ in range(2)]
        MX = at([P, 4, 8], F32)
        MT = at([8, P], F32)
        MR = at([8, P], F32)
        MR2 = at([8, P], F32)
        MP = at([8, 4, 3, P], BF16)
        OS = at([P, 2, S], F32)
        RC = at([P, 8, 2], F32)
        CM = at([P, 8, 32], F32)
        CH = at([P, 8, 32], F32)
        CX = at([P, 8, B * D], F32)
        CXT = at([DH, DC, T], F32)
        attn_end = cur[0]
        W1s = at([DH, 2, DC, FF], F32, 4096)
        W2s = at([P, 2, FC, D], F32)
        B1s = at([P, 2, FC], F32)
        HT = at([P, 2, FC, G], F32)
        GC = at([P, 2, NB], F32)
        LG = at([P, NB, E0], F32)
        L2 = at([P, NB, E0], F32)
        EX = at([P, NB, E0], F32)
        SEL = at([P, NB, E0], F32)
        GT = at([P, NB, E0], F32)
        t1 = at([P, NB], F32)
        t2 = at([P, NB], F32)
        t3 = at([P, NB], F32)
        GTT = at([E0, T], F32)
        XC = at([P, IC, B, S + 3], F32, 4096)
        XV = at([P, IC, T], F32)
        XS = at([P, IC, T], F32)
        RT = at([72, T], F32)
        ZT = at([NS, T], F32)
        ZS = at([NS, T], F32)
        YG = at([NS, T], F32)
        REP = [at([P, S], F32) for _ in range(4)]
        UU = at([P, S], F32)
        HH = at([P, S], F32)
        q32 = at([DH, 4, G], F32, attn_end)
        r32 = at([DH, 4, G], F32)
        v32 = at([P, 4, D], F32)
        mark = cur[0]
        PR = at([P, 8, S], F32, mark)
        LO = at([P, 8, S], F16)
        parts = at([DH, 2, 3, DC, T], BF16, mark)

        QK = [[dram(f"{n}parts{l}", [NH, TERMS, HD, S], BF16) for n in "kq"] for l in range(2)]

        block = ctx.enter_context(nc.Block())
        nphase = [0]

        def barrier(eng, k):
            s = sem("phase_left")
            eng.drain().then_inc(s, 1)
            eng.wait_ge(s, 5 * k)

        class Stage:
            pass

        LOADS = [(c96[:, :], A["c96"]), (c128[:, :], A["c128"]), (rows[:, :], A["rows"]),
                 (ident[:, :], A["ident"]), (projT[:, :], A["projT"]),
                 (wqkv[0][:, :, :], A["wqkv0"]), (wo[0][:, :, :], A["wo0"]),
                 (wqkv[1][:, :, :], A["wqkv1"]), (wo[1][:, :, :], A["wo1"]),
                 (wr[0][:, :, :], A["wr0"]), (wr[1][:, :, :], A["wr1"]), (b2[0][:, :], A["b20"]), (b2[1][:, :], A["b21"]),
                 (order[:, :], A["order"]), (w_in[:, :, :], A["w_in"]), (w_x[:, :, :], A["w_x"]), (b_x[:, :], A["b_x"]),
                 (b_z[:, :], A["b_z"]), (w_out[:, :], A["w_out"]), (ssum[:, :, :], A["ssum"])]

        def embed_sp(sp):
            sp.dma_start(idx_in[:, :], A["x"]).then_inc(sem("idx_loaded"), 16)
            for dst, src in LOADS:
                sp.dma_start(dst, src).then_inc(sem("consts"), 16)

        def consts_loaded(eng):
            eng.wait_ge(sem("consts"), 16 * len(LOADS))

        def embed_dve(v):
            v.memset(epsc[:, 0:1], 1e-5)
            v.memset(epsc[:, 1:2], 1e-8).then_inc(sem("eps_set"), 1)
            c = Chain(v, sem("embed_dve"))
            v.wait_ge(sem("idx_loaded"), 16)
            c(v.tensor_scalar(idx_w[:, :], idx_in[:, :], 0.0, float(VOCAB), ALU.is_lt, ALU.mult))
            c(v.tensor_tensor(idx_f[:, :], idx_in[:, :], idx_w[:, :], ALU.add))
            v.tensor_scalar(idx[:, :], idx_f[:, :], 0.0, float(VOCAB - 1), ALU.max, ALU.min).then_inc(sem("idx_ready"), 1)
            consts_loaded(v)
            for g in range(NG):
                v.wait_ge(sem("embT_turned"), g + 1)
                v.tensor_copy(embT[:, g * G:(g + 1) * G], PS[0:BASIN, g, :]).then_inc(sem("embT_ready"), 1)
                for b in range(4 * g, 4 * g + 4):
                    v.wait_ge(sem("emb_projected"), b + 1)
                    v.tensor_copy(H[:, b, :], PS[:, 4 + b % 4, 0:D]).then_inc(sem("emb_evac"), 1)
            v.wait_ge(sem("rms_root"), 1)
            c(v.reciprocal(rr_e[:, :], rr_e[:, :]))
            o = ROW["norm_w"]
            for b in range(NB):
                last = v.scalar_tensor_tensor(H[:, b, :], H[:, b, :], rr_e[:, b:b + 1], rows[:, o:o + D], ALU.mult, ALU.mult)
            last.then_inc(sem("H_embedded"), 1)

        def embed_pool(pool):
            pool.wait_ge(sem("idx_ready"), 1)
            for blk in range(NB):
                pool.indirect_dma_start(emb[:, blk, :], None, A["coords"], bass.IndirectOffsetOnAxis(ap=idx[:, blk:blk + 1], axis=0)).then_inc(sem(f"gathered{blk // 4}"), 16)

        def embed_pe(pe):
            consts_loaded(pe)
            for g in range(NG):
                for q in range(4):
                    blk = 4 * g + q
                    pe.wait_ge(sem(f"gathered{g}"), 64)
                    last = pe.transpose(PS[0:BASIN, g, q * P:(q + 1) * P], emb[:, blk, :], ident[:, :])
                last.then_inc(sem("embT_turned"), 1)
            for b in range(NB):
                pe.wait_ge(sem("embT_ready"), b // 4 + 1)
                if b >= 4:
                    pe.wait_ge(sem("emb_evac"), b - 3)
                pe.matmul(PS[:, 4 + b % 4, 0:D], embT[:, b * P:(b + 1) * P], projT[:, :], start=True, stop=True)\
                  .then_inc(sem("emb_projected"), 1)

        def embed_act(act):
            c = Chain(act, sem("embed_act"))
            for b in range(NB):
                act.wait_ge(sem("emb_evac"), b + 1)
                c(act.activation(sq_e[:, :], H[:, b, :], ACT.Square, accum_out=ms_e[:, b:b + 1]))
            act.wait_ge(sem("eps_set"), 1)
            act.activation(rr_e[:, :], ms_e[:, :], ACT.Sqrt, bias=epsc[:, 1:2], scale=1.0 / D).then_inc(sem("rms_root"), 1)

        def ln_dve(v, n):
            c = Chain(v, sem("ln_dve"))
            for b in range(NB):
                last = v.bn_stats(ST[:, b, :], H[:, b, :])
            c(last)
            for b in range(NB):
                last = v.bn_aggr(MV[:, b, :], ST[:, b, :])
            last.then_inc(sem("ln_var"), 1)
            v.wait_ge(sem("ln_root"), 1)
            c(v.reciprocal(RI[:, :], RS[:, :]))
            for b in range(NB):
                v.tensor_scalar(XT[:, b, :], H[:, b, :], MV[:, b, 0:1], RI[:, b:b + 1], ALU.subtract, ALU.mult)\
                 .then_inc(sem("ln_scaled"), 1)

        def ln_act(act, n, gain=None, bias=None):
            act.wait_ge(sem("ln_var"), 1)
            act.activation(RS[:, :], MV[:, :, 1], ACT.Sqrt, bias=epsc[:, 0:1]).then_inc(sem("ln_root"), 1)
            for j in range(NG * DC):
                g, k = j // DC, j % DC
                act.wait_ge(sem("ln_turned"), j + 1)
                dst, src = XN[:, k, g * G:(g + 1) * G], PS[0:DH, j, :]
                if gain is None:
                    ins = act.activation(dst, src, ACT.Copy)
                else:
                    ins = act.activation(dst, src, ACT.Identity, scale=c96[:, C96[gain] + k:C96[gain] + k + 1],
                                         bias=c96[:, C96[bias] + k:C96[bias] + k + 1])
                ins.then_inc(sem("ln_done"), 1)

        def ln_pe(pe, n):
            for j in range(NG * DC):
                g, k = j // DC, j % DC
                for q in range(4):
                    b = 4 * g + q
                    pe.wait_ge(sem("ln_scaled"), b + 1)
                    last = pe.transpose(PS[0:DH, j, q * P:(q + 1) * P], XT[:, b, k * DH:(k + 1) * DH], ident[:, :])
                last.then_inc(sem("ln_turned"), 1)

        NJ = 4 * NG

        def job(j):
            return j // 4, (j // 2) % 2, j % 2

        def qkv_pe(pe, l, n):
            for j in range(NJ):
                g, qk, ch = job(j)
                pe.wait_ge(sem("ln_done"), 2 * g + 2)
                if j >= 4:
                    pe.wait_ge(sem("qk_evac"), j - 3)
                col = (1 - qk) * D + ch * DH
                for k in range(DC):
                    last = pe.matmul(PS[0:DH, j % 4, :], wqkv[l][:, k, col:col + DH], XN[:, k, g * G:(g + 1) * G],
                                     start=k == 0, stop=k == 1)
                last.then_inc(sem("qk_projected"), 1)
            for b in range(NB):
                if b >= 4:
                    pe.wait_ge(sem("v_evac"), b - 3)
                for k in range(DC):
                    last = pe.matmul(PS[:, 4 + b % 4, 0:D], XN[:, k, b * P:(b + 1) * P], wqkv[l][:, k, 2 * D:3 * D],
                                     start=k == 0, stop=k == 1)
                last.then_inc(sem("v_projected"), 1)

        def qkv_dve(v, l):
            for s in range(4):
                v.memset(KQ[0][s][KA:KM, :], -1.0)
            v.memset(VS[:, :, :, :, 0:64], 0.0)
            v.memset(VS[:, :, :, :, 64:P], 0.0).then_inc(sem("vs_zeroed"), 1)
            v.wait_ge(sem("vs_zeroed"), 1)
            v.memset(VS[:, :, :, 0, 64:80], 1.0)
            v.memset(VS[:, :, :, 0, 96:112], 1.0)
            v.memset(VS[:, :, :, 1, 80:96], 1.0)
            v.memset(VS[:, :, :, 1, 112:128], 1.0).then_inc(sem("vs_zeroed"), 1)
            for j in range(NJ):
                g, qk, ch = job(j)
                v.wait_ge(sem("qk_projected"), j + 1)
                if j >= 4:
                    v.wait_ge(sem("qk_rest"), j - 3)
                o = C96[("bk", "bq")[qk] + str(l)] + ch
                v.tensor_scalar(q32[:, j % 4, :], PS[0:DH, j % 4, :], c96[:, o:o + 1], (1.0, HD ** -0.5)[qk],
                                ALU.add, ALU.mult).then_inc(sem("qk_evac"), 1)
            for b in range(NB):
                v.wait_ge(sem("v_projected"), b + 1)
                if b >= 4:
                    v.wait_ge(sem("v_lo"), b - 3)
                o = ROW[f"bv{l}"]
                v.tensor_tensor(v32[:, b % 4, :], PS[:, 4 + b % 4, 0:D], rows[:, o:o + D], ALU.add).then_inc(sem("v_evac"), 1)

        def part(j, n):
            g, qk, ch = job(j)
            return parts[:, qk, n, ch, g * G:(g + 1) * G]

        def vpart(b, n):
            return VC[:, b // 8 * HEADS:(b // 8 + 1) * HEADS, b % 8, n, :]

        def heads(ap):
            return ap.rearrange("p (h d) -> p h d", h=HEADS)

        def qkv_act(act, l):
            for j in range(NJ + 1):
                if j < NJ:
                    act.wait_ge(sem("qk_evac"), j + 1)
                    act.activation(part(j, 0), q32[:, j % 4, :], ACT.Copy).then_inc(sem("qk_hi"), 1)
                if j >= 1:
                    act.wait_ge(sem("qk_rest"), j)
                    act.activation(part(j - 1, 1), r32[:, (j - 1) % 4, :], ACT.Copy).then_inc(sem("qk_mid"), 1)
            for b in range(NB):
                act.wait_ge(sem("v_evac"), b + 1)
                act.activation(vpart(b, 0), heads(v32[:, b % 4, :]), ACT.Copy).then_inc(sem("v_hi"), 1)

        def qkv_pool(pool, l):
            for j in range(NJ + 1):
                if j < NJ:
                    pool.wait_ge(sem("qk_hi"), j + 1)
                    if j >= 4:
                        pool.wait_ge(sem("qk_lo"), j - 3)
                    pool.tensor_tensor(r32[:, j % 4, :], q32[:, j % 4, :], part(j, 0), ALU.subtract).then_inc(sem("qk_rest"), 1)
                if j >= 1:
                    pool.wait_ge(sem("qk_mid"), j)
                    pool.tensor_tensor(part(j - 1, 2), r32[:, (j - 1) % 4, :], part(j - 1, 1), ALU.subtract)\
                        .then_inc(sem("qk_lo"), 1)
            for b in range(NB):
                pool.wait_ge(sem("v_hi"), b + 1)
                pool.tensor_tensor(vpart(b, 1), heads(v32[:, b % 4, :]), vpart(b, 0), ALU.subtract).then_inc(sem("v_lo"), 1)

        TERM = [(0, 0), (1, 0), (0, 1), (1, 1), (2, 0), (0, 2)]

        def qkv_sp(sp, l):
            for b in range(B):
                sp.wait_ge(sem("qk_lo"), 8 * (b + 1))
                for qk in range(2):
                    for ch in range(DC):
                        h0 = b * HEADS + 6 * ch
                        for t in range(TERMS):
                            sp.dma_start(QK[l][qk][h0:h0 + 6, t], parts[:, qk, TERM[t][qk], ch, b * S:(b + 1) * S])\
                              .then_inc(sem("qk_stored"), 16)
            sp.wait_ge(sem("qk_stored"), 16 * B * 2 * DC * TERMS)

        NV = 8 * NH
        ALEAD, BLEAD = 15, 4
        ON_DVE = (3, 7)
        lo_rank = {}
        cnt = {"d": 0, "p": 0}
        for r in range(8):
            w = "d" if r in ON_DVE else "p"
            cnt[w] += 1
            lo_rank[r] = (w, cnt[w])

        def steps(eng, body):
            body(0, 0)
            with eng.Fori(1, NV // 32 - 1) as i:
                body(i, None)
            body(NV // 32 - 1, NV - 32)

        def attn_pe(pe, l):
            def scores_q(i, x):
                s, qb = x // 8 % 4, x % 8
                if qb == 0:
                    pe.wait_ge(sem(f"kq_{s}"), 32 * i + 32 * (x // 32 + 1))
                if qb == 0 and not (isinstance(i, int) and 32 * i + x == 0):
                    pe.wait_ge(sem("max_taken"), 4 * i + x // 8)
                if not (isinstance(i, int) and 32 * i + x == 0):
                    pe.wait_ge(sem("max_part"), 32 * i + x)
                for half in range(2):
                    last = pe.matmul(PS[:, half, :], KQ[1][s][0:KA, qb * P:(qb + 1) * P],
                                     KQ[0][s][0:KA, half * 512:(half + 1) * 512], start=True, stop=True)
                last.then_inc(sem("sq_done"), 1)

            def turn_max(i, h):
                pe.wait_ge(sem("max_part"), 32 * i + 8 * (h + 1))
                pe.transpose(PS[0:8, 0, 0:P], MX[:, h % 4, :], ident[:, :]).then_inc(sem("max_turned"), 1)

            def scores_k(i, x):
                s, kb = x // 8 % 4, x % 8
                if kb == 0:
                    pe.wait_ge(sem(f"mrow_{s}"), 48 * i + 48 * (x // 32 + 1))
                if not (isinstance(i, int) and 32 * i + x < 2):
                    pe.wait_ge(sem("exp_done"), 32 * i + x - 1)
                for half in range(2):
                    last = pe.matmul(PS[:, 2 + 2 * (x % 2) + half, :], KQ[0][s][:, kb * P:(kb + 1) * P],
                                     KQ[1][s][:, half * 512:(half + 1) * 512], start=True, stop=True)
                last.then_inc(sem("sk_done"), 1)

            def values(i, x):
                s, kb, pair = x // 8 % 2, x % 8, x // 16
                first, lastt = x % 16 == 0, x % 16 == 15
                if first:
                    pe.wait_ge(sem("vs_ready"), 2 * i + pair + 1)
                    if not (isinstance(i, int) and i == 0 and pair == 0):
                        pe.wait_ge(sem("o_evac"), 2 * i + pair)
                w, r = lo_rank[x % 8]
                pe.wait_ge(sem(f"lo_{w}"), 4 * cnt[w] * i + x // 8 * cnt[w] + r)
                lhsT = VS[:, pair, kb, s, :]
                hi = PR[:, x % 8, :].bitcast(BF16).rearrange("p (n two) -> p n two", two=2)
                for q in range(2):
                    pe.matmul(PS[:, 6 + q, :], lhsT, hi[:, q * 512:(q + 1) * 512, 1], start=first, stop=False)
                for q in range(2):
                    last = pe.matmul(PS[:, 6 + q, :], lhsT, LO[:, x % 8, q * 512:(q + 1) * 512], start=False, stop=lastt)
                last.then_inc(sem("pv_done"), 1)

            def turn_out(i, pair):
                if isinstance(i, int) and 2 * i + pair < 0:
                    return
                pe.wait_ge(sem("o_evac"), 2 * i + pair + 1)
                for k in range(8):
                    last = pe.transpose(PS[:, k // 4, k % 4 * P:(k % 4 + 1) * P], OS[:, pair % 2, k * P:(k + 1) * P], ident[:, :])
                last.then_inc(sem("o_turned"), 1)

            for a in range(ALEAD):
                if a and a % 8 == 0:
                    turn_max(0, a // 8 - 1)
                scores_q(0, a)
            for b in range(BLEAD):
                scores_k(0, b)

            def body(i, v0):
                for x in range(32):
                    if v0 is None or v0 + x + BLEAD < NV:
                        scores_k(i, x + BLEAD)
                    if v0 is None or v0 + x + ALEAD <= NV:
                        if (x + ALEAD) % 8 == 0:
                            turn_max(i, (x + ALEAD) // 8 - 1)
                    if x % 16 == 6:
                        if not (isinstance(i, int) and 2 * i + x // 16 == 0):
                            if v0 is None or v0 + x + ALEAD <= NV:
                                pe.wait_ge(sem("max_part"), 32 * i + x + ALEAD)
                        turn_out(i, x // 16 - 1)
                    if v0 is None or v0 + x + ALEAD < NV:
                        if x % 16 == 6 and not (isinstance(i, int) and 2 * i + x // 16 == 0):
                            pe.wait_ge(sem("norm_done"), 2 * i + x // 16)
                        scores_q(i, x + ALEAD)
                    values(i, x)

            steps(pe, body)
            turn_out(NV // 32 - 1, 1)

        def attn_act(act, l):
            def evac(i, pair):
                first = isinstance(i, int) and 2 * i + pair < 0
                if first:
                    return
                act.wait_ge(sem("pv_done"), 32 * i + 16 * (pair + 1))
                if not (isinstance(i, int) and 2 * i + pair < 2):
                    act.wait_ge(sem("o_turned"), 2 * i + pair - 1)
                act.activation(OS[:, pair % 2, :].rearrange("p (a b) -> p a b", a=2), PS[:, 6:8, :], ACT.Copy)\
                   .then_inc(sem("o_evac"), 1)

            def body(i, v0):
                for x in range(32):
                    act.wait_ge(sem("sk_done"), 32 * i + x + 1)
                    if not (isinstance(i, int) and 32 * i + x < 8):
                        act.wait_ge(sem("pv_done"), 32 * i + x - 7)
                    act.activation(PR[:, x % 8, :].rearrange("p (a b) -> p a b", a=2),
                                   PS[:, 2 + 2 * (x % 2):4 + 2 * (x % 2), :], ACT.Exp).then_inc(sem("exp_done"), 1)
                    if x % 16 == 3:
                        evac(i, x // 16 - 1)

            steps(act, body)
            evac(NV // 32 - 1, 1)

        def lo_part(eng, l, i, x, w):
            eng.wait_ge(sem("exp_done"), 32 * i + x + 1)
            if not (isinstance(i, int) and 32 * i + x < 8):
                eng.wait_ge(sem("pv_done"), 32 * i + x - 7)
            hi = PR[:, x % 8, :].bitcast(BF16).rearrange("p (n two) -> p n two", two=2)[:, :, 1]
            eng.tensor_tensor(LO[:, x % 8, :], PR[:, x % 8, :], hi, ALU.subtract).then_inc(sem(f"lo_{w}"), 1)

        def attn_pool(pool, l):
            def body(i, v0):
                for x in range(32):
                    if lo_rank[x % 8][0] == "p":
                        lo_part(pool, l, i, x, "p")
            steps(pool, body)

        def attn_dve(v, l):
            def reduce_max(i, x):
                v.wait_ge(sem("sq_done"), 32 * i + x + 1)
                v.tensor_reduce(MX[:, x // 8 % 4, x % 8:x % 8 + 1], PS[:, 0:2, :], mybir.AxisListType.XY, ALU.max)\
                 .then_inc(sem("max_part"), 1)

            def max_rows(i, h):
                c = Chain(v, sem("max_split"), 16 * i + 4 * h)
                v.wait_ge(sem("max_turned"), 4 * i + h + 1)
                v.tensor_copy(MT[:, :], PS[0:8, 0, 0:P]).then_inc(sem("max_taken"), 1)
                v.wait_ge(sem("max_taken"), 4 * i + h + 1)
                if not (isinstance(i, int) and 4 * i + h < 4):
                    v.wait_ge(sem(f"mrow_{h % 4}"), 48 * i + 48 * (h // 4))
                m = [MP[:, h % 4, n, :] for n in range(3)]
                c(v.tensor_copy(m[0], MT[:, :]))
                c(v.tensor_tensor(MR[:, :], MT[:, :], m[0], ALU.subtract))
                c(v.tensor_copy(m[1], MR[:, :]))
                c(v.tensor_tensor(m[2], MR[:, :], m[1], ALU.subtract))

            def copy_values(i, pair):
                for s in range(2):
                    dst = VS[:, pair % 2, :, s, 0:64].rearrange("p k (n c) -> p k n c", n=2)[:, :, :, s * HD:(s + 1) * HD]
                    h = 2 * pair + s
                    if isinstance(i, int):
                        src = VC[:, 4 * i + h]
                    else:
                        src = VC[:, bass.ds(4 * i + h, 1)].rearrange("p o k n c -> p (o k) n c")
                    last = v.tensor_copy(dst, src)
                last.then_inc(sem("vs_ready"), 1)

            def cx_at(i, pair):
                if isinstance(i, int):
                    return CX[:, :, 32 * (2 * i + pair):32 * (2 * i + pair) + 32]
                return CX[:, :, bass.ds(64 * i + 32 * pair, 32)]

            def normalise(i, pair):
                if isinstance(i, int) and 2 * i + pair < 0:
                    return
                v.wait_ge(sem("o_turned"), 2 * i + pair + 1)
                c = Chain(v, sem("norm_dve"), 4 * i + 2 * pair)
                t = PS[:, 0:2, :].rearrange("p a (k n) -> p (a k) n", n=P)
                c(v.reciprocal(RC[:, :, :], t[:, :, 64:96].rearrange("p k (h d) -> p k h d", h=2)[:, :, :, 0]))
                w = RC[:, :, :].unsqueeze(3).broadcast_to([P, 8, 2, HD])
                c(v.tensor_tensor(CM[:, :, :].rearrange("p k (h d) -> p k h d", h=2),
                                  t[:, :, 32:64].rearrange("p k (h d) -> p k h d", h=2), w, ALU.mult))
                dst = cx_at(i, pair)
                c2 = Chain(v, sem("norm_hi"), 2 * i + pair)
                c2(v.tensor_tensor(CH[:, :, :].rearrange("p k (h d) -> p k h d", h=2),
                                   t[:, :, 0:32].rearrange("p k (h d) -> p k h d", h=2), w, ALU.mult))
                v.tensor_tensor(dst, CH[:, :, :], CM[:, :, :], ALU.add).then_inc(sem("norm_done"), 1)
                v.wait_ge(sem("norm_done"), 2 * i + pair + 1)

            v.wait_ge(sem("v_lo"), NB)
            v.wait_ge(sem("vs_zeroed"), 2)
            copy_values(0, 0)
            for a in range(ALEAD):
                if a and a % 8 == 0:
                    max_rows(0, a // 8 - 1)
                reduce_max(0, a)

            def body(i, v0):
                for x in range(32):
                    if v0 is None or v0 + x + ALEAD <= NV:
                        if (x + ALEAD) % 8 == 0:
                            max_rows(i, (x + ALEAD) // 8 - 1)
                    if x % 16 == 6:
                        normalise(i, x // 16 - 1)
                    if v0 is None or v0 + x + ALEAD < NV:
                        reduce_max(i, x + ALEAD)
                    if lo_rank[(x + 2) % 8][0] == "d" and (v0 is None or v0 + x + 2 < NV):
                        lo_part(v, l, i, x + 2, "d")
                    if x % 16 == 8 and (v0 is None or v0 + x + 8 < NV):
                        if not (isinstance(i, int) and i == 0 and x == 8):
                            v.wait_ge(sem("pv_done"), 32 * i + x - 8)
                        copy_values(i, x // 16 + 1)

            steps(v, body)
            normalise(NV // 32 - 1, 1)

        def attn_sp(sp, l):
            def load(i, h):
                for qk in range(2):
                    if isinstance(i, int):
                        src = QK[l][qk][4 * i + h]
                    else:
                        src = QK[l][qk][bass.ds(4 * i + h, 1)].rearrange("o t d q -> (o t) d q")
                    sp.dma_start(KQ[qk][h % 4][0:KA, :], src).then_inc(sem(f"kq_{h % 4}"), 16)

            def max_row(i, h):
                sp.wait_ge(sem("max_split"), 16 * i + 4 * (h + 1))
                for n in range(3):
                    sp.dma_start(KQ[1][h % 4][KA + n:KA + n + 1, :], MP[:, h % 4, n, :]).then_inc(sem(f"mrow_{h % 4}"), 16)

            for h in range(4):
                load(0, h)
            max_row(0, 0)
            with sp.Fori(0, NH // 4 - 1) as i:
                for h in range(1, 5):
                    max_row(i, h)
                    sp.wait_ge(sem("sk_done"), 32 * i + 8 * h)
                    load(i, h + 3)
            for h in range(1, 4):
                max_row(NH // 4 - 1, h)

        def wo_pe(pe, l):
            for j in range(NG * DC):
                g, k = j // DC, j % DC
                for q in range(4):
                    b = 4 * g + q
                    src = CX[:, b % 8, b // 8 * D + k * DH:b // 8 * D + (k + 1) * DH]
                    last = pe.transpose(PS[0:DH, j, q * P:(q + 1) * P], src, ident[:, :])
                last.then_inc(sem("cx_turned"), 1)
            for b in range(NB):
                pe.wait_ge(sem("cxT_ready"), 2 * (b // 4) + 2)
                pe.wait_ge(sem("cxT_ready"), min(b % 8 + 1, 8))
                if b >= 8:
                    pe.wait_ge(sem("wo_added"), b - 7)
                for k in range(DC):
                    last = pe.matmul(PS[:, b % 8, 0:D], CXT[:, k, b * P:(b + 1) * P], wo[l][:, k, :], start=k == 0, stop=k == 1)
                last.then_inc(sem("wo_projected"), 1)

        def wo_act(act, l):
            for j in range(NG * DC):
                g, k = j // DC, j % DC
                act.wait_ge(sem("cx_turned"), j + 1)
                act.activation(CXT[:, k, g * G:(g + 1) * G], PS[0:DH, j, :], ACT.Copy).then_inc(sem("cxT_ready"), 1)

        def wo_pool(pool, l):
            o = ROW[f"bo{l}"]
            pool.tensor_tensor(H[:, :, :], H[:, :, :], rows[:, o:o + D].unsqueeze(1).broadcast_to([P, NB, D]), ALU.add)\
                .then_inc(sem("bo_added"), 1)

        def wo_dve(v, l):
            v.wait_ge(sem("bo_added"), 1)
            for b in range(NB):
                v.wait_ge(sem("wo_projected"), b + 1)
                v.tensor_tensor(H[:, b, :], PS[:, b % 8, 0:D], H[:, b, :], ALU.add).then_inc(sem("wo_added"), 1)

        def router_pe(pe, l, n):
            E = (E0, E1)[l]
            for b in range(NB):
                for k in range(DC):
                    last = pe.matmul(PS[:, 0, b * E:(b + 1) * E], XN[:, k, b * P:(b + 1) * P], wr[l][:, k, :], start=k == 0, stop=k == 1)
            last.then_inc(sem("logits"), 1)
            pe.wait_ge(sem("gates"), 1)
            for b in range(NB):
                last = pe.transpose(PS[0:E, 1 + b // 4, b % 4 * P:(b % 4 + 1) * P], GT[:, b, 0:E], ident[:, :])
                if b % 4 == 3:
                    last.then_inc(sem("gates_turned"), 1)
            for b in range(NB):
                pe.wait_ge(sem("gates_rows"), b // 4 + 1)
                if b >= 3:
                    pe.wait_ge(sem("b2_added"), b - 2)
                pe.matmul(PS[:, 5 + b % 3, 0:D], GTT[0:E, b * P:(b + 1) * P], b2[l][:, :], start=True, stop=True)\
                  .then_inc(sem("b2_weighted"), 1)

        def router_act(act, l):
            act.wait_ge(sem("shifted"), 1)
            if l == 0:
                act.activation(EX[:, :, :], L2[:, :, :], ACT.Exp).then_inc(sem("exp_router"), 1)
            else:
                act.activation(t2[:, :], t2[:, :], ACT.Exp).then_inc(sem("exp_router"), 1)
            for g in range(NG):
                act.wait_ge(sem("gates_turned"), g + 1)
                act.activation(GTT[0:(E0, E1)[l], g * G:(g + 1) * G], PS[0:(E0, E1)[l], 1 + g, :], ACT.Copy)\
                   .then_inc(sem("gates_rows"), 1)

        def router_dve(v, l):
            E = (E0, E1)[l]
            c = Chain(v, sem("router_dve"))
            lg, l2, ex, sel, gt = (x[:, :, 0:E] for x in (LG, L2, EX, SEL, GT))
            wide = lambda x: x[:, :].unsqueeze(2).broadcast_to([P, NB, E])
            rank = order[:, 0:E].unsqueeze(1).broadcast_to([P, NB, E])

            def largest(m, out_sel):
                c(v.tensor_reduce(m, lg, AX, ALU.max))
                c(v.tensor_tensor(out_sel, lg, m.unsqueeze(2).broadcast_to([P, NB, E]), ALU.is_equal))
                c(v.tensor_tensor(out_sel, out_sel, rank, ALU.mult))
                c(v.tensor_reduce(t3[:, :], out_sel, AX, ALU.max))
                c(v.tensor_tensor(out_sel, rank, wide(t3), ALU.is_equal))

            v.wait_ge(sem("logits"), 1)
            o = ROW["bs"] if l == 0 else ROW["gb"]
            c(v.tensor_tensor(lg, PS[:, 0, 0:NB * E].rearrange("p (b e) -> p b e", e=E),
                              rows[:, o:o + E].unsqueeze(1).broadcast_to([P, NB, E]), ALU.add))
            if l == 0:
                largest(t1[:, :], sel)
                c(v.tensor_tensor(l2, lg, wide(t1), ALU.subtract))
                v.nop().then_inc(sem("shifted"), 1)
                v.wait_ge(sem("exp_router"), 1)
                c(v.tensor_reduce(t2[:, :], ex, AX, ALU.add))
                c(v.reciprocal(t2[:, :], t2[:, :]))
                v.tensor_tensor(gt, sel, wide(t2), ALU.mult).then_inc(sem("gates"), 1)
            else:
                largest(t1[:, :], sel)
                c(v.scalar_tensor_tensor(lg, sel, -3.0e38, lg, ALU.mult, ALU.add))
                largest(t2[:, :], ex)
                c(v.tensor_tensor(t2[:, :], t2[:, :], t1[:, :], ALU.subtract))
                v.nop().then_inc(sem("shifted"), 1)
                v.wait_ge(sem("exp_router"), 1)
                c(v.tensor_scalar(t1[:, :], t2[:, :], 1.0, None, ALU.add))
                c(v.reciprocal(t1[:, :], t1[:, :]))
                c(v.tensor_tensor(ex, ex, wide(t2), ALU.mult))
                c(v.tensor_tensor(ex, ex, sel, ALU.add))
                v.tensor_tensor(gt, ex, wide(t1), ALU.mult).then_inc(sem("gates"), 1)
            for b in range(NB):
                v.wait_ge(sem("b2_weighted"), b + 1)
                v.tensor_tensor(H[:, b, :], PS[:, 5 + b % 3, 0:D], H[:, b, :], ALU.add).then_inc(sem("b2_added"), 1)

        def mlp_steps(eng, E, body):
            if E <= 2:
                return body(0, 4 * E, True)
            body(0, 8, False)
            if E > 4:
                with eng.Fori(1, E // 2 - 1) as i:
                    body(i, 8, False)
            body(E // 2 - 1, 8, True)

        def mlp_sp(sp, nm, E, W):
            w1, w2, bb1 = W

            def load(i, e):
                def of(a):
                    return a[2 * i + e] if isinstance(i, int) else a[bass.ds(2 * i + e, 1)].rearrange("o p n -> (o p) n")
                s = e % 2
                sp.dma_start(W1s[:, s, :, :].rearrange("p k n -> p (k n)"), of(w1)).then_inc(sem(f"mlp_w{s}"), 16)
                sp.dma_start(W2s[:, s, :, :].rearrange("p k n -> p (k n)"), of(w2)).then_inc(sem(f"mlp_w{s}"), 16)
                sp.dma_start(B1s[:, s, :], of(bb1)).then_inc(sem(f"mlp_w{s}"), 16)

            for e in range(min(E, 2)):
                load(0, e)
            if E > 2:
                def body(i):
                    for e in range(2):
                        sp.wait_ge(sem("mlp_down"), 32 * i + 16 * (e + 1))
                        load(i, e + 2)
                if E > 4:
                    with sp.Fori(0, E // 2 - 1) as i:
                        body(i)
                else:
                    body(0)

        def mlp_pe(pe, nm, E):
            def up(i, m):
                s, g = m // 4 % 2, m % 4
                if g == 0:
                    pe.wait_ge(sem(f"mlp_w{s}"), 48 * i + 48 * (m // 8 + 1))
                for f in range(FC):
                    n = 6 * m + f
                    if not (isinstance(i, int) and 48 * i + n < 4):
                        pe.wait_ge(sem("mlp_gelu"), 48 * i + n - 3)
                    for k in range(DC):
                        last = pe.matmul(PS[:, n % 4, :], W1s[:, s, k, f * P:(f + 1) * P], XN[:, k, g * G:(g + 1) * G],
                                         start=k == 0, stop=k == 1)
                    last.then_inc(sem("mlp_up"), 1)

            def down(i, m):
                s, g = m // 4 % 2, m % 4
                pe.wait_ge(sem("mlp_gelu"), 48 * i + 6 * (m + 1))
                for q in range(4):
                    n = 4 * m + q
                    if not (isinstance(i, int) and 32 * i + n < 4):
                        pe.wait_ge(sem("mlp_added"), 32 * i + n - 3)
                    for f in range(FC):
                        last = pe.matmul(PS[:, 4 + q, 0:D], HT[:, m % 2, f, q * P:(q + 1) * P], W2s[:, s, f, :],
                                         start=f == 0, stop=f == FC - 1)
                    last.then_inc(sem("mlp_down"), 1)

            up(0, 0)

            def body(i, n, lastb):
                for m in range(n):
                    if not (lastb and m == n - 1):
                        up(i, m + 1)
                    down(i, m)

            mlp_steps(pe, E, body)

        def mlp_act(act, nm, E):
            def body(i, n, lastb):
                for m in range(n):
                    s = m // 4 % 2
                    if not (isinstance(i, int) and 8 * i + m < 2):
                        act.wait_ge(sem("mlp_down"), 32 * i + 4 * (m - 1))
                    for f in range(FC):
                        act.wait_ge(sem("mlp_up"), 48 * i + 6 * m + f + 1)
                        act.activation(HT[:, m % 2, f, :], PS[:, (6 * m + f) % 4, :], ACT.Gelu, bias=B1s[:, s, f:f + 1])\
                           .then_inc(sem("mlp_gelu"), 1)

            mlp_steps(act, E, body)

        def mlp_dve(v, nm, E):
            def body(i, n, lastb):
                for m in range(n):
                    e, g = m // 4, m % 4
                    if g == 0 and E > 1:
                        if not (isinstance(i, int) and 2 * i + e < 2):
                            v.wait_ge(sem("mlp_added"), 32 * i + 16 * e - 16)
                        if isinstance(i, int):
                            src = GT[:, :, 2 * i + e:2 * i + e + 1]
                        else:
                            src = GT[:, :, bass.ds(2 * i + e, 1)]
                        v.tensor_copy(GC[:, e % 2, :].unsqueeze(2), src).then_inc(sem("mlp_gcol"), 1)
                        v.wait_ge(sem("mlp_gcol"), 2 * i + e + 1)
                    for q in range(4):
                        b = 4 * g + q
                        v.wait_ge(sem("mlp_down"), 32 * i + 4 * m + q + 1)
                        if not (isinstance(i, int) and 2 * i + e == 0):
                            v.wait_ge(sem("mlp_added"), 32 * i + 4 * m + q - 15)
                        if E > 1:
                            ins = v.scalar_tensor_tensor(H[:, b, :], PS[:, 4 + q, 0:D], GC[:, e % 2, b:b + 1], H[:, b, :], ALU.mult, ALU.add)
                        else:
                            ins = v.tensor_tensor(H[:, b, :], PS[:, 4 + q, 0:D], H[:, b, :], ALU.add)
                        ins.then_inc(sem("mlp_added"), 1)

            if E == 1:
                v.wait_ge(sem("mlp_b2_added"), 1)
            mlp_steps(v, E, body)

        def add_row(pool, row, name):
            o = ROW[row]
            pool.tensor_tensor(H[:, :, :], H[:, :, :], rows[:, o:o + D].unsqueeze(1).broadcast_to([P, NB, D]), ALU.add)\
                .then_inc(sem(name), 1)

        SCAN = dram("scan_rows", [4, B, NS, S], F32)

        def mamba_pe(pe):
            n = 0
            for g in range(NG):
                for c in range(IC + 1):
                    M = P if c < IC else NS
                    if n >= 4:
                        pe.wait_ge(sem("xz_evac"), n - 3)
                    for k in range(DC):
                        last = pe.matmul(PS[0:M, n % 4, :], w_in[:, k, c * P:c * P + M], XN[:, k, g * G:(g + 1) * G],
                                         start=k == 0, stop=k == 1)
                    last.then_inc(sem("xz_projected"), 1)
                    n += 1
            for g in range(NG):
                pe.wait_ge(sem("silu_done"), 3 * B if g >= 2 else 3)
                for k in range(IC):
                    last = pe.matmul(PS[0:72, 4 + g, :], w_x[:, k, :], XS[:, k, g * G:(g + 1) * G], start=k == 0, stop=k == IC - 1)
                last.then_inc(sem("dbc_projected"), 1)
            pe.wait_ge(sem("weighted_states"), 1)
            for g in range(NG):
                pe.matmul(PS[0:NS, g, :], ssum[:, g // 2, :], UU[:, g % 2 * G:(g % 2 + 1) * G], start=True, stop=True)\
                  .then_inc(sem("ys_summed"), 1)
            for b in range(NB):
                pe.wait_ge(sem("ys_gated"), b // 4 + 1)
                if b >= 4:
                    pe.wait_ge(sem("mamba_added"), b - 3)
                pe.matmul(PS[:, 4 + b % 4, 0:D], YG[:, b * P:(b + 1) * P], w_out[:, :], start=True, stop=True)\
                  .then_inc(sem("mamba_projected"), 1)

        def mamba_act(act):
            n = 0
            act.wait_ge(sem("pads_zeroed"), 1)
            for g in range(NG):
                b, o = g // 2, g % 2 * G
                for c in range(IC + 1):
                    act.wait_ge(sem("xz_projected"), n + 1)
                    if c < IC:
                        ins = act.activation(XC[:, c, b, 3 + o:3 + o + G], PS[:, n % 4, :], ACT.Identity,
                                             bias=c128[:, C128["b_in"] + c:C128["b_in"] + c + 1])
                    else:
                        ins = act.activation(ZT[:, g * G:(g + 1) * G], PS[0:NS, n % 4, :], ACT.Identity, bias=b_z[:, 0:1])
                    ins.then_inc(sem("xz_evac"), 1)
                    n += 1
            for b in range(B):
                for c in range(IC):
                    act.wait_ge(sem("conv_done"), 3 * b + c + 1)
                    act.activation(XS[:, c, b * S:(b + 1) * S], XV[:, c, b * S:(b + 1) * S], ACT.Silu).then_inc(sem("silu_done"), 1)
            act.activation(ZS[:, :], ZT[:, :], ACT.Silu).then_inc(sem("z_silu"), 1)
            act.wait_ge(sem("dbc_evac"), NG)
            act.activation(RT[0:NS, :], RT[0:NS, :], ACT.Sigmoid, scale=-1.0).then_inc(sem("decay_ready"), 1)

        def mamba_sp(sp):
            sp.wait_ge(sem("silu_done"), 4)
            for b in range(B):
                sp.dma_start(SCAN[3, b], XS[0:NS, 0, b * S:(b + 1) * S]).then_inc(sem("scan_stored"), 16)
            sp.wait_ge(sem("decay_ready"), 1)
            for q in range(3):
                for b in range(B):
                    sp.dma_start(SCAN[q, b], RT[32 * q:32 * q + NS, b * S:(b + 1) * S]).then_inc(sem("scan_stored"), 16)
            sp.wait_ge(sem("scan_stored"), 16 * 8)
            for q in range(4):
                for b in range(B):
                    src = SCAN[q, b]
                    if q < 3:
                        src = src.unsqueeze(0).broadcast_to([NS, NS, S])
                    else:
                        src = src.unsqueeze(1).broadcast_to([NS, NS, S])
                    sp.dma_start(REP[q][b * 64:(b + 1) * 64, :], src).then_inc(sem("scan_loaded"), 16)

        def mamba_dve(v):
            v.memset(XC[:, :, :, 0:3], 0.0).then_inc(sem("pads_zeroed"), 1)
            c = Chain(v, sem("mamba_dve"))
            w = lambda j, ch: c128[:, C128["conv_w"] + 3 * j + ch:C128["conv_w"] + 3 * j + ch + 1]
            for b in range(B):
                v.wait_ge(sem("xz_evac"), 8 * (b + 1))
                for j in range(4):
                    for ch in range(IC):
                        o, x = XV[:, ch, b * S:(b + 1) * S], XC[:, ch, b, j:j + S]
                        if j == 0:
                            cb = C128["conv_b"] + ch
                            ins = v.tensor_scalar(o, x, w(j, ch), c128[:, cb:cb + 1], ALU.mult, ALU.add)
                        else:
                            ins = v.scalar_tensor_tensor(o, x, w(j, ch), o, ALU.mult, ALU.add)
                        if j == 3:
                            ins.then_inc(sem("conv_done"), 1)
                        elif ch == IC - 1:
                            c(ins)
            for g in range(NG):
                v.wait_ge(sem("dbc_projected"), g + 1)
                v.tensor_scalar(RT[:, g * G:(g + 1) * G], PS[0:72, 4 + g, :], b_x[:, 0:1], None, ALU.add).then_inc(sem("dbc_evac"), 1)
            v.wait_ge(sem("scan_loaded"), 16 * 8)
            c(v.tensor_tensor(UU[:, :], REP[1][:, :], REP[3][:, :], ALU.mult))
            c(v.tensor_tensor_scan(HH[:, :], REP[0][:, :], UU[:, :], 0.0, ALU.mult, ALU.add))
            v.tensor_tensor(UU[:, :], HH[:, :], REP[2][:, :], ALU.mult).then_inc(sem("weighted_states"), 1)
            v.wait_ge(sem("z_silu"), 1)
            for g in range(NG):
                v.wait_ge(sem("ys_summed"), g + 1)
                v.tensor_tensor(YG[:, g * G:(g + 1) * G], PS[0:NS, g, :], ZS[:, g * G:(g + 1) * G], ALU.mult).then_inc(sem("ys_gated"), 1)
            v.wait_ge(sem("b_out_added"), 1)
            for b in range(NB):
                v.wait_ge(sem("mamba_projected"), b + 1)
                v.tensor_tensor(H[:, b, :], PS[:, 4 + b % 4, 0:D], H[:, b, :], ALU.add).then_inc(sem("mamba_added"), 1)

        def store_sp(sp):
            sp.wait_ge(sem("phase_left"), 5 * nphase[0])
            sp.dma_start(out.rearrange("(b p) d -> p b d", p=P), H[:, :, :]).then_inc(sem("stored"), 16)
            sp.wait_ge(sem("stored"), 16)

        def plan(name, eng, st):
            k = 0
            for ph in PHASES:
                if name in ph:
                    ph[name](eng)
                k += 1
                barrier(eng, k)
            nphase[0] = k

        H_KEPT = dram("h_kept", [P, NB * D], F32)
        HK = at([P, NB, D], F32, 20000)

        def keep_sp(sp):
            sp.dma_start(H_KEPT, H[:, :, :].rearrange("p b d -> p (b d)")).then_inc(sem("h_kept"), 16)
            sp.wait_ge(sem("h_kept"), 16)

        def norm_dve(v):
            c = Chain(v, sem("norm_in_place"))
            for b in range(NB):
                last = v.bn_stats(ST[:, b, :], H[:, b, :])
            c(last)
            for b in range(NB):
                last = v.bn_aggr(MV[:, b, :], ST[:, b, :])
            last.then_inc(sem("norm_var"), 1)
            v.wait_ge(sem("norm_root"), 1)
            c(v.reciprocal(RI[:, :], RS[:, :]))
            v.wait_ge(sem("h_kept"), 16)
            for b in range(NB):
                v.tensor_scalar(H[:, b, :], H[:, b, :], MV[:, b, 0:1], RI[:, b:b + 1], ALU.subtract, ALU.mult)

        def norm_act(act):
            act.wait_ge(sem("norm_var"), 1)
            act.activation(RS[:, :], MV[:, :, 1], ACT.Sqrt, bias=epsc[:, 0:1]).then_inc(sem("norm_root"), 1)

        def last_sp(sp):
            sp.dma_start(HK[:, :, :].rearrange("p b d -> p (b d)"), H_KEPT).then_inc(sem("h_back"), 16)

        def last_dve(v):
            v.wait_ge(sem("h_back"), 16)
            v.tensor_tensor(H[:, :, :], H[:, :, :], HK[:, :, :], ALU.add)

        def turn_pe(pe):
            for j in range(NG * DC):
                g, k = j // DC, j % DC
                for q in range(4):
                    b = 4 * g + q
                    last = pe.transpose(PS[0:DH, j, q * P:(q + 1) * P], H[:, b, k * DH:(k + 1) * DH], ident[:, :])
                last.then_inc(sem("x_turned"), 1)

        def turn_act(act):
            for j in range(NG * DC):
                g, k = j // DC, j % DC
                act.wait_ge(sem("x_turned"), j + 1)
                act.activation(XN[:, k, g * G:(g + 1) * G], PS[0:DH, j, :], ACT.Copy)

        def ln(n, gain=None, bias=None):
            return dict(pe=lambda e: ln_pe(e, n), act=lambda e: ln_act(e, n, gain, bias), dve=lambda e: ln_dve(e, n))

        def router(l, n):
            return dict(pe=lambda e: router_pe(e, l, n), act=lambda e: router_act(e, l), dve=lambda e: router_dve(e, l))

        def attention(l, n=0, gain=None, bias=None):
            return [
                ln(n, gain, bias),
                dict(pe=lambda e: qkv_pe(e, l, n), act=lambda e: qkv_act(e, l), dve=lambda e: qkv_dve(e, l),
                     pool=lambda e: qkv_pool(e, l), sp=lambda e: qkv_sp(e, l)),
                dict(pe=lambda e: attn_pe(e, l), act=lambda e: attn_act(e, l), dve=lambda e: attn_dve(e, l),
                     pool=lambda e: attn_pool(e, l), sp=lambda e: attn_sp(e, l)),
                dict(pe=lambda e: wo_pe(e, l), act=lambda e: wo_act(e, l), pool=lambda e: wo_pool(e, l), dve=lambda e: wo_dve(e, l)),
            ]

        PHASES = [
            dict(sp=embed_sp, dve=embed_dve, pool=embed_pool, pe=embed_pe, act=embed_act),
            *attention(0),
            clear(1), ln(1), router(0, 1),
            dict(pe=lambda e: mlp_pe(e, "moe0", E0), act=lambda e: mlp_act(e, "moe0", E0), dve=lambda e: mlp_dve(e, "moe0", E0),
                 sp=lambda e: mlp_sp(e, "moe0", E0, [A[f"moe0_{k}"] for k in ("w1", "w2", "b1")])),
            clear(2), ln(2),
            dict(pe=mamba_pe, act=mamba_act, sp=mamba_sp, dve=mamba_dve, pool=lambda e: add_row(e, "b_out", "b_out_added")),
            clear(3), dict(sp=keep_sp, dve=norm_dve, act=norm_act), *attention(1, 3, "ln1_g", "ln1_b"),
            clear(4), dict(pe=turn_pe, act=turn_act),
            dict(pe=lambda e: mlp_pe(e, "mlp", 1), act=lambda e: mlp_act(e, "mlp", 1), dve=lambda e: mlp_dve(e, "mlp", 1),
                 pool=lambda e: add_row(e, "mlp_b2", "mlp_b2_added"),
                 sp=lambda e: mlp_sp(e, "mlp", 1, [A[f"mlp_{k}"] for k in ("w1", "w2", "b1")])),
            clear(5), ln(4, "ln2_g", "ln2_b"), router(1, 4),
            dict(pe=lambda e: mlp_pe(e, "moe1", E1), act=lambda e: mlp_act(e, "moe1", E1), dve=lambda e: mlp_dve(e, "moe1", E1),
                 sp=lambda e: mlp_sp(e, "moe1", E1, [A[f"moe1_{k}"] for k in ("w1", "w2", "b1")])),
            dict(sp=last_sp, dve=last_dve),
        ][:stop]

        @block.sync
        def _(sp):
            plan("sp", sp, None)
            store_sp(sp)

        @block.gpsimd
        def _(pool):
            plan("pool", pool, None)

        @block.scalar
        def _(act):
            plan("act", act, None)

        @block.tensor
        def _(pe):
            plan("pe", pe, None)

        @block.vector
        def _(v):
            plan("dve", v, None)


def kernel(**inputs):
    import numpy as np
    import concourse.bacc as bacc
    from concourse.bass_utils import run_bass_kernel_spmd as run

    w = {k: np.asarray(v) for k, v in inputs.items()}

    def chunk(a, n):
        return np.ascontiguousarray(a.reshape(-1, n, a.shape[-1]).transpose(1, 0, 2))

    def col(a, n):
        return a.reshape(-1, n).T

    v96 = {"bq0": w["L0_attn_bq"], "bk0": w["L0_attn_bk"], "ln1_g": w["L1_ffn_ln1_g"], "ln1_b": w["L1_ffn_ln1_b"],
           "bq1": w["L1_ffn_in_b"][0:D], "bk1": w["L1_ffn_in_b"][D:2 * D], "ln2_g": w["L1_ffn_ln2_g"], "ln2_b": w["L1_ffn_ln2_b"]}
    v128 = [w["L1_attn_b_in"][0:DI], w["L1_attn_conv_b"], np.ascontiguousarray(w["L1_attn_conv_w"][:, 0, :].T), w["L1_ffn_mlp_b1"]]

    row = np.concatenate([w["L0_attn_bv"].reshape(-1), w["L1_ffn_in_b"][2 * D:], w["L0_attn_bo"], w["L1_ffn_out_b"],
                          w["L1_attn_b_out"], w["L1_ffn_mlp_b2"], w["L0_tok_norm_w"], w["L0_ffn_bs"], w["L1_ffn_gate_b"]])
    arrays = {
        "x": np.ascontiguousarray(w["x"].reshape(NB, P).T),
        "coords": w["L0_tok_basin_coords"],
        "c96": np.ascontiguousarray(np.concatenate([col(v96[k], DH) for k in C96], 1)),
        "c128": np.ascontiguousarray(np.concatenate([col(v, P) for v in v128], 1)),
        "rows": np.ascontiguousarray(np.broadcast_to(row, (P, NROW))),
        "ident": np.eye(P, dtype=np.float32),
        "projT": np.ascontiguousarray(w["L0_tok_proj_w"].T),
        "wqkv0": chunk(np.concatenate([w[f"L0_attn_W{n}"].reshape(D, D) for n in "qkv"], 1), DH),
        "wo0": chunk(w["L0_attn_Wo"].reshape(D, D), DH),
        "wqkv1": chunk(np.ascontiguousarray(w["L1_ffn_in_w"].T), DH),
        "wo1": chunk(np.ascontiguousarray(w["L1_ffn_out_w"].T), DH),
    }
    def experts(nm, w1, b1, w2):
        E = w1.shape[0]
        arrays[f"{nm}_w1"] = np.ascontiguousarray(w1.reshape(E, DC, DH, FF).transpose(0, 2, 1, 3).reshape(E, DH, DC * FF))
        arrays[f"{nm}_w2"] = np.ascontiguousarray(w2.reshape(E, FC, P, D).transpose(0, 2, 1, 3).reshape(E, P, FC * D))
        arrays[f"{nm}_b1"] = np.ascontiguousarray(b1.reshape(E, FC, P).transpose(0, 2, 1))

    experts("moe0", w["L0_ffn_W1"], w["L0_ffn_b1"], w["L0_ffn_W2"])
    experts("moe1", w["L1_ffn_exp_w1"], w["L1_ffn_exp_b1"], w["L1_ffn_exp_w2"])
    experts("mlp", w["L1_ffn_mlp_w1"][None], w["L1_ffn_mlp_b1"][None], w["L1_ffn_mlp_w2"][None])
    arrays["wr0"] = chunk(w["L0_ffn_Ws"], DH)
    arrays["wr1"] = chunk(np.ascontiguousarray(w["L1_ffn_gate_w"].T), DH)
    arrays["b20"] = w["L0_ffn_b2"]
    arrays["b21"] = w["L1_ffn_exp_b2"]
    arrays["order"] = np.ascontiguousarray(np.broadcast_to(np.arange(E0, 0, -1, dtype=np.float32), (P, E0)))
    arrays["w_in"] = chunk(w["L1_attn_W_in"][:, 0:DI + NS], DH)
    w_x = np.zeros((DI, 72), np.float32)
    b_x = np.zeros((72, 1), np.float32)
    w_x[:, 0:NS] = w["L1_attn_W_dt"][:, 0:NS]
    b_x[0:NS, 0] = w["L1_attn_b_dt"][0:NS]
    for q in range(2):
        w_x[:, 32 * (q + 1):32 * (q + 1) + NS] = w["L1_attn_W_x"][:, (2 + q) * NS:(3 + q) * NS]
        b_x[32 * (q + 1):32 * (q + 1) + NS, 0] = w["L1_attn_b_x"][(2 + q) * NS:(3 + q) * NS]
    arrays["w_x"] = chunk(w_x, P)
    arrays["b_x"] = b_x
    arrays["b_z"] = np.ascontiguousarray(w["L1_attn_b_in"][DI:DI + NS, None])
    arrays["w_out"] = np.ascontiguousarray(w["L1_attn_W_out"][0:NS])
    ssum = np.zeros((P, 2, NS), np.float32)
    for p in range(P):
        ssum[p, p // 64, p % 64 // NS] = 1.0
    arrays["ssum"] = ssum
    nc = bacc.Bacc("TRN2", target_bir_lowering=False, num_devices=1)
    A = {k: nc.dram_tensor(f"in_{k}", a.shape, mybir.dt.from_np(a.dtype), kind="ExternalInput").ap() for k, a in arrays.items()}
    out = nc.dram_tensor("out", (T, D), F32, kind="ExternalOutput").ap()
    build(nc, A, out, STOP)
    r = run(nc, [{f"in_{k}": a for k, a in arrays.items()}], core_ids=[0])
    y = r.results[0]["out"]
    return y.reshape(B, S, D)
```

```python
from contextlib import ExitStack

import concourse.bass as bass
from concourse import mybir

F32 = mybir.dt.float32
BF16 = mybir.dt.bfloat16
F16 = mybir.dt.float16
I32 = mybir.dt.int32
ALU = mybir.AluOpType
ACT = mybir.ActivationFunctionType
AX = mybir.AxisListType.X

P = 128
B, S, D = 2, 1024, 192
T = B * S
DC, DH = 2, 96
G = 512
NG = T // G
NB = T // P
VOCAB, BASIN = 32000, 64
HEADS, HD = 12, 16
NH = B * HEADS
TERMS = 6
KA = TERMS * HD
KM = KA + 3
FF, FC = 768, 6
E0, E1 = 8, 4
TOPK = (1, 2)
R = 256
NT = [(T * k - E) // R + E for k, E in zip(TOPK, (E0, E1))]
DI, IC = 384, 3
NS = 8

C96 = {}
for _n in ("bq0", "bk0", "ln1_g", "ln1_b", "bq1", "bk1", "ln2_g", "ln2_b"):
    C96[_n] = 2 * len(C96)
N96 = 2 * len(C96)
C128 = {"b_in": 0, "conv_b": 3, "conv_w": 6, "mlp_b1": 18}
N128 = 24
ROW = {"bv0": 0, "bv1": D, "bo0": 2 * D, "bo1": 3 * D, "b_out": 4 * D, "mlp_b2": 5 * D, "norm_w": 6 * D, "bs": 7 * D, "gb": 7 * D + E0}
NROW = 7 * D + E0 + E1

RECURRING = [
    "counted", "slots_ready", "tile_experts", "xt_evac", "tile_turned", "y_evac", "y_stored0", "y_stored1", "combined",
    "b2_added", "b2_weighted", "bo_added", "cxT_ready", "cx_turned", "exp_done", "exp_router", "gates", "gates_rows",
    "gates_turned", "kq_0", "kq_1", "kq_2", "kq_3", "ln_done", "ln_dve", "ln_root", "ln_scaled", "ln_turned",
    "ln_var", "lo_d", "lo_p", "logits", "max_part", "max_split", "max_taken", "max_turned", "mlp_added",
    "mlp_b2_added", "mlp_down", "mlp_gcol", "mlp_gelu", "mlp_up", "mlp_w0", "mlp_w1", "mlp_v0", "mlp_v1", "mrow_0", "mrow_1", "mrow_2",
    "mrow_3", "norm_done", "norm_dve", "norm_hi", "o_evac", "o_turned", "pv_done", "qk_evac", "qk_hi", "qk_lo",
    "qk_mid", "qk_projected", "qk_rest", "qk_stored", "router_dve", "shifted", "sk_done", "sq_done", "v_evac", "v_hi",
    "v_lo", "v_projected", "vs_ready", "vs_zeroed", "wo_added", "wo_projected",
]

STOP = None


class Chain:

    def __init__(self, eng, sem, base=0):
        self.eng, self.sem, self.base, self.n = eng, sem, base, 0

    def __call__(self, ins):
        self.n += 1
        ins.then_inc(self.sem, 1)
        self.eng.wait_ge(self.sem, self.base + self.n)


def build(nc, A, out, stop):
    ctx = ExitStack()
    with ctx:
        def sb(name, shape, dt):
            return ctx.enter_context(nc.sbuf_tensor(name, shape, dt))

        sems = {}

        def sem(name):
            if name not in sems:
                sems[name] = ctx.enter_context(nc.semaphore(name))
            return sems[name]

        for name in RECURRING:
            sem(name)
        numbers = [sems[name].num for name in RECURRING]
        assert numbers == list(range(numbers[0], numbers[0] + len(numbers)))

        def clear(k):
            def wait(eng):
                eng.wait_ge(sem("cleared"), k)
            return dict(sp=lambda e: e.sem_clear(range(numbers[0], numbers[-1] + 1)).then_inc(sem("cleared"), 1),
                        pe=wait, act=wait, dve=wait, pool=wait)

        def dram(name, shape, dt):
            return nc.dram_tensor(name, shape, dt, kind="Internal").ap()

        ps = [ctx.enter_context(nc.psum_tensor(f"bank{i}", [P, 512], F32)) for i in range(0)]
        PS = ctx.enter_context(nc.psum_tensor("PS", [P, 8, 512], F32))
        H = sb("H", [P, NB, D], F32)
        XN = sb("XN", [DH, DC, T], F32)
        c96 = sb("c96", [DH, N96], F32)
        c128 = sb("c128", [P, N128], F32)
        rows = sb("rows", [P, NROW], F32)
        ident = sb("ident", [P, P], F32)
        zrow = sb("zrow", [P, D], F32)
        epsc = sb("epsc", [P, 2], F32)
        projT = sb("projT", [BASIN, D], F32)
        wqkv = [sb(f"wqkv{l}", [DH, DC, 3 * D], F32) for l in range(2)]
        wo = [sb(f"wo{l}", [DH, DC, D], F32) for l in range(2)]
        wr = [sb(f"wr{l}", [DH, DC, E], F32) for l, E in enumerate((E0, E1))]
        b2 = [sb(f"b2{l}", [E, D], F32) for l, E in enumerate((E0, E1))]
        upper = sb("upper", [P, P], F32)
        ones = sb("ones", [P, P], F32)
        smask = sb("smask", [P, 2, P], F32)
        iota = sb("iota", [P, max(NT)], F32)
        order = sb("order", [P, E0], F32)
        w_in = sb("w_in", [DH, DC, DI + NS], F32)
        w_x = sb("w_x", [P, IC, 72], F32)
        b_x = sb("b_x", [72, 1], F32)
        b_z = sb("b_z", [NS, 1], F32)
        w_out = sb("w_out", [NS, D], F32)
        ssum = sb("ssum", [P, 2, NS], F32)
        ARENA = 38048
        arena = sb("arena", [P, ARENA], F32)
        cur = [0]

        def at(shape, dt, reset=None):
            if reset is not None:
                cur[0] = reset
            n = 1
            for s in shape[1:]:
                n *= s
            words = n if dt in (F32, I32) else (n + 1) // 2
            o = cur[0]
            cur[0] += words
            assert cur[0] <= ARENA, (cur[0], ARENA)
            v = arena[0:shape[0], o:o + words]
            if dt != F32:
                v = v.bitcast(dt)
            if len(shape) > 2:
                names = "abcdef"[:len(shape) - 1]
                v = v.rearrange(f"p ({' '.join(names)}) -> p {' '.join(names)}", **{k: s for k, s in zip(names, shape[1:])})
            return v

        idx_in = at([P, NB], I32, 0)
        idx_f = at([P, NB], F32)
        idx_w = at([P, NB], F32)
        idx = at([P, NB], I32)
        emb = at([P, NB, BASIN], F32)
        embT = at([BASIN, T], F32)
        sq_e = at([P, D], F32)
        ms_e = at([P, NB], F32)
        rr_e = at([P, NB], F32)
        XT = at([P, NB, D], F32, 0)
        ST = at([P, NB, 6], F32)
        MV = at([P, NB, 2], F32)
        RS = at([P, NB], F32)
        RI = at([P, NB], F32)
        VC = at([P, NH, 8, 2, HD], BF16, 0)
        VS = at([P, 2, 8, 2, P], BF16)
        KQ = [[at([KM, S], BF16) for _ in range(4)] for _ in range(2)]
        MX = at([P, 4, 8], F32)
        MT = at([8, P], F32)
        MR = at([8, P], F32)
        MR2 = at([8, P], F32)
        MP = at([8, 4, 3, P], BF16)
        OS = at([P, 2, S], F32)
        RC = at([P, 8, 2], F32)
        CM = at([P, 8, 32], F32)
        CH = at([P, 8, 32], F32)
        CX = at([P, 8, B * D], F32)
        CXT = at([DH, DC, T], F32)
        attn_end = cur[0]
        W1s = at([DH, 2, DC, FF], F32, 4096)
        W2s = at([P, 2, FC, D], F32)
        B1s = at([P, 2, FC], F32)
        HT = at([P, 2, FC, G], F32)
        GC = at([P, 2, NB], F32)
        LG = at([P, NB, E0], F32)
        L2 = at([P, NB, E0], F32)
        EX = at([P, NB, E0], F32)
        SELF = at([P, P], F32)
        GT = at([P, NB, E0], F32)
        GK = at([P, 2, NB], F32)
        CNT = at([P, P], F32)
        INC = at([P, P], F32)
        POS = at([P, P], F32)
        TI = at([P, E0], I32)
        TF = at([P, E0], F32)
        TINC = at([P, E0], F32)
        TB = at([P, E0], F32)
        SLF = at([P, 2 * NB], F32)
        SLOT = at([P, 2 * NB], I32)
        GE = at([P, max(NT), E0], F32)
        TEF = at([P, max(NT)], F32)
        TE = at([P, max(NT)], I32)
        XIN = at([P, 2, 2, D], F32)
        XTT = at([DH, 2, DC, R], F32)
        YB = at([P, 2, 2, D], F32)
        YGT = at([P, 2 * NB, D], F32)
        t1 = at([P, NB], F32)
        t2 = at([P, NB], F32)
        t3 = at([P, NB], F32)
        GTT = at([E0, T], F32)
        XC = at([P, IC, B, S + 3], F32, 4096)
        XV = at([P, IC, T], F32)
        XS = at([P, IC, T], F32)
        RT = at([72, T], F32)
        ZT = at([NS, T], F32)
        ZS = at([NS, T], F32)
        YG = at([NS, T], F32)
        REP = [at([P, S], F32) for _ in range(4)]
        UU = at([P, S], F32)
        HH = at([P, S], F32)
        q32 = at([DH, 4, G], F32, attn_end)
        r32 = at([DH, 4, G], F32)
        v32 = at([P, 4, D], F32)
        mark = cur[0]
        PR = at([P, 8, S], F32, mark)
        LO = at([P, 8, S], F16)
        parts = at([DH, 2, 3, DC, T], BF16, mark)

        QK = [[dram(f"{n}parts{l}", [NH, TERMS, HD, S], BF16) for n in "kq"] for l in range(2)]

        XSORT = [dram(f"xsort{l}", [NT[l] * R, D], F32) for l in range(2)]
        YSORT = [dram(f"ysort{l}", [NT[l] * R, D], F32) for l in range(2)]

        block = ctx.enter_context(nc.Block())
        nphase = [0]

        def barrier(eng, k):
            s = sem("phase_left")
            eng.drain().then_inc(s, 1)
            eng.wait_ge(s, 5 * k)

        class Stage:
            pass

        LOADS = [(c96[:, :], A["c96"]), (c128[:, :], A["c128"]), (rows[:, :], A["rows"]),
                 (ident[:, :], A["ident"]), (projT[:, :], A["projT"]),
                 (wqkv[0][:, :, :], A["wqkv0"]), (wo[0][:, :, :], A["wo0"]),
                 (wqkv[1][:, :, :], A["wqkv1"]), (wo[1][:, :, :], A["wo1"]),
                 (wr[0][:, :, :], A["wr0"]), (wr[1][:, :, :], A["wr1"]), (b2[0][:, :], A["b20"]), (b2[1][:, :], A["b21"]),
                 (order[:, :], A["order"]), (upper[:, :], A["upper"]), (ones[:, :], A["ones"]),
                 (smask[:, :, :], A["smask"]), (iota[:, :], A["iota"]), (w_in[:, :, :], A["w_in"]), (w_x[:, :, :], A["w_x"]), (b_x[:, :], A["b_x"]),
                 (b_z[:, :], A["b_z"]), (w_out[:, :], A["w_out"]), (ssum[:, :, :], A["ssum"])]

        def embed_sp(sp):
            sp.dma_start(idx_in[:, :], A["x"]).then_inc(sem("idx_loaded"), 16)
            for dst, src in LOADS:
                sp.dma_start(dst, src).then_inc(sem("consts"), 16)
            sp.wait_ge(sem("zeros_set"), 1)
            for l in range(2):
                sp.dma_start(XSORT[l].rearrange("(j p) d -> p j d", p=P), zrow[:, :].unsqueeze(1).broadcast_to([P, NT[l] * R // P, D]))\
                  .then_inc(sem("rows_zeroed"), 16)

        def consts_loaded(eng):
            eng.wait_ge(sem("consts"), 16 * len(LOADS))

        def embed_dve(v):
            v.memset(zrow[:, :], 0.0).then_inc(sem("zeros_set"), 1)
            v.memset(epsc[:, 0:1], 1e-5)
            v.memset(epsc[:, 1:2], 1e-8).then_inc(sem("eps_set"), 1)
            c = Chain(v, sem("embed_dve"))
            v.wait_ge(sem("idx_loaded"), 16)
            c(v.tensor_scalar(idx_w[:, :], idx_in[:, :], 0.0, float(VOCAB), ALU.is_lt, ALU.mult))
            c(v.tensor_tensor(idx_f[:, :], idx_in[:, :], idx_w[:, :], ALU.add))
            v.tensor_scalar(idx[:, :], idx_f[:, :], 0.0, float(VOCAB - 1), ALU.max, ALU.min).then_inc(sem("idx_ready"), 1)
            consts_loaded(v)
            for g in range(NG):
                v.wait_ge(sem("embT_turned"), g + 1)
                v.tensor_copy(embT[:, g * G:(g + 1) * G], PS[0:BASIN, g, :]).then_inc(sem("embT_ready"), 1)
                for b in range(4 * g, 4 * g + 4):
                    v.wait_ge(sem("emb_projected"), b + 1)
                    v.tensor_copy(H[:, b, :], PS[:, 4 + b % 4, 0:D]).then_inc(sem("emb_evac"), 1)
            v.wait_ge(sem("rms_root"), 1)
            c(v.reciprocal(rr_e[:, :], rr_e[:, :]))
            o = ROW["norm_w"]
            for b in range(NB):
                last = v.scalar_tensor_tensor(H[:, b, :], H[:, b, :], rr_e[:, b:b + 1], rows[:, o:o + D], ALU.mult, ALU.mult)
            last.then_inc(sem("H_embedded"), 1)

        def embed_pool(pool):
            pool.wait_ge(sem("idx_ready"), 1)
            for blk in range(NB):
                pool.indirect_dma_start(emb[:, blk, :], None, A["coords"], bass.IndirectOffsetOnAxis(ap=idx[:, blk:blk + 1], axis=0)).then_inc(sem(f"gathered{blk // 4}"), 16)

        def embed_pe(pe):
            consts_loaded(pe)
            for g in range(NG):
                for q in range(4):
                    blk = 4 * g + q
                    pe.wait_ge(sem(f"gathered{g}"), 64)
                    last = pe.transpose(PS[0:BASIN, g, q * P:(q + 1) * P], emb[:, blk, :], ident[:, :])
                last.then_inc(sem("embT_turned"), 1)
            for b in range(NB):
                pe.wait_ge(sem("embT_ready"), b // 4 + 1)
                if b >= 4:
                    pe.wait_ge(sem("emb_evac"), b - 3)
                pe.matmul(PS[:, 4 + b % 4, 0:D], embT[:, b * P:(b + 1) * P], projT[:, :], start=True, stop=True)\
                  .then_inc(sem("emb_projected"), 1)

        def embed_act(act):
            c = Chain(act, sem("embed_act"))
            for b in range(NB):
                act.wait_ge(sem("emb_evac"), b + 1)
                c(act.activation(sq_e[:, :], H[:, b, :], ACT.Square, accum_out=ms_e[:, b:b + 1]))
            act.wait_ge(sem("eps_set"), 1)
            act.activation(rr_e[:, :], ms_e[:, :], ACT.Sqrt, bias=epsc[:, 1:2], scale=1.0 / D).then_inc(sem("rms_root"), 1)

        def ln_dve(v, n):
            c = Chain(v, sem("ln_dve"))
            for b in range(NB):
                last = v.bn_stats(ST[:, b, :], H[:, b, :])
            c(last)
            for b in range(NB):
                last = v.bn_aggr(MV[:, b, :], ST[:, b, :])
            last.then_inc(sem("ln_var"), 1)
            v.wait_ge(sem("ln_root"), 1)
            c(v.reciprocal(RI[:, :], RS[:, :]))
            for b in range(NB):
                v.tensor_scalar(XT[:, b, :], H[:, b, :], MV[:, b, 0:1], RI[:, b:b + 1], ALU.subtract, ALU.mult)\
                 .then_inc(sem("ln_scaled"), 1)

        def ln_act(act, n, gain=None, bias=None):
            act.wait_ge(sem("ln_var"), 1)
            act.activation(RS[:, :], MV[:, :, 1], ACT.Sqrt, bias=epsc[:, 0:1]).then_inc(sem("ln_root"), 1)
            for j in range(NG * DC):
                g, k = j // DC, j % DC
                act.wait_ge(sem("ln_turned"), j + 1)
                dst, src = XN[:, k, g * G:(g + 1) * G], PS[0:DH, j, :]
                if gain is None:
                    ins = act.activation(dst, src, ACT.Copy)
                else:
                    ins = act.activation(dst, src, ACT.Identity, scale=c96[:, C96[gain] + k:C96[gain] + k + 1],
                                         bias=c96[:, C96[bias] + k:C96[bias] + k + 1])
                ins.then_inc(sem("ln_done"), 1)

        def ln_pe(pe, n):
            for j in range(NG * DC):
                g, k = j // DC, j % DC
                for q in range(4):
                    b = 4 * g + q
                    pe.wait_ge(sem("ln_scaled"), b + 1)
                    last = pe.transpose(PS[0:DH, j, q * P:(q + 1) * P], XT[:, b, k * DH:(k + 1) * DH], ident[:, :])
                last.then_inc(sem("ln_turned"), 1)

        NJ = 4 * NG

        def job(j):
            return j // 4, (j // 2) % 2, j % 2

        def qkv_pe(pe, l, n):
            for j in range(NJ):
                g, qk, ch = job(j)
                pe.wait_ge(sem("ln_done"), 2 * g + 2)
                if j >= 4:
                    pe.wait_ge(sem("qk_evac"), j - 3)
                col = (1 - qk) * D + ch * DH
                for k in range(DC):
                    last = pe.matmul(PS[0:DH, j % 4, :], wqkv[l][:, k, col:col + DH], XN[:, k, g * G:(g + 1) * G],
                                     start=k == 0, stop=k == 1)
                last.then_inc(sem("qk_projected"), 1)
            for b in range(NB):
                if b >= 4:
                    pe.wait_ge(sem("v_evac"), b - 3)
                for k in range(DC):
                    last = pe.matmul(PS[:, 4 + b % 4, 0:D], XN[:, k, b * P:(b + 1) * P], wqkv[l][:, k, 2 * D:3 * D],
                                     start=k == 0, stop=k == 1)
                last.then_inc(sem("v_projected"), 1)

        def qkv_dve(v, l):
            for s in range(4):
                v.memset(KQ[0][s][KA:KM, :], -1.0)
            v.memset(VS[:, :, :, :, 0:64], 0.0)
            v.memset(VS[:, :, :, :, 64:P], 0.0).then_inc(sem("vs_zeroed"), 1)
            v.wait_ge(sem("vs_zeroed"), 1)
            v.memset(VS[:, :, :, 0, 64:80], 1.0)
            v.memset(VS[:, :, :, 0, 96:112], 1.0)
            v.memset(VS[:, :, :, 1, 80:96], 1.0)
            v.memset(VS[:, :, :, 1, 112:128], 1.0).then_inc(sem("vs_zeroed"), 1)
            for j in range(NJ):
                g, qk, ch = job(j)
                v.wait_ge(sem("qk_projected"), j + 1)
                if j >= 4:
                    v.wait_ge(sem("qk_rest"), j - 3)
                o = C96[("bk", "bq")[qk] + str(l)] + ch
                v.tensor_scalar(q32[:, j % 4, :], PS[0:DH, j % 4, :], c96[:, o:o + 1], (1.0, HD ** -0.5)[qk],
                                ALU.add, ALU.mult).then_inc(sem("qk_evac"), 1)
            for b in range(NB):
                v.wait_ge(sem("v_projected"), b + 1)
                if b >= 4:
                    v.wait_ge(sem("v_lo"), b - 3)
                o = ROW[f"bv{l}"]
                v.tensor_tensor(v32[:, b % 4, :], PS[:, 4 + b % 4, 0:D], rows[:, o:o + D], ALU.add).then_inc(sem("v_evac"), 1)

        def part(j, n):
            g, qk, ch = job(j)
            return parts[:, qk, n, ch, g * G:(g + 1) * G]

        def vpart(b, n):
            return VC[:, b // 8 * HEADS:(b // 8 + 1) * HEADS, b % 8, n, :]

        def heads(ap):
            return ap.rearrange("p (h d) -> p h d", h=HEADS)

        def qkv_act(act, l):
            for j in range(NJ + 1):
                if j < NJ:
                    act.wait_ge(sem("qk_evac"), j + 1)
                    act.activation(part(j, 0), q32[:, j % 4, :], ACT.Copy).then_inc(sem("qk_hi"), 1)
                if j >= 1:
                    act.wait_ge(sem("qk_rest"), j)
                    act.activation(part(j - 1, 1), r32[:, (j - 1) % 4, :], ACT.Copy).then_inc(sem("qk_mid"), 1)
            for b in range(NB):
                act.wait_ge(sem("v_evac"), b + 1)
                act.activation(vpart(b, 0), heads(v32[:, b % 4, :]), ACT.Copy).then_inc(sem("v_hi"), 1)

        def qkv_pool(pool, l):
            for j in range(NJ + 1):
                if j < NJ:
                    pool.wait_ge(sem("qk_hi"), j + 1)
                    if j >= 4:
                        pool.wait_ge(sem("qk_lo"), j - 3)
                    pool.tensor_tensor(r32[:, j % 4, :], q32[:, j % 4, :], part(j, 0), ALU.subtract).then_inc(sem("qk_rest"), 1)
                if j >= 1:
                    pool.wait_ge(sem("qk_mid"), j)
                    pool.tensor_tensor(part(j - 1, 2), r32[:, (j - 1) % 4, :], part(j - 1, 1), ALU.subtract)\
                        .then_inc(sem("qk_lo"), 1)
            for b in range(NB):
                pool.wait_ge(sem("v_hi"), b + 1)
                pool.tensor_tensor(vpart(b, 1), heads(v32[:, b % 4, :]), vpart(b, 0), ALU.subtract).then_inc(sem("v_lo"), 1)

        TERM = [(0, 0), (1, 0), (0, 1), (1, 1), (2, 0), (0, 2)]

        def qkv_sp(sp, l):
            for b in range(B):
                sp.wait_ge(sem("qk_lo"), 8 * (b + 1))
                for qk in range(2):
                    for ch in range(DC):
                        h0 = b * HEADS + 6 * ch
                        for t in range(TERMS):
                            sp.dma_start(QK[l][qk][h0:h0 + 6, t], parts[:, qk, TERM[t][qk], ch, b * S:(b + 1) * S])\
                              .then_inc(sem("qk_stored"), 16)
            sp.wait_ge(sem("qk_stored"), 16 * B * 2 * DC * TERMS)

        NV = 8 * NH
        ALEAD, BLEAD = 15, 4
        ON_DVE = (3, 7)
        lo_rank = {}
        cnt = {"d": 0, "p": 0}
        for r in range(8):
            w = "d" if r in ON_DVE else "p"
            cnt[w] += 1
            lo_rank[r] = (w, cnt[w])

        def steps(eng, body):
            body(0, 0)
            with eng.Fori(1, NV // 32 - 1) as i:
                body(i, None)
            body(NV // 32 - 1, NV - 32)

        def attn_pe(pe, l):
            def scores_q(i, x):
                s, qb = x // 8 % 4, x % 8
                if qb == 0:
                    pe.wait_ge(sem(f"kq_{s}"), 32 * i + 32 * (x // 32 + 1))
                if qb == 0 and not (isinstance(i, int) and 32 * i + x == 0):
                    pe.wait_ge(sem("max_taken"), 4 * i + x // 8)
                if not (isinstance(i, int) and 32 * i + x == 0):
                    pe.wait_ge(sem("max_part"), 32 * i + x)
                for half in range(2):
                    last = pe.matmul(PS[:, half, :], KQ[1][s][0:KA, qb * P:(qb + 1) * P],
                                     KQ[0][s][0:KA, half * 512:(half + 1) * 512], start=True, stop=True)
                last.then_inc(sem("sq_done"), 1)

            def turn_max(i, h):
                pe.wait_ge(sem("max_part"), 32 * i + 8 * (h + 1))
                pe.transpose(PS[0:8, 0, 0:P], MX[:, h % 4, :], ident[:, :]).then_inc(sem("max_turned"), 1)

            def scores_k(i, x):
                s, kb = x // 8 % 4, x % 8
                if kb == 0:
                    pe.wait_ge(sem(f"mrow_{s}"), 48 * i + 48 * (x // 32 + 1))
                if not (isinstance(i, int) and 32 * i + x < 2):
                    pe.wait_ge(sem("exp_done"), 32 * i + x - 1)
                for half in range(2):
                    last = pe.matmul(PS[:, 2 + 2 * (x % 2) + half, :], KQ[0][s][:, kb * P:(kb + 1) * P],
                                     KQ[1][s][:, half * 512:(half + 1) * 512], start=True, stop=True)
                last.then_inc(sem("sk_done"), 1)

            def values(i, x):
                s, kb, pair = x // 8 % 2, x % 8, x // 16
                first, lastt = x % 16 == 0, x % 16 == 15
                if first:
                    pe.wait_ge(sem("vs_ready"), 2 * i + pair + 1)
                    if not (isinstance(i, int) and i == 0 and pair == 0):
                        pe.wait_ge(sem("o_evac"), 2 * i + pair)
                w, r = lo_rank[x % 8]
                pe.wait_ge(sem(f"lo_{w}"), 4 * cnt[w] * i + x // 8 * cnt[w] + r)
                lhsT = VS[:, pair, kb, s, :]
                hi = PR[:, x % 8, :].bitcast(BF16).rearrange("p (n two) -> p n two", two=2)
                for q in range(2):
                    pe.matmul(PS[:, 6 + q, :], lhsT, hi[:, q * 512:(q + 1) * 512, 1], start=first, stop=False)
                for q in range(2):
                    last = pe.matmul(PS[:, 6 + q, :], lhsT, LO[:, x % 8, q * 512:(q + 1) * 512], start=False, stop=lastt)
                last.then_inc(sem("pv_done"), 1)

            def turn_out(i, pair):
                if isinstance(i, int) and 2 * i + pair < 0:
                    return
                pe.wait_ge(sem("o_evac"), 2 * i + pair + 1)
                for k in range(8):
                    last = pe.transpose(PS[:, k // 4, k % 4 * P:(k % 4 + 1) * P], OS[:, pair % 2, k * P:(k + 1) * P], ident[:, :])
                last.then_inc(sem("o_turned"), 1)

            for a in range(ALEAD):
                if a and a % 8 == 0:
                    turn_max(0, a // 8 - 1)
                scores_q(0, a)
            for b in range(BLEAD):
                scores_k(0, b)

            def body(i, v0):
                for x in range(32):
                    if v0 is None or v0 + x + BLEAD < NV:
                        scores_k(i, x + BLEAD)
                    if v0 is None or v0 + x + ALEAD <= NV:
                        if (x + ALEAD) % 8 == 0:
                            turn_max(i, (x + ALEAD) // 8 - 1)
                    if x % 16 == 6:
                        if not (isinstance(i, int) and 2 * i + x // 16 == 0):
                            if v0 is None or v0 + x + ALEAD <= NV:
                                pe.wait_ge(sem("max_part"), 32 * i + x + ALEAD)
                        turn_out(i, x // 16 - 1)
                    if v0 is None or v0 + x + ALEAD < NV:
                        if x % 16 == 6 and not (isinstance(i, int) and 2 * i + x // 16 == 0):
                            pe.wait_ge(sem("norm_done"), 2 * i + x // 16)
                        scores_q(i, x + ALEAD)
                    values(i, x)

            steps(pe, body)
            turn_out(NV // 32 - 1, 1)

        def attn_act(act, l):
            def evac(i, pair):
                first = isinstance(i, int) and 2 * i + pair < 0
                if first:
                    return
                act.wait_ge(sem("pv_done"), 32 * i + 16 * (pair + 1))
                if not (isinstance(i, int) and 2 * i + pair < 2):
                    act.wait_ge(sem("o_turned"), 2 * i + pair - 1)
                act.activation(OS[:, pair % 2, :].rearrange("p (a b) -> p a b", a=2), PS[:, 6:8, :], ACT.Copy)\
                   .then_inc(sem("o_evac"), 1)

            def body(i, v0):
                for x in range(32):
                    act.wait_ge(sem("sk_done"), 32 * i + x + 1)
                    if not (isinstance(i, int) and 32 * i + x < 8):
                        act.wait_ge(sem("pv_done"), 32 * i + x - 7)
                    act.activation(PR[:, x % 8, :].rearrange("p (a b) -> p a b", a=2),
                                   PS[:, 2 + 2 * (x % 2):4 + 2 * (x % 2), :], ACT.Exp).then_inc(sem("exp_done"), 1)
                    if x % 16 == 3:
                        evac(i, x // 16 - 1)

            steps(act, body)
            evac(NV // 32 - 1, 1)

        def lo_part(eng, l, i, x, w):
            eng.wait_ge(sem("exp_done"), 32 * i + x + 1)
            if not (isinstance(i, int) and 32 * i + x < 8):
                eng.wait_ge(sem("pv_done"), 32 * i + x - 7)
            hi = PR[:, x % 8, :].bitcast(BF16).rearrange("p (n two) -> p n two", two=2)[:, :, 1]
            eng.tensor_tensor(LO[:, x % 8, :], PR[:, x % 8, :], hi, ALU.subtract).then_inc(sem(f"lo_{w}"), 1)

        def attn_pool(pool, l):
            def body(i, v0):
                for x in range(32):
                    if lo_rank[x % 8][0] == "p":
                        lo_part(pool, l, i, x, "p")
            steps(pool, body)

        def attn_dve(v, l):
            def reduce_max(i, x):
                v.wait_ge(sem("sq_done"), 32 * i + x + 1)
                v.tensor_reduce(MX[:, x // 8 % 4, x % 8:x % 8 + 1], PS[:, 0:2, :], mybir.AxisListType.XY, ALU.max)\
                 .then_inc(sem("max_part"), 1)

            def max_rows(i, h):
                c = Chain(v, sem("max_split"), 16 * i + 4 * h)
                v.wait_ge(sem("max_turned"), 4 * i + h + 1)
                v.tensor_copy(MT[:, :], PS[0:8, 0, 0:P]).then_inc(sem("max_taken"), 1)
                v.wait_ge(sem("max_taken"), 4 * i + h + 1)
                if not (isinstance(i, int) and 4 * i + h < 4):
                    v.wait_ge(sem(f"mrow_{h % 4}"), 48 * i + 48 * (h // 4))
                m = [MP[:, h % 4, n, :] for n in range(3)]
                c(v.tensor_copy(m[0], MT[:, :]))
                c(v.tensor_tensor(MR[:, :], MT[:, :], m[0], ALU.subtract))
                c(v.tensor_copy(m[1], MR[:, :]))
                c(v.tensor_tensor(m[2], MR[:, :], m[1], ALU.subtract))

            def copy_values(i, pair):
                for s in range(2):
                    dst = VS[:, pair % 2, :, s, 0:64].rearrange("p k (n c) -> p k n c", n=2)[:, :, :, s * HD:(s + 1) * HD]
                    h = 2 * pair + s
                    if isinstance(i, int):
                        src = VC[:, 4 * i + h]
                    else:
                        src = VC[:, bass.ds(4 * i + h, 1)].rearrange("p o k n c -> p (o k) n c")
                    last = v.tensor_copy(dst, src)
                last.then_inc(sem("vs_ready"), 1)

            def cx_at(i, pair):
                if isinstance(i, int):
                    return CX[:, :, 32 * (2 * i + pair):32 * (2 * i + pair) + 32]
                return CX[:, :, bass.ds(64 * i + 32 * pair, 32)]

            def normalise(i, pair):
                if isinstance(i, int) and 2 * i + pair < 0:
                    return
                v.wait_ge(sem("o_turned"), 2 * i + pair + 1)
                c = Chain(v, sem("norm_dve"), 4 * i + 2 * pair)
                t = PS[:, 0:2, :].rearrange("p a (k n) -> p (a k) n", n=P)
                c(v.reciprocal(RC[:, :, :], t[:, :, 64:96].rearrange("p k (h d) -> p k h d", h=2)[:, :, :, 0]))
                w = RC[:, :, :].unsqueeze(3).broadcast_to([P, 8, 2, HD])
                c(v.tensor_tensor(CM[:, :, :].rearrange("p k (h d) -> p k h d", h=2),
                                  t[:, :, 32:64].rearrange("p k (h d) -> p k h d", h=2), w, ALU.mult))
                dst = cx_at(i, pair)
                c2 = Chain(v, sem("norm_hi"), 2 * i + pair)
                c2(v.tensor_tensor(CH[:, :, :].rearrange("p k (h d) -> p k h d", h=2),
                                   t[:, :, 0:32].rearrange("p k (h d) -> p k h d", h=2), w, ALU.mult))
                v.tensor_tensor(dst, CH[:, :, :], CM[:, :, :], ALU.add).then_inc(sem("norm_done"), 1)
                v.wait_ge(sem("norm_done"), 2 * i + pair + 1)

            v.wait_ge(sem("v_lo"), NB)
            v.wait_ge(sem("vs_zeroed"), 2)
            copy_values(0, 0)
            for a in range(ALEAD):
                if a and a % 8 == 0:
                    max_rows(0, a // 8 - 1)
                reduce_max(0, a)

            def body(i, v0):
                for x in range(32):
                    if v0 is None or v0 + x + ALEAD <= NV:
                        if (x + ALEAD) % 8 == 0:
                            max_rows(i, (x + ALEAD) // 8 - 1)
                    if x % 16 == 6:
                        normalise(i, x // 16 - 1)
                    if v0 is None or v0 + x + ALEAD < NV:
                        reduce_max(i, x + ALEAD)
                    if lo_rank[(x + 2) % 8][0] == "d" and (v0 is None or v0 + x + 2 < NV):
                        lo_part(v, l, i, x + 2, "d")
                    if x % 16 == 8 and (v0 is None or v0 + x + 8 < NV):
                        if not (isinstance(i, int) and i == 0 and x == 8):
                            v.wait_ge(sem("pv_done"), 32 * i + x - 8)
                        copy_values(i, x // 16 + 1)

            steps(v, body)
            normalise(NV // 32 - 1, 1)

        def attn_sp(sp, l):
            def load(i, h):
                for qk in range(2):
                    if isinstance(i, int):
                        src = QK[l][qk][4 * i + h]
                    else:
                        src = QK[l][qk][bass.ds(4 * i + h, 1)].rearrange("o t d q -> (o t) d q")
                    sp.dma_start(KQ[qk][h % 4][0:KA, :], src).then_inc(sem(f"kq_{h % 4}"), 16)

            def max_row(i, h):
                sp.wait_ge(sem("max_split"), 16 * i + 4 * (h + 1))
                for n in range(3):
                    sp.dma_start(KQ[1][h % 4][KA + n:KA + n + 1, :], MP[:, h % 4, n, :]).then_inc(sem(f"mrow_{h % 4}"), 16)

            for h in range(4):
                load(0, h)
            max_row(0, 0)
            with sp.Fori(0, NH // 4 - 1) as i:
                for h in range(1, 5):
                    max_row(i, h)
                    sp.wait_ge(sem("sk_done"), 32 * i + 8 * h)
                    load(i, h + 3)
            for h in range(1, 4):
                max_row(NH // 4 - 1, h)

        def wo_pe(pe, l):
            for j in range(NG * DC):
                g, k = j // DC, j % DC
                for q in range(4):
                    b = 4 * g + q
                    src = CX[:, b % 8, b // 8 * D + k * DH:b // 8 * D + (k + 1) * DH]
                    last = pe.transpose(PS[0:DH, j, q * P:(q + 1) * P], src, ident[:, :])
                last.then_inc(sem("cx_turned"), 1)
            for b in range(NB):
                pe.wait_ge(sem("cxT_ready"), 2 * (b // 4) + 2)
                pe.wait_ge(sem("cxT_ready"), min(b % 8 + 1, 8))
                if b >= 8:
                    pe.wait_ge(sem("wo_added"), b - 7)
                for k in range(DC):
                    last = pe.matmul(PS[:, b % 8, 0:D], CXT[:, k, b * P:(b + 1) * P], wo[l][:, k, :], start=k == 0, stop=k == 1)
                last.then_inc(sem("wo_projected"), 1)

        def wo_act(act, l):
            for j in range(NG * DC):
                g, k = j // DC, j % DC
                act.wait_ge(sem("cx_turned"), j + 1)
                act.activation(CXT[:, k, g * G:(g + 1) * G], PS[0:DH, j, :], ACT.Copy).then_inc(sem("cxT_ready"), 1)

        def wo_pool(pool, l):
            o = ROW[f"bo{l}"]
            pool.tensor_tensor(H[:, :, :], H[:, :, :], rows[:, o:o + D].unsqueeze(1).broadcast_to([P, NB, D]), ALU.add)\
                .then_inc(sem("bo_added"), 1)

        def wo_dve(v, l):
            v.wait_ge(sem("bo_added"), 1)
            for b in range(NB):
                v.wait_ge(sem("wo_projected"), b + 1)
                v.tensor_tensor(H[:, b, :], PS[:, b % 8, 0:D], H[:, b, :], ALU.add).then_inc(sem("wo_added"), 1)

        def router_pe(pe, l, n):
            E = (E0, E1)[l]
            for b in range(NB):
                for k in range(DC):
                    last = pe.matmul(PS[:, 0, b * E:(b + 1) * E], XN[:, k, b * P:(b + 1) * P], wr[l][:, k, :], start=k == 0, stop=k == 1)
            last.then_inc(sem("logits"), 1)
            pe.wait_ge(sem("shifted"), 1)
            pe.matmul(PS[:, 1, 0:P], upper[:, :], SELF[:, :], start=True, stop=True)
            pe.matmul(PS[:, 2, 0:P], ones[:, :], SELF[:, :], start=True, stop=True).then_inc(sem("counted"), 1)
            pe.wait_ge(sem("gates"), 1)
            for b in range(NB):
                last = pe.transpose(PS[0:E, 1 + b // 4, b % 4 * P:(b % 4 + 1) * P], GT[:, b, 0:E], ident[:, :])
                if b % 4 == 3:
                    last.then_inc(sem("gates_turned"), 1)
            for b in range(NB):
                pe.wait_ge(sem("gates_rows"), b // 4 + 1)
                if b >= 3:
                    pe.wait_ge(sem("b2_added"), b - 2)
                pe.matmul(PS[:, 5 + b % 3, 0:D], GTT[0:E, b * P:(b + 1) * P], b2[l][:, :], start=True, stop=True)\
                  .then_inc(sem("b2_weighted"), 1)

        def router_act(act, l):
            act.wait_ge(sem("shifted"), 1)
            if l == 0:
                act.activation(EX[:, :, :], L2[:, :, :], ACT.Exp).then_inc(sem("exp_router"), 1)
            else:
                act.activation(t2[:, :], t2[:, :], ACT.Exp).then_inc(sem("exp_router"), 1)
            for g in range(NG):
                act.wait_ge(sem("gates_turned"), g + 1)
                act.activation(GTT[0:(E0, E1)[l], g * G:(g + 1) * G], PS[0:(E0, E1)[l], 1 + g, :], ACT.Copy)\
                   .then_inc(sem("gates_rows"), 1)

        def router_dve(v, l):
            E, K = (E0, E1)[l], TOPK[l]
            KB = K * NB
            c = Chain(v, sem("router_dve"))
            lg, l2, ex, gt = (x[:, :, 0:E] for x in (LG, L2, EX, GT))
            sel = SELF[:, :].rearrange("p (k b e) -> p k b e", k=K, e=E)
            wide = lambda x: x.unsqueeze(2).broadcast_to([P, NB, E])
            rank = order[:, 0:E].unsqueeze(1).broadcast_to([P, NB, E])

            def largest(m, out_sel):
                c(v.tensor_reduce(m, lg, AX, ALU.max))
                c(v.tensor_tensor(out_sel, lg, wide(m), ALU.is_equal))
                c(v.tensor_tensor(out_sel, out_sel, rank, ALU.mult))
                c(v.tensor_reduce(t3[:, :], out_sel, AX, ALU.max))
                c(v.tensor_tensor(out_sel, rank, wide(t3[:, :]), ALU.is_equal))

            v.wait_ge(sem("logits"), 1)
            o = ROW["bs"] if l == 0 else ROW["gb"]
            c(v.tensor_tensor(lg, PS[:, 0, 0:NB * E].rearrange("p (b e) -> p b e", e=E),
                              rows[:, o:o + E].unsqueeze(1).broadcast_to([P, NB, E]), ALU.add))
            largest(t1[:, :], sel[:, 0])
            if l == 0:
                c(v.tensor_tensor(l2, lg, wide(t1[:, :]), ALU.subtract))
            else:
                c(v.scalar_tensor_tensor(lg, sel[:, 0], -3.0e38, lg, ALU.mult, ALU.add))
                largest(t2[:, :], sel[:, 1])
                c(v.tensor_tensor(t2[:, :], t2[:, :], t1[:, :], ALU.subtract))
            v.nop().then_inc(sem("shifted"), 1)

            v.wait_ge(sem("counted"), 1)
            eb = "p (b e) -> p e b"
            cnt, inc, pos = (x[:, :].rearrange("p (e b) -> p e b", e=E) for x in (CNT, INC, POS))
            te = slice(0, E)
            c(v.tensor_copy(cnt, PS[:, 2, 0:P].rearrange(eb, e=E)))
            c(v.tensor_tensor_scan(INC[:, :], smask[:, l, :], CNT[:, :], 0.0, ALU.mult, ALU.add))
            c(v.tensor_scalar(TI[:, te], inc[:, :, KB - 1], float(R - 1), None, ALU.add))
            c(v.tensor_scalar(TI[:, te], TI[:, te], 8, None, ALU.logical_shift_right))
            c(v.tensor_copy(TF[:, te], TI[:, te]))
            c(v.tensor_tensor_scan(TINC[:, te], ones[:, te], TF[:, te], 0.0, ALU.mult, ALU.add))
            c(v.tensor_tensor(TB[:, te], TINC[:, te], TF[:, te], ALU.subtract))
            c(v.tensor_scalar(TB[:, te], TB[:, te], float(R), None, ALU.mult))
            c(v.tensor_tensor(inc, inc, cnt, ALU.subtract))
            c(v.tensor_tensor(inc, inc, TB[:, te].unsqueeze(2).broadcast_to([P, E, KB]), ALU.add))
            c(v.tensor_tensor(pos, PS[:, 1, 0:P].rearrange(eb, e=E), inc, ALU.add))
            c(v.tensor_tensor(pos, pos, SELF[:, :].rearrange(eb, e=E), ALU.mult))
            c(v.tensor_reduce(SLF[:, 0:KB], POS[:, :].rearrange("p (e b) -> p b e", e=E), AX, ALU.add))
            v.tensor_copy(SLOT[:, 0:KB], SLF[:, 0:KB]).then_inc(sem("slots_ready"), 1)
            nt = NT[l]
            c(v.tensor_tensor(GE[:, 0:nt, te], iota[:, 0:nt].unsqueeze(2).broadcast_to([P, nt, E]),
                              TINC[:, te].unsqueeze(1).broadcast_to([P, nt, E]), ALU.is_ge))
            c(v.tensor_reduce(TEF[:, 0:nt], GE[:, 0:nt, te], AX, ALU.add))
            v.tensor_scalar(TE[:, 0:nt], TEF[:, 0:nt], float(E - 1), None, ALU.min).then_inc(sem("tile_experts"), 1)

            v.wait_ge(sem("exp_router"), 1)
            if l == 0:
                c(v.tensor_reduce(t2[:, :], ex, AX, ALU.add))
                c(v.reciprocal(GK[:, 0, :], t2[:, :]))
                v.tensor_tensor(gt, sel[:, 0], wide(GK[:, 0, :]), ALU.mult).then_inc(sem("gates"), 1)
            else:
                c(v.tensor_scalar(t1[:, :], t2[:, :], 1.0, None, ALU.add))
                c(v.reciprocal(GK[:, 0, :], t1[:, :]))
                c(v.tensor_tensor(GK[:, 1, :], t2[:, :], GK[:, 0, :], ALU.mult))
                c(v.tensor_tensor(ex, sel[:, 1], wide(GK[:, 1, :]), ALU.mult))
                c(v.tensor_tensor(l2, sel[:, 0], wide(GK[:, 0, :]), ALU.mult))
                v.tensor_tensor(gt, ex, l2, ALU.add).then_inc(sem("gates"), 1)
            for b in range(NB):
                v.wait_ge(sem("b2_weighted"), b + 1)
                v.tensor_tensor(H[:, b, :], PS[:, 5 + b % 3, 0:D], H[:, b, :], ALU.add).then_inc(sem("b2_added"), 1)

        def router_pool(pool, l):
            pool.wait_ge(sem("slots_ready"), 1)
            pool.wait_ge(sem("rows_zeroed"), 32)
            for n in range(TOPK[l] * NB):
                pool.indirect_dma_start(XSORT[l], bass.IndirectOffsetOnAxis(ap=SLOT[:, n:n + 1], axis=0), XT[:, n % NB, :], None)\
                    .then_inc(sem(f"scattered{l}"), 16)
            pool.wait_ge(sem(f"scattered{l}"), 16 * TOPK[l] * NB)

        def tile_steps(eng, l, body):
            body(0, 0)
            body(0, 1)
            with eng.Fori(1, (NT[l] - 3) // 2) as i:
                body(i, 0)
                body(i, 1)
            for j in range(NT[l] - 3, NT[l]):
                body((NT[l] - 3) // 2, j - (NT[l] - 3))

        def is0(i, x, below):
            return isinstance(i, int) and 2 * i + x < below

        def there(i, x, l):
            return not isinstance(i, int) or 2 * i + x < NT[l]

        def moe_sp(sp, l, W):
            def expert(i, x):
                at = TE[0:1, 2 * i + x:2 * i + x + 1] if isinstance(i, int) else TE[0:1, bass.ds(2 * i + x, 1)]
                return sp.value_load(at, min_val=0, max_val=(E0, E1)[l] - 1)

            def fetch(dst, a, e, name):
                sp.dma_start(dst, a[bass.ds(e, 1)].rearrange("o p n -> (o p) n")).then_inc(sem(name), 16)

            def first_layer(e, s):
                fetch(W1s[:, s, :, :].rearrange("p k n -> p (k n)"), W[0], e, f"mlp_w{s}")
                fetch(B1s[:, s, :], W[2], e, f"mlp_w{s}")

            def second_layer(e, s):
                fetch(W2s[:, s, :, :].rearrange("p k n -> p (k n)"), W[1], e, f"mlp_v{s}")

            for x in range(2):
                e = expert(0, x)
                first_layer(e, x)
                second_layer(e, x)

            def body(i, x):
                if there(i, x + 2, l):
                    e = expert(i, x + 2)
                    sp.wait_ge(sem("mlp_gelu"), 12 * i + 6 * (x + 1))
                    first_layer(e, x % 2)
                    sp.wait_ge(sem("mlp_down"), 4 * i + 2 * (x + 1))
                    second_layer(e, x % 2)
                sp.wait_ge(sem("y_evac"), 4 * i + 2 * (x + 1))
                if isinstance(i, int):
                    j = 2 * i + x
                    dst = YSORT[l][R * j:R * (j + 1), :]
                else:
                    dst = YSORT[l][bass.ds(2 * R * i + R * x, R), :]
                sp.dma_start(dst.rearrange("(r p) d -> p r d", p=P), YB[:, x % 2, :, :]).then_inc(sem(f"y_stored{x % 2}"), 16)

            tile_steps(sp, l, body)
            sp.wait_ge(sem("y_stored0"), 16 * ((NT[l] + 1) // 2))
            sp.wait_ge(sem("y_stored1"), 16 * (NT[l] // 2))

        def moe_pool(pool, l):
            def load(i, x):
                if isinstance(i, int):
                    j = 2 * i + x
                    src = XSORT[l][R * j:R * (j + 1), :]
                else:
                    src = XSORT[l][bass.ds(2 * R * i + R * x, R), :]
                pool.dma_start(XIN[:, x % 2, :, :], src.rearrange("(r p) d -> p r d", p=P)).then_inc(sem(f"x_loaded{l}_{x % 2}"), 16)

            load(0, 0)
            load(0, 1)

            def body(i, x):
                if there(i, x + 2, l):
                    pool.wait_ge(sem("tile_turned"), 2 * i + x + 1)
                    load(i, x + 2)

            tile_steps(pool, l, body)

        def moe_pe(pe, l):
            def turn(i, x):
                s = x % 2
                pe.wait_ge(sem(f"x_loaded{l}_{s}"), 16 * i + 16 * (x // 2 + 1))
                if not is0(i, x, 2):
                    pe.wait_ge(sem("xt_evac"), 2 * i + x - 1)
                for k in range(DC):
                    for r in range(2):
                        last = pe.transpose(PS[0:DH, s, k * R + r * P:k * R + (r + 1) * P], XIN[:, s, r, k * DH:(k + 1) * DH], ident[:, :])
                last.then_inc(sem("tile_turned"), 1)

            def up(i, x):
                s = x % 2
                pe.wait_ge(sem(f"mlp_w{s}"), 32 * i + 32 * (x // 2 + 1))
                pe.wait_ge(sem("xt_evac"), 2 * i + x + 1)
                for f in range(FC):
                    n = 6 * x + f
                    if not (isinstance(i, int) and 12 * i + n < 4):
                        pe.wait_ge(sem("mlp_gelu"), 12 * i + n - 3)
                    for k in range(DC):
                        last = pe.matmul(PS[:, 2 + n % 4, 0:R], W1s[:, s, k, f * P:(f + 1) * P], XTT[:, s, k, :], start=k == 0, stop=k == 1)
                    last.then_inc(sem("mlp_up"), 1)

            def down(i, x):
                s = x % 2
                pe.wait_ge(sem(f"mlp_v{s}"), 16 * i + 16 * (x // 2 + 1))
                pe.wait_ge(sem("mlp_gelu"), 12 * i + 6 * (x + 1))
                for r in range(2):
                    if not is0(i, x, 1):
                        pe.wait_ge(sem("y_evac"), 4 * i + 2 * x + r - 1)
                    for f in range(FC):
                        last = pe.matmul(PS[:, 6 + r, 0:D], HT[:, s, f, r * P:(r + 1) * P], W2s[:, s, f, :], start=f == 0, stop=f == FC - 1)
                    last.then_inc(sem("mlp_down"), 1)

            turn(0, 0)
            turn(0, 1)
            up(0, 0)

            def body(i, x):
                if there(i, x + 2, l):
                    turn(i, x + 2)
                if there(i, x + 1, l):
                    up(i, x + 1)
                down(i, x)

            tile_steps(pe, l, body)

        def moe_act(act, l, gain=None, bias=None):
            def evac(i, x):
                s = x % 2
                act.wait_ge(sem("tile_turned"), 2 * i + x + 1)
                if not is0(i, x, 2):
                    act.wait_ge(sem("mlp_up"), 12 * i + 6 * (x - 1))
                dst, src = XTT[:, s, :, :], PS[0:DH, s, :].rearrange("p (k n) -> p k n", k=DC)
                if gain is None:
                    ins = act.activation(dst, src, ACT.Copy)
                else:
                    for k in range(DC):
                        ins = act.activation(dst[:, k, :], src[:, k, :], ACT.Identity, scale=c96[:, C96[gain] + k:C96[gain] + k + 1],
                                             bias=c96[:, C96[bias] + k:C96[bias] + k + 1])
                ins.then_inc(sem("xt_evac"), 1)

            def gelu(i, x):
                s = x % 2
                if not is0(i, x, 2):
                    act.wait_ge(sem("mlp_down"), 4 * i + 2 * (x - 1))
                for f in range(FC):
                    act.wait_ge(sem("mlp_up"), 12 * i + 6 * x + f + 1)
                    act.activation(HT[:, s, f, 0:R], PS[:, 2 + (6 * x + f) % 4, 0:R], ACT.Gelu, bias=B1s[:, s, f:f + 1])\
                       .then_inc(sem("mlp_gelu"), 1)

            evac(0, 0)
            evac(0, 1)
            gelu(0, 0)

            def body(i, x):
                if there(i, x + 2, l):
                    evac(i, x + 2)
                if there(i, x + 1, l):
                    gelu(i, x + 1)

            tile_steps(act, l, body)

        def moe_dve(v, l):
            def body(i, x):
                s = x % 2
                if not is0(i, x, 2):
                    v.wait_ge(sem(f"y_stored{s}"), 16 * i + 16 * (x // 2))
                for r in range(2):
                    v.wait_ge(sem("mlp_down"), 4 * i + 2 * x + r + 1)
                    v.tensor_copy(YB[:, s, r, :], PS[:, 6 + r, 0:D]).then_inc(sem("y_evac"), 1)

            tile_steps(v, l, body)

        def combine_pool(pool, l):
            for n in range(TOPK[l] * NB):
                pool.indirect_dma_start(YGT[:, n, :], None, YSORT[l], bass.IndirectOffsetOnAxis(ap=SLOT[:, n:n + 1], axis=0))\
                    .then_inc(sem(f"y_gathered{l}_{n // 4}"), 16)

        def combine_dve(v, l):
            for n in range(TOPK[l] * NB):
                k, b = n // NB, n % NB
                v.wait_ge(sem(f"y_gathered{l}_{n // 4}"), 64)
                if k:
                    v.wait_ge(sem("combined"), b + 1)
                v.scalar_tensor_tensor(H[:, b, :], YGT[:, n, :], GK[:, k, b:b + 1], H[:, b, :], ALU.mult, ALU.add).then_inc(sem("combined"), 1)

        def mlp_steps(eng, E, body):
            if E <= 2:
                return body(0, 4 * E, True)
            body(0, 8, False)
            if E > 4:
                with eng.Fori(1, E // 2 - 1) as i:
                    body(i, 8, False)
            body(E // 2 - 1, 8, True)

        def mlp_sp(sp, nm, E, W):
            w1, w2, bb1 = W

            def load(i, e):
                def of(a):
                    return a[2 * i + e] if isinstance(i, int) else a[bass.ds(2 * i + e, 1)].rearrange("o p n -> (o p) n")
                s = e % 2
                sp.dma_start(W1s[:, s, :, :].rearrange("p k n -> p (k n)"), of(w1)).then_inc(sem(f"mlp_w{s}"), 16)
                sp.dma_start(W2s[:, s, :, :].rearrange("p k n -> p (k n)"), of(w2)).then_inc(sem(f"mlp_w{s}"), 16)
                sp.dma_start(B1s[:, s, :], of(bb1)).then_inc(sem(f"mlp_w{s}"), 16)

            for e in range(min(E, 2)):
                load(0, e)
            if E > 2:
                def body(i):
                    for e in range(2):
                        sp.wait_ge(sem("mlp_down"), 32 * i + 16 * (e + 1))
                        load(i, e + 2)
                if E > 4:
                    with sp.Fori(0, E // 2 - 1) as i:
                        body(i)
                else:
                    body(0)

        def mlp_pe(pe, nm, E):
            def up(i, m):
                s, g = m // 4 % 2, m % 4
                if g == 0:
                    pe.wait_ge(sem(f"mlp_w{s}"), 48 * i + 48 * (m // 8 + 1))
                for f in range(FC):
                    n = 6 * m + f
                    if not (isinstance(i, int) and 48 * i + n < 4):
                        pe.wait_ge(sem("mlp_gelu"), 48 * i + n - 3)
                    for k in range(DC):
                        last = pe.matmul(PS[:, n % 4, :], W1s[:, s, k, f * P:(f + 1) * P], XN[:, k, g * G:(g + 1) * G],
                                         start=k == 0, stop=k == 1)
                    last.then_inc(sem("mlp_up"), 1)

            def down(i, m):
                s, g = m // 4 % 2, m % 4
                pe.wait_ge(sem("mlp_gelu"), 48 * i + 6 * (m + 1))
                for q in range(4):
                    n = 4 * m + q
                    if not (isinstance(i, int) and 32 * i + n < 4):
                        pe.wait_ge(sem("mlp_added"), 32 * i + n - 3)
                    for f in range(FC):
                        last = pe.matmul(PS[:, 4 + q, 0:D], HT[:, m % 2, f, q * P:(q + 1) * P], W2s[:, s, f, :],
                                         start=f == 0, stop=f == FC - 1)
                    last.then_inc(sem("mlp_down"), 1)

            up(0, 0)

            def body(i, n, lastb):
                for m in range(n):
                    if not (lastb and m == n - 1):
                        up(i, m + 1)
                    down(i, m)

            mlp_steps(pe, E, body)

        def mlp_act(act, nm, E):
            def body(i, n, lastb):
                for m in range(n):
                    s = m // 4 % 2
                    if not (isinstance(i, int) and 8 * i + m < 2):
                        act.wait_ge(sem("mlp_down"), 32 * i + 4 * (m - 1))
                    for f in range(FC):
                        act.wait_ge(sem("mlp_up"), 48 * i + 6 * m + f + 1)
                        act.activation(HT[:, m % 2, f, :], PS[:, (6 * m + f) % 4, :], ACT.Gelu, bias=B1s[:, s, f:f + 1])\
                           .then_inc(sem("mlp_gelu"), 1)

            mlp_steps(act, E, body)

        def mlp_dve(v, nm, E):
            def body(i, n, lastb):
                for m in range(n):
                    e, g = m // 4, m % 4
                    if g == 0 and E > 1:
                        if not (isinstance(i, int) and 2 * i + e < 2):
                            v.wait_ge(sem("mlp_added"), 32 * i + 16 * e - 16)
                        if isinstance(i, int):
                            src = GT[:, :, 2 * i + e:2 * i + e + 1]
                        else:
                            src = GT[:, :, bass.ds(2 * i + e, 1)]
                        v.tensor_copy(GC[:, e % 2, :].unsqueeze(2), src).then_inc(sem("mlp_gcol"), 1)
                        v.wait_ge(sem("mlp_gcol"), 2 * i + e + 1)
                    for q in range(4):
                        b = 4 * g + q
                        v.wait_ge(sem("mlp_down"), 32 * i + 4 * m + q + 1)
                        if not (isinstance(i, int) and 2 * i + e == 0):
                            v.wait_ge(sem("mlp_added"), 32 * i + 4 * m + q - 15)
                        if E > 1:
                            ins = v.scalar_tensor_tensor(H[:, b, :], PS[:, 4 + q, 0:D], GC[:, e % 2, b:b + 1], H[:, b, :], ALU.mult, ALU.add)
                        else:
                            ins = v.tensor_tensor(H[:, b, :], PS[:, 4 + q, 0:D], H[:, b, :], ALU.add)
                        ins.then_inc(sem("mlp_added"), 1)

            if E == 1:
                v.wait_ge(sem("mlp_b2_added"), 1)
            mlp_steps(v, E, body)

        def add_row(pool, row, name):
            o = ROW[row]
            pool.tensor_tensor(H[:, :, :], H[:, :, :], rows[:, o:o + D].unsqueeze(1).broadcast_to([P, NB, D]), ALU.add)\
                .then_inc(sem(name), 1)

        SCAN = dram("scan_rows", [4, B, NS, S], F32)

        def mamba_pe(pe):
            n = 0
            for g in range(NG):
                for c in range(IC + 1):
                    M = P if c < IC else NS
                    if n >= 4:
                        pe.wait_ge(sem("xz_evac"), n - 3)
                    for k in range(DC):
                        last = pe.matmul(PS[0:M, n % 4, :], w_in[:, k, c * P:c * P + M], XN[:, k, g * G:(g + 1) * G],
                                         start=k == 0, stop=k == 1)
                    last.then_inc(sem("xz_projected"), 1)
                    n += 1
            for g in range(NG):
                pe.wait_ge(sem("silu_done"), 3 * B if g >= 2 else 3)
                for k in range(IC):
                    last = pe.matmul(PS[0:72, 4 + g, :], w_x[:, k, :], XS[:, k, g * G:(g + 1) * G], start=k == 0, stop=k == IC - 1)
                last.then_inc(sem("dbc_projected"), 1)
            pe.wait_ge(sem("weighted_states"), 1)
            for g in range(NG):
                pe.matmul(PS[0:NS, g, :], ssum[:, g // 2, :], UU[:, g % 2 * G:(g % 2 + 1) * G], start=True, stop=True)\
                  .then_inc(sem("ys_summed"), 1)
            for b in range(NB):
                pe.wait_ge(sem("ys_gated"), b // 4 + 1)
                if b >= 4:
                    pe.wait_ge(sem("mamba_added"), b - 3)
                pe.matmul(PS[:, 4 + b % 4, 0:D], YG[:, b * P:(b + 1) * P], w_out[:, :], start=True, stop=True)\
                  .then_inc(sem("mamba_projected"), 1)

        def mamba_act(act):
            n = 0
            act.wait_ge(sem("pads_zeroed"), 1)
            for g in range(NG):
                b, o = g // 2, g % 2 * G
                for c in range(IC + 1):
                    act.wait_ge(sem("xz_projected"), n + 1)
                    if c < IC:
                        ins = act.activation(XC[:, c, b, 3 + o:3 + o + G], PS[:, n % 4, :], ACT.Identity,
                                             bias=c128[:, C128["b_in"] + c:C128["b_in"] + c + 1])
                    else:
                        ins = act.activation(ZT[:, g * G:(g + 1) * G], PS[0:NS, n % 4, :], ACT.Identity, bias=b_z[:, 0:1])
                    ins.then_inc(sem("xz_evac"), 1)
                    n += 1
            for b in range(B):
                for c in range(IC):
                    act.wait_ge(sem("conv_done"), 3 * b + c + 1)
                    act.activation(XS[:, c, b * S:(b + 1) * S], XV[:, c, b * S:(b + 1) * S], ACT.Silu).then_inc(sem("silu_done"), 1)
            act.activation(ZS[:, :], ZT[:, :], ACT.Silu).then_inc(sem("z_silu"), 1)
            act.wait_ge(sem("dbc_evac"), NG)
            act.activation(RT[0:NS, :], RT[0:NS, :], ACT.Sigmoid, scale=-1.0).then_inc(sem("decay_ready"), 1)

        def mamba_sp(sp):
            sp.wait_ge(sem("silu_done"), 4)
            for b in range(B):
                sp.dma_start(SCAN[3, b], XS[0:NS, 0, b * S:(b + 1) * S]).then_inc(sem("scan_stored"), 16)
            sp.wait_ge(sem("decay_ready"), 1)
            for q in range(3):
                for b in range(B):
                    sp.dma_start(SCAN[q, b], RT[32 * q:32 * q + NS, b * S:(b + 1) * S]).then_inc(sem("scan_stored"), 16)
            sp.wait_ge(sem("scan_stored"), 16 * 8)
            for q in range(4):
                for b in range(B):
                    src = SCAN[q, b]
                    if q < 3:
                        src = src.unsqueeze(0).broadcast_to([NS, NS, S])
                    else:
                        src = src.unsqueeze(1).broadcast_to([NS, NS, S])
                    sp.dma_start(REP[q][b * 64:(b + 1) * 64, :], src).then_inc(sem("scan_loaded"), 16)

        def mamba_dve(v):
            v.memset(XC[:, :, :, 0:3], 0.0).then_inc(sem("pads_zeroed"), 1)
            c = Chain(v, sem("mamba_dve"))
            w = lambda j, ch: c128[:, C128["conv_w"] + 3 * j + ch:C128["conv_w"] + 3 * j + ch + 1]
            for b in range(B):
                v.wait_ge(sem("xz_evac"), 8 * (b + 1))
                for j in range(4):
                    for ch in range(IC):
                        o, x = XV[:, ch, b * S:(b + 1) * S], XC[:, ch, b, j:j + S]
                        if j == 0:
                            cb = C128["conv_b"] + ch
                            ins = v.tensor_scalar(o, x, w(j, ch), c128[:, cb:cb + 1], ALU.mult, ALU.add)
                        else:
                            ins = v.scalar_tensor_tensor(o, x, w(j, ch), o, ALU.mult, ALU.add)
                        if j == 3:
                            ins.then_inc(sem("conv_done"), 1)
                        elif ch == IC - 1:
                            c(ins)
            for g in range(NG):
                v.wait_ge(sem("dbc_projected"), g + 1)
                v.tensor_scalar(RT[:, g * G:(g + 1) * G], PS[0:72, 4 + g, :], b_x[:, 0:1], None, ALU.add).then_inc(sem("dbc_evac"), 1)
            v.wait_ge(sem("scan_loaded"), 16 * 8)
            c(v.tensor_tensor(UU[:, :], REP[1][:, :], REP[3][:, :], ALU.mult))
            c(v.tensor_tensor_scan(HH[:, :], REP[0][:, :], UU[:, :], 0.0, ALU.mult, ALU.add))
            v.tensor_tensor(UU[:, :], HH[:, :], REP[2][:, :], ALU.mult).then_inc(sem("weighted_states"), 1)
            v.wait_ge(sem("z_silu"), 1)
            for g in range(NG):
                v.wait_ge(sem("ys_summed"), g + 1)
                v.tensor_tensor(YG[:, g * G:(g + 1) * G], PS[0:NS, g, :], ZS[:, g * G:(g + 1) * G], ALU.mult).then_inc(sem("ys_gated"), 1)
            v.wait_ge(sem("b_out_added"), 1)
            for b in range(NB):
                v.wait_ge(sem("mamba_projected"), b + 1)
                v.tensor_tensor(H[:, b, :], PS[:, 4 + b % 4, 0:D], H[:, b, :], ALU.add).then_inc(sem("mamba_added"), 1)

        def store_sp(sp):
            sp.wait_ge(sem("phase_left"), 5 * nphase[0])
            sp.dma_start(out.rearrange("(b p) d -> p b d", p=P), H[:, :, :]).then_inc(sem("stored"), 16)
            sp.wait_ge(sem("stored"), 16)

        def plan(name, eng, st):
            k = 0
            for ph in PHASES:
                if name in ph:
                    ph[name](eng)
                k += 1
                barrier(eng, k)
            nphase[0] = k

        H_KEPT = dram("h_kept", [P, NB * D], F32)
        HK = at([P, NB, D], F32, 20000)

        def keep_sp(sp):
            sp.dma_start(H_KEPT, H[:, :, :].rearrange("p b d -> p (b d)")).then_inc(sem("h_kept"), 16)
            sp.wait_ge(sem("h_kept"), 16)

        def norm_dve(v):
            c = Chain(v, sem("norm_in_place"))
            for b in range(NB):
                last = v.bn_stats(ST[:, b, :], H[:, b, :])
            c(last)
            for b in range(NB):
                last = v.bn_aggr(MV[:, b, :], ST[:, b, :])
            last.then_inc(sem("norm_var"), 1)
            v.wait_ge(sem("norm_root"), 1)
            c(v.reciprocal(RI[:, :], RS[:, :]))
            v.wait_ge(sem("h_kept"), 16)
            for b in range(NB):
                v.tensor_scalar(H[:, b, :], H[:, b, :], MV[:, b, 0:1], RI[:, b:b + 1], ALU.subtract, ALU.mult)

        def norm_act(act):
            act.wait_ge(sem("norm_var"), 1)
            act.activation(RS[:, :], MV[:, :, 1], ACT.Sqrt, bias=epsc[:, 0:1]).then_inc(sem("norm_root"), 1)

        def last_sp(sp):
            sp.dma_start(HK[:, :, :].rearrange("p b d -> p (b d)"), H_KEPT).then_inc(sem("h_back"), 16)

        def last_dve(v):
            v.wait_ge(sem("h_back"), 16)
            v.tensor_tensor(H[:, :, :], H[:, :, :], HK[:, :, :], ALU.add)

        def turn_pe(pe):
            for j in range(NG * DC):
                g, k = j // DC, j % DC
                for q in range(4):
                    b = 4 * g + q
                    last = pe.transpose(PS[0:DH, j, q * P:(q + 1) * P], H[:, b, k * DH:(k + 1) * DH], ident[:, :])
                last.then_inc(sem("x_turned"), 1)

        def turn_act(act):
            for j in range(NG * DC):
                g, k = j // DC, j % DC
                act.wait_ge(sem("x_turned"), j + 1)
                act.activation(XN[:, k, g * G:(g + 1) * G], PS[0:DH, j, :], ACT.Copy)

        def ln(n, gain=None, bias=None):
            return dict(pe=lambda e: ln_pe(e, n), act=lambda e: ln_act(e, n, gain, bias), dve=lambda e: ln_dve(e, n))

        def router(l, n):
            return dict(pe=lambda e: router_pe(e, l, n), act=lambda e: router_act(e, l), dve=lambda e: router_dve(e, l),
                        pool=lambda e: router_pool(e, l))

        def experts(l, nm, gain=None, bias=None):
            return [dict(pe=lambda e: moe_pe(e, l), act=lambda e: moe_act(e, l, gain, bias), dve=lambda e: moe_dve(e, l),
                         pool=lambda e: moe_pool(e, l), sp=lambda e: moe_sp(e, l, [A[f"{nm}_{k}"] for k in ("w1", "w2", "b1")])),
                    dict(pool=lambda e: combine_pool(e, l), dve=lambda e: combine_dve(e, l))]

        def attention(l, n=0, gain=None, bias=None):
            return [
                ln(n, gain, bias),
                dict(pe=lambda e: qkv_pe(e, l, n), act=lambda e: qkv_act(e, l), dve=lambda e: qkv_dve(e, l),
                     pool=lambda e: qkv_pool(e, l), sp=lambda e: qkv_sp(e, l)),
                dict(pe=lambda e: attn_pe(e, l), act=lambda e: attn_act(e, l), dve=lambda e: attn_dve(e, l),
                     pool=lambda e: attn_pool(e, l), sp=lambda e: attn_sp(e, l)),
                dict(pe=lambda e: wo_pe(e, l), act=lambda e: wo_act(e, l), pool=lambda e: wo_pool(e, l), dve=lambda e: wo_dve(e, l)),
            ]

        PHASES = [
            dict(sp=embed_sp, dve=embed_dve, pool=embed_pool, pe=embed_pe, act=embed_act),
            *attention(0),
            clear(1), ln(1), router(0, 1),
            *experts(0, "moe0"),
            clear(2), ln(2),
            dict(pe=mamba_pe, act=mamba_act, sp=mamba_sp, dve=mamba_dve, pool=lambda e: add_row(e, "b_out", "b_out_added")),
            clear(3), dict(sp=keep_sp, dve=norm_dve, act=norm_act), *attention(1, 3, "ln1_g", "ln1_b"),
            clear(4), dict(pe=turn_pe, act=turn_act),
            dict(pe=lambda e: mlp_pe(e, "mlp", 1), act=lambda e: mlp_act(e, "mlp", 1), dve=lambda e: mlp_dve(e, "mlp", 1),
                 pool=lambda e: add_row(e, "mlp_b2", "mlp_b2_added"),
                 sp=lambda e: mlp_sp(e, "mlp", 1, [A[f"mlp_{k}"] for k in ("w1", "w2", "b1")])),
            clear(5), ln(4, "ln2_g", "ln2_b"), router(1, 4),
            *experts(1, "moe1", "ln2_g", "ln2_b"),
            dict(sp=last_sp, dve=last_dve),
        ][:stop]

        @block.sync
        def _(sp):
            plan("sp", sp, None)
            store_sp(sp)

        @block.gpsimd
        def _(pool):
            plan("pool", pool, None)

        @block.scalar
        def _(act):
            plan("act", act, None)

        @block.tensor
        def _(pe):
            plan("pe", pe, None)

        @block.vector
        def _(v):
            plan("dve", v, None)


def kernel(**inputs):
    import numpy as np
    import concourse.bacc as bacc
    from concourse.bass_utils import run_bass_kernel_spmd as run

    w = {k: np.asarray(v) for k, v in inputs.items()}

    def chunk(a, n):
        return np.ascontiguousarray(a.reshape(-1, n, a.shape[-1]).transpose(1, 0, 2))

    def col(a, n):
        return a.reshape(-1, n).T

    v96 = {"bq0": w["L0_attn_bq"], "bk0": w["L0_attn_bk"], "ln1_g": w["L1_ffn_ln1_g"], "ln1_b": w["L1_ffn_ln1_b"],
           "bq1": w["L1_ffn_in_b"][0:D], "bk1": w["L1_ffn_in_b"][D:2 * D], "ln2_g": w["L1_ffn_ln2_g"], "ln2_b": w["L1_ffn_ln2_b"]}
    v128 = [w["L1_attn_b_in"][0:DI], w["L1_attn_conv_b"], np.ascontiguousarray(w["L1_attn_conv_w"][:, 0, :].T), w["L1_ffn_mlp_b1"]]

    row = np.concatenate([w["L0_attn_bv"].reshape(-1), w["L1_ffn_in_b"][2 * D:], w["L0_attn_bo"], w["L1_ffn_out_b"],
                          w["L1_attn_b_out"], w["L1_ffn_mlp_b2"], w["L0_tok_norm_w"], w["L0_ffn_bs"], w["L1_ffn_gate_b"]])
    arrays = {
        "x": np.ascontiguousarray(w["x"].reshape(NB, P).T),
        "coords": w["L0_tok_basin_coords"],
        "c96": np.ascontiguousarray(np.concatenate([col(v96[k], DH) for k in C96], 1)),
        "c128": np.ascontiguousarray(np.concatenate([col(v, P) for v in v128], 1)),
        "rows": np.ascontiguousarray(np.broadcast_to(row, (P, NROW))),
        "ident": np.eye(P, dtype=np.float32),
        "projT": np.ascontiguousarray(w["L0_tok_proj_w"].T),
        "wqkv0": chunk(np.concatenate([w[f"L0_attn_W{n}"].reshape(D, D) for n in "qkv"], 1), DH),
        "wo0": chunk(w["L0_attn_Wo"].reshape(D, D), DH),
        "wqkv1": chunk(np.ascontiguousarray(w["L1_ffn_in_w"].T), DH),
        "wo1": chunk(np.ascontiguousarray(w["L1_ffn_out_w"].T), DH),
    }
    def experts(nm, w1, b1, w2):
        E = w1.shape[0]
        arrays[f"{nm}_w1"] = np.ascontiguousarray(w1.reshape(E, DC, DH, FF).transpose(0, 2, 1, 3).reshape(E, DH, DC * FF))
        arrays[f"{nm}_w2"] = np.ascontiguousarray(w2.reshape(E, FC, P, D).transpose(0, 2, 1, 3).reshape(E, P, FC * D))
        arrays[f"{nm}_b1"] = np.ascontiguousarray(b1.reshape(E, FC, P).transpose(0, 2, 1))

    experts("moe0", w["L0_ffn_W1"], w["L0_ffn_b1"], w["L0_ffn_W2"])
    experts("moe1", w["L1_ffn_exp_w1"], w["L1_ffn_exp_b1"], w["L1_ffn_exp_w2"])
    experts("mlp", w["L1_ffn_mlp_w1"][None], w["L1_ffn_mlp_b1"][None], w["L1_ffn_mlp_w2"][None])
    arrays["wr0"] = chunk(w["L0_ffn_Ws"], DH)
    arrays["wr1"] = chunk(np.ascontiguousarray(w["L1_ffn_gate_w"].T), DH)
    arrays["b20"] = w["L0_ffn_b2"]
    arrays["b21"] = w["L1_ffn_exp_b2"]
    arrays["upper"] = np.triu(np.ones((P, P), np.float32), 1)
    arrays["ones"] = np.ones((P, P), np.float32)
    smask = np.ones((P, 2, P), np.float32)
    for l, E in enumerate((E0, E1)):
        smask[:, l, ::P // E] = 0.0
    arrays["smask"] = smask
    arrays["iota"] = np.ascontiguousarray(np.broadcast_to(np.arange(max(NT), dtype=np.float32), (P, max(NT))))
    arrays["order"] = np.ascontiguousarray(np.broadcast_to(np.arange(E0, 0, -1, dtype=np.float32), (P, E0)))
    arrays["w_in"] = chunk(w["L1_attn_W_in"][:, 0:DI + NS], DH)
    w_x = np.zeros((DI, 72), np.float32)
    b_x = np.zeros((72, 1), np.float32)
    w_x[:, 0:NS] = w["L1_attn_W_dt"][:, 0:NS]
    b_x[0:NS, 0] = w["L1_attn_b_dt"][0:NS]
    for q in range(2):
        w_x[:, 32 * (q + 1):32 * (q + 1) + NS] = w["L1_attn_W_x"][:, (2 + q) * NS:(3 + q) * NS]
        b_x[32 * (q + 1):32 * (q + 1) + NS, 0] = w["L1_attn_b_x"][(2 + q) * NS:(3 + q) * NS]
    arrays["w_x"] = chunk(w_x, P)
    arrays["b_x"] = b_x
    arrays["b_z"] = np.ascontiguousarray(w["L1_attn_b_in"][DI:DI + NS, None])
    arrays["w_out"] = np.ascontiguousarray(w["L1_attn_W_out"][0:NS])
    ssum = np.zeros((P, 2, NS), np.float32)
    for p in range(P):
        ssum[p, p // 64, p % 64 // NS] = 1.0
    arrays["ssum"] = ssum
    nc = bacc.Bacc("TRN2", target_bir_lowering=False, num_devices=1)
    A = {k: nc.dram_tensor(f"in_{k}", a.shape, mybir.dt.from_np(a.dtype), kind="ExternalInput").ap() for k, a in arrays.items()}
    out = nc.dram_tensor("out", (T, D), F32, kind="ExternalOutput").ap()
    build(nc, A, out, STOP)
    r = run(nc, [{f"in_{k}": a for k, a in arrays.items()}], core_ids=[0])
    y = r.results[0]["out"]
    return y.reshape(B, S, D)
```

```python
from contextlib import ExitStack

import concourse.bass as bass
from concourse import mybir

F32 = mybir.dt.float32
BF16 = mybir.dt.bfloat16
F16 = mybir.dt.float16
I32 = mybir.dt.int32
ALU = mybir.AluOpType
ACT = mybir.ActivationFunctionType
AX = mybir.AxisListType.X

P = 128
B, S, D = 2, 1024, 192
T = B * S
DC, DH = 2, 96
G = 512
NG = T // G
NB = T // P
VOCAB, BASIN = 32000, 64
HEADS, HD = 12, 16
NH = B * HEADS
NO = 34
TERMS = 6
KA = TERMS * HD
KM = KA + 3
FF, FC = 768, 6
E0, E1 = 8, 4
TOPK = (1, 2)
R = 256
NT = [(T * k - E) // R + E for k, E in zip(TOPK, (E0, E1))]
DI, IC = 384, 3
NS = 8

C96 = {}
for _n in ("bq0", "bk0", "ln1_g", "ln1_b", "bq1", "bk1", "ln2_g", "ln2_b"):
    C96[_n] = 2 * len(C96)
N96 = 2 * len(C96)
C128 = {"b_in": 0, "conv_b": 3, "conv_w": 6, "mlp_b1": 18}
N128 = 24
ROW = {"bv0": 0, "bv1": D, "bo0": 2 * D, "bo1": 3 * D, "b_out": 4 * D, "mlp_b2": 5 * D, "norm_w": 6 * D, "bs": 7 * D, "gb": 7 * D + E0}
NROW = 7 * D + E0 + E1

RECURRING = [
    "counted", "slots_ready", "tile_experts", "xt_evac", "tile_turned", "y_evac", "y_stored0", "y_stored1", "combined",
    "b2_added", "b2_weighted", "bo_added", "cxT_ready", "cx_turned", "k_taken", "max_whole", "exp_router", "gates", "gates_rows",
    "gates_turned", "kq_0", "kq_1", "kq_2", "kq_3", "ln_done", "ln_dve", "ln_root", "ln_scaled", "ln_turned",
    "ln_var", "lo_d", "lo_p", "logits", "max_part", "max_split", "max_turned", "mlp_added",
    "mlp_b2_added", "mlp_down", "mlp_gelu", "mlp_up", "mlp_w0", "mlp_w1", "mlp_v0", "mlp_v1", "mrow_0", "mrow_1", "mrow_2",
    "mrow_3", "norm_done", "rc_ready", "o_evac", "o_turned", "pv_done", "qk_evac", "qk_hi", "qk_lo",
    "qk_mid", "qk_projected", "qk_rest", "qk_stored00", "qk_stored01", "qk_stored10", "qk_stored11", "router_dve", "shifted", "sk_done", "sq_done", "v_evac", "v_hi",
    "v_lo", "v_projected", "vs_ready", "vs_zeroed", "wo_added", "wo_projected",
]



class Chain:

    def __init__(self, eng, sem, base=0):
        self.eng, self.sem, self.base, self.n = eng, sem, base, 0

    def __call__(self, ins):
        self.n += 1
        ins.then_inc(self.sem, 1)
        self.eng.wait_ge(self.sem, self.base + self.n)


def build(nc, A, out):
    ctx = ExitStack()
    with ctx:
        def sb(name, shape, dt):
            return ctx.enter_context(nc.sbuf_tensor(name, shape, dt))

        sems = {}

        def sem(name):
            if name not in sems:
                sems[name] = ctx.enter_context(nc.semaphore(name))
            return sems[name]

        for name in RECURRING:
            sem(name)
        numbers = [sems[name].num for name in RECURRING]
        assert numbers == list(range(numbers[0], numbers[0] + len(numbers)))

        def clear(k):
            def wait(eng):
                eng.wait_ge(sem("cleared"), k)
            return [MEET, dict(sp=lambda e: e.sem_clear(range(numbers[0], numbers[-1] + 1)).then_inc(sem("cleared"), 1),
                               pe=wait, act=wait, dve=wait, pool=wait), MEET]

        def dram(name, shape, dt):
            return nc.dram_tensor(name, shape, dt, kind="Internal").ap()

        PS = ctx.enter_context(nc.psum_tensor("PS", [P, 8, 512], F32))
        H = sb("H", [P, NB, D], F32)
        XN = sb("XN", [DH, DC, T], F32)
        c96 = sb("c96", [DH, N96], F32)
        c128 = sb("c128", [P, N128], F32)
        rows = sb("rows", [P, NROW], F32)
        ident = sb("ident", [P, P], F32)
        zrow = sb("zrow", [P, D], F32)
        epsc = sb("epsc", [P, 2], F32)
        projT = sb("projT", [BASIN, D], F32)
        wqkv = [sb(f"wqkv{l}", [DH, DC, 3 * D], F32) for l in range(2)]
        wo = [sb(f"wo{l}", [DH, DC, D], F32) for l in range(2)]
        wr = [sb(f"wr{l}", [DH, DC, E], F32) for l, E in enumerate((E0, E1))]
        b2 = [sb(f"b2{l}", [E, D], F32) for l, E in enumerate((E0, E1))]
        join = sb("join", [P, NO], F32)
        upper = sb("upper", [P, P], F32)
        ones = sb("ones", [P, P], F32)
        smask = sb("smask", [P, 2, P], F32)
        iota = sb("iota", [P, max(NT)], F32)
        order = sb("order", [P, E0], F32)
        w_in = sb("w_in", [DH, DC, DI + NS], F32)
        w_x = sb("w_x", [P, IC, 72], F32)
        b_x = sb("b_x", [72, 1], F32)
        b_z = sb("b_z", [NS, 1], F32)
        w_out = sb("w_out", [NS, D], F32)
        ssum = sb("ssum", [P, 2, NS], F32)
        ARENA = 37700
        arena = sb("arena", [P, ARENA], F32)
        cur = [0]

        def at(shape, dt, reset=None):
            if reset is not None:
                cur[0] = reset
            n = 1
            for s in shape[1:]:
                n *= s
            words = n if dt in (F32, I32) else (n + 1) // 2
            o = cur[0]
            cur[0] += words
            assert cur[0] <= ARENA, (cur[0], ARENA)
            v = arena[0:shape[0], o:o + words]
            if dt != F32:
                v = v.bitcast(dt)
            if len(shape) > 2:
                names = "abcdef"[:len(shape) - 1]
                v = v.rearrange(f"p ({' '.join(names)}) -> p {' '.join(names)}", **{k: s for k, s in zip(names, shape[1:])})
            return v

        idx_in = at([P, NB], I32, 4096)
        idx_f = at([P, NB], F32)
        idx_w = at([P, NB], F32)
        idx = at([P, NB], I32)
        emb = at([P, NB, BASIN], F32)
        embT = at([BASIN, T], F32)
        sq_e = at([P, D], F32)
        ms_e = at([P, NB], F32)
        rr_e = at([P, NB], F32)
        XT = at([P, NB, D], F32, 0)
        ST = at([P, NB, 6], F32)
        MV = at([P, NB, 2], F32)
        RS = at([P, NB], F32)
        RI = at([P, NB], F32)
        VC = at([P, NH, 8, 2, HD], BF16, 0)
        VS = at([P, 2, 8, 2, P], BF16)
        KQ = [[at([KM, S], BF16) for _ in range(4)] for _ in range(2)]
        MH = at([P, 4, 8, 2], F32)
        MX = at([P, 2, 8], F32)
        MR = at([8, P], F32)
        MP = at([8, 4, 3, P], BF16)
        os_at = cur[0]
        OS = at([P, 2, S], F32)
        OT = at([P, 8, NO], F32)
        RC = at([P, 8, 2], F32)
        CX = at([P, 8, B * D], F32)
        mark = cur[0]
        W1s = at([DH, 2, DC, FF], F32, 4096)
        W2s = at([P, 2, FC, D], F32)
        B1s = at([P, 2, FC], F32)
        HT = at([P, 2, FC, G], F32)
        LG = at([P, NB, E0], F32)
        L2 = at([P, NB, E0], F32)
        EX = at([P, NB, E0], F32)
        SELF = at([P, P], F32)
        GT = at([P, NB, E0], F32)
        GK = at([P, 2, NB], F32)
        CNT = at([P, P], F32)
        INC = at([P, P], F32)
        POS = at([P, P], F32)
        TI = at([P, E0], I32)
        TF = at([P, E0], F32)
        TINC = at([P, E0], F32)
        TB = at([P, E0], F32)
        SLF = at([P, 2 * NB], F32)
        SLOT = at([P, 2 * NB], I32)
        GE = at([P, max(NT), E0], F32)
        TEF = at([P, max(NT)], F32)
        TE = at([P, max(NT)], I32)
        XIN = at([P, 2, 2, D], F32)
        XTT = at([DH, 2, DC, R], F32)
        YB = at([P, 2, 2, D], F32)
        YGT = at([P, 2 * NB, D], F32)
        t1 = at([P, NB], F32)
        t2 = at([P, NB], F32)
        t3 = at([P, NB], F32)
        GTT = at([E0, T], F32)
        XC = at([P, IC, B, S + 3], F32, 4096)
        XV = at([P, IC, T], F32)
        XS = at([P, IC, T], F32)
        RT = at([72, T], F32)
        ZT = at([NS, T], F32)
        ZS = at([NS, T], F32)
        YG = at([NS, T], F32)
        REP = [at([P, S], F32) for _ in range(4)]
        UU = at([P, S], F32)
        HH = at([P, S], F32)
        q32 = at([DH, 4, G], F32, os_at)
        r32 = at([DH, 4, G], F32)
        v32 = at([P, 4, D], F32)
        assert cur[0] <= mark
        CXT = at([DH, DC, T], F32, mark)
        PR = at([P, 8, S], F32, mark)
        LO = at([P, 8, S], F16)
        parts = at([DH, 2, 3, DC, T], BF16, mark)

        QK = [[dram(f"{n}parts{l}", [NH, 3, HD, S], BF16) for n in "kq"] for l in range(2)]

        XSORT = [dram(f"xsort{l}", [NT[l] * R, D], F32) for l in range(2)]
        YSORT = [dram(f"ysort{l}", [NT[l] * R, D], F32) for l in range(2)]

        block = ctx.enter_context(nc.Block())

        def barrier(eng, k):
            s = sem("phase_left")
            eng.drain().then_inc(s, 1)
            eng.wait_ge(s, 5 * k)

        FIRST_LOADS = [(ident[:, :], A["ident"]), (projT[:, :], A["projT"]), (rows[:, :], A["rows"])]
        LOADS = [(c96[:, :], A["c96"]), (c128[:, :], A["c128"]),
                 (wqkv[0][:, :, :], A["wqkv0"]), (wo[0][:, :, :], A["wo0"]),
                 (wqkv[1][:, :, :], A["wqkv1"]), (wo[1][:, :, :], A["wo1"]),
                 (wr[0][:, :, :], A["wr0"]), (wr[1][:, :, :], A["wr1"]), (b2[0][:, :], A["b20"]), (b2[1][:, :], A["b21"]),
                 (order[:, :], A["order"]), (upper[:, :], A["upper"]), (join[:, :], A["join"]), (ones[:, :], A["ones"]),
                 (smask[:, :, :], A["smask"]), (iota[:, :], A["iota"]), (w_in[:, :, :], A["w_in"]), (w_x[:, :, :], A["w_x"]), (b_x[:, :], A["b_x"]),
                 (b_z[:, :], A["b_z"]), (w_out[:, :], A["w_out"]), (ssum[:, :, :], A["ssum"])]

        def embed_sp(sp):
            sp.dma_start(idx_in[:, :], A["x"]).then_inc(sem("idx_loaded"), 16)
            for dst, src in FIRST_LOADS:
                sp.dma_start(dst, src).then_inc(sem("first_consts"), 16)
            for dst, src in LOADS:
                sp.dma_start(dst, src).then_inc(sem("consts"), 16)

        def first_loaded(eng):
            eng.wait_ge(sem("first_consts"), 16 * len(FIRST_LOADS))

        def consts_loaded(eng):
            eng.wait_ge(sem("consts"), 16 * len(LOADS))

        def embed_dve(v):
            v.memset(zrow[:, :], 0.0).then_inc(sem("zeros_set"), 1)
            v.memset(epsc[:, 0:1], 1e-5)
            v.memset(epsc[:, 1:2], 1e-8).then_inc(sem("eps_set"), 1)
            c = Chain(v, sem("embed_dve"))
            v.wait_ge(sem("idx_loaded"), 16)
            c(v.tensor_scalar(idx_w[:, :], idx_in[:, :], 0.0, float(VOCAB), ALU.is_lt, ALU.mult))
            c(v.tensor_tensor(idx_f[:, :], idx_in[:, :], idx_w[:, :], ALU.add))
            v.tensor_scalar(idx[:, :], idx_f[:, :], 0.0, float(VOCAB - 1), ALU.max, ALU.min).then_inc(sem("idx_ready"), 1)
            first_loaded(v)
            o = ROW["norm_w"]

            def finish(g):
                v.wait_ge(sem("rms_root"), g + 1)
                c(v.reciprocal(rr_e[:, 4 * g:4 * g + 4], rr_e[:, 4 * g:4 * g + 4]))
                for b in range(4 * g, 4 * g + 4):
                    v.scalar_tensor_tensor(H[:, b, :], H[:, b, :], rr_e[:, b:b + 1], rows[:, o:o + D], ALU.mult, ALU.mult)\
                     .then_inc(sem("H_embedded"), 1)
                for b in range(4 * g, 4 * g + 4):
                    v.wait_ge(sem("H_embedded"), b + 1)
                    stats(v, b)

            for g in range(NG):
                for b in range(4 * g, 4 * g + 4):
                    v.wait_ge(sem("emb_projected"), b + 1)
                    v.tensor_copy(H[:, b, :], PS[:, 4 + b % 4, 0:D]).then_inc(sem("emb_evac"), 1)
                if g:
                    finish(g - 1)
            finish(NG - 1)
            consts_loaded(v)

        def embed_pool(pool):
            pool.wait_ge(sem("idx_ready"), 1)
            for blk in range(NB):
                pool.indirect_dma_start(emb[:, blk, :], None, A["coords"], bass.IndirectOffsetOnAxis(ap=idx[:, blk:blk + 1], axis=0)).then_inc(sem(f"gathered{blk // 4}"), 16)

        def embed_pe(pe):
            first_loaded(pe)
            for b in range(NB):
                g = b // 4
                if b % 4 == 0:
                    for q in range(4):
                        blk = 4 * g + q
                        pe.wait_ge(sem(f"gathered{g}"), 64)
                        last = pe.transpose(PS[0:BASIN, g, q * P:(q + 1) * P], emb[:, blk, :], ident[:, :])
                    last.then_inc(sem("embT_turned"), 1)
                pe.wait_ge(sem("embT_ready"), g + 1)
                if b >= 4:
                    pe.wait_ge(sem("emb_evac"), b - 3)
                pe.matmul(PS[:, 4 + b % 4, 0:D], embT[:, b * P:(b + 1) * P], projT[:, :], start=True, stop=True)\
                  .then_inc(sem("emb_projected"), 1)
            consts_loaded(pe)

        def embed_act(act):
            c = Chain(act, sem("embed_act"))
            act.wait_ge(sem("eps_set"), 1)
            for g in range(NG):
                act.wait_ge(sem("embT_turned"), g + 1)
                act.activation(embT[:, g * G:(g + 1) * G], PS[0:BASIN, g, :], ACT.Copy).then_inc(sem("embT_ready"), 1)
                for b in range(4 * g, 4 * g + 4):
                    act.wait_ge(sem("emb_evac"), b + 1)
                    c(act.activation(sq_e[:, :], H[:, b, :], ACT.Square, accum_out=ms_e[:, b:b + 1]))
                act.activation(rr_e[:, 4 * g:4 * g + 4], ms_e[:, 4 * g:4 * g + 4], ACT.Sqrt, bias=epsc[:, 1:2], scale=1.0 / D)\
                   .then_inc(sem("rms_root"), 1)

        BEFORE = {0: 1, 1: 2, 2: 3, "again": 4, 3: 5, 4: 6}

        def stats(v, b):
            if b >= 0:
                v.bn_stats(ST[:, b, :], H[:, b, :]).then_inc(sem("blocks_seen"), 1)

        def ln_dve(v, n):
            c = Chain(v, sem("ln_dve"))
            v.wait_ge(sem("blocks_seen"), NB * BEFORE[n])
            for b in range(NB):
                last = v.bn_aggr(MV[:, b, :], ST[:, b, :])
            last.then_inc(sem("ln_var"), 1)
            v.wait_ge(sem("ln_root"), 1)
            c(v.reciprocal(RI[:, :], RS[:, :]))
            for b in range(NB):
                v.tensor_scalar(XT[:, b, :], H[:, b, :], MV[:, b, 0:1], RI[:, b:b + 1], ALU.subtract, ALU.mult)\
                 .then_inc(sem("ln_scaled"), 1)

        def ln_act(act, n, gain=None, bias=None):
            act.wait_ge(sem("ln_var"), 1)
            act.activation(RS[:, :], MV[:, :, 1], ACT.Sqrt, bias=epsc[:, 0:1]).then_inc(sem("ln_root"), 1)
            for j in range(NG * DC):
                g, k = j // DC, j % DC
                act.wait_ge(sem("ln_turned"), j + 1)
                dst, src = XN[:, k, g * G:(g + 1) * G], PS[0:DH, j, :]
                if gain is None:
                    ins = act.activation(dst, src, ACT.Copy)
                else:
                    ins = act.activation(dst, src, ACT.Identity, scale=c96[:, C96[gain] + k:C96[gain] + k + 1],
                                         bias=c96[:, C96[bias] + k:C96[bias] + k + 1])
                ins.then_inc(sem("ln_done"), 1)

        def ln_pe(pe, n):
            for j in range(NG * DC):
                g, k = j // DC, j % DC
                for q in range(4):
                    b = 4 * g + q
                    pe.wait_ge(sem("ln_scaled"), b + 1)
                    last = pe.transpose(PS[0:DH, j, q * P:(q + 1) * P], XT[:, b, k * DH:(k + 1) * DH], ident[:, :])
                last.then_inc(sem("ln_turned"), 1)

        NJ = 4 * NG

        def job(j):
            return 2 * (j // 8) + j % 2, j // 2 % 2, j // 4 % 2

        def qkv_pe(pe, l, n):
            for j in range(NJ):
                g, qk, ch = job(j)
                pe.wait_ge(sem("ln_done"), max(2 * g + 2, min(j, 3) + 1))
                if j >= 4:
                    pe.wait_ge(sem("qk_evac"), j - 3)
                col = (1 - qk) * D + ch * DH
                for k in range(DC):
                    last = pe.matmul(PS[0:DH, j % 4, :], wqkv[l][:, k, col:col + DH], XN[:, k, g * G:(g + 1) * G],
                                     start=k == 0, stop=k == 1)
                last.then_inc(sem("qk_projected"), 1)
            for b in range(NB):
                if b >= 4:
                    pe.wait_ge(sem("v_evac"), b - 3)
                for k in range(DC):
                    last = pe.matmul(PS[:, 4 + b % 4, 0:D], XN[:, k, b * P:(b + 1) * P], wqkv[l][:, k, 2 * D:3 * D],
                                     start=k == 0, stop=k == 1)
                last.then_inc(sem("v_projected"), 1)

        def qkv_dve(v, l):
            for j in range(NJ + 1):
                if j < NJ:
                    g, qk, ch = job(j)
                    v.wait_ge(sem("qk_projected"), j + 1)
                    if j >= 4:
                        v.wait_ge(sem("qk_rest"), j - 3)
                    o = C96[("bk", "bq")[qk] + str(l)] + ch
                    v.tensor_scalar(q32[:, j % 4, :], PS[0:DH, j % 4, :], c96[:, o:o + 1], (1.0, HD ** -0.5)[qk],
                                    ALU.add, ALU.mult).then_inc(sem("qk_evac"), 1)
                if j >= 1:
                    v.wait_ge(sem("qk_hi"), j)
                    if j >= 5:
                        v.wait_ge(sem("qk_lo"), j - 4)
                    v.tensor_tensor(r32[:, (j - 1) % 4, :], q32[:, (j - 1) % 4, :], part(j - 1, 0), ALU.subtract).then_inc(sem("qk_rest"), 1)
            for b in range(NB):
                v.wait_ge(sem("v_projected"), b + 1)
                if b >= 4:
                    v.wait_ge(sem("v_lo"), b - 3)
                o = ROW[f"bv{l}"]
                v.tensor_tensor(v32[:, b % 4, :], PS[:, 4 + b % 4, 0:D], rows[:, o:o + D], ALU.add).then_inc(sem("v_evac"), 1)

        def part(j, n):
            g, qk, ch = job(j)
            return parts[:, qk, n, ch, g * G:(g + 1) * G]

        def vpart(b, n):
            return VC[:, b // 8 * HEADS:(b // 8 + 1) * HEADS, b % 8, n, :]

        def heads(ap):
            return ap.rearrange("p (h d) -> p h d", h=HEADS)

        def qkv_act(act, l):
            for j in range(NJ + 1):
                if j < NJ:
                    act.wait_ge(sem("qk_evac"), j + 1)
                    act.activation(part(j, 0), q32[:, j % 4, :], ACT.Copy).then_inc(sem("qk_hi"), 1)
                if j >= 1:
                    act.wait_ge(sem("qk_rest"), j)
                    act.activation(part(j - 1, 1), r32[:, (j - 1) % 4, :], ACT.Copy).then_inc(sem("qk_mid"), 1)
            for b in range(NB):
                act.wait_ge(sem("v_evac"), b + 1)
                act.activation(vpart(b, 0), heads(v32[:, b % 4, :]), ACT.Copy).then_inc(sem("v_hi"), 1)

        def qkv_pool(pool, l):
            pool.wait_ge(sem("ln_scaled"), NB)
            for s in range(4):
                pool.memset(KQ[0][s][KA:KM, :], -1.0)
            pool.drain()
            pool.memset(VS[:, :, :, :, 0:64], 0.0)
            pool.memset(VS[:, :, :, :, 64:P], 0.0).then_inc(sem("vs_zeroed"), 1)
            pool.wait_ge(sem("vs_zeroed"), 1)
            pool.memset(VS[:, :, :, 0, 64:80], 1.0)
            pool.memset(VS[:, :, :, 0, 96:112], 1.0)
            pool.memset(VS[:, :, :, 1, 80:96], 1.0)
            pool.memset(VS[:, :, :, 1, 112:128], 1.0).then_inc(sem("vs_zeroed"), 1)
            for j in range(NJ):
                pool.wait_ge(sem("qk_mid"), j + 1)
                pool.tensor_tensor(part(j, 2), r32[:, j % 4, :], part(j, 1), ALU.subtract).then_inc(sem("qk_lo"), 1)
            for b in range(NB):
                pool.wait_ge(sem("v_hi"), b + 1)
                pool.tensor_tensor(vpart(b, 1), heads(v32[:, b % 4, :]), vpart(b, 0), ALU.subtract).then_inc(sem("v_lo"), 1)
            o = ROW[f"bo{l}"]
            for b in range(NB):
                last = pool.tensor_tensor(H[:, b, :], H[:, b, :], rows[:, o:o + D], ALU.add)
            last.then_inc(sem("bo_added"), 1)

        def qkv_sp(sp, l):
            for b in range(B):
                for ch in range(DC):
                    sp.wait_ge(sem("qk_lo"), 4 * (2 * b + ch + 1))
                    h0 = b * HEADS + 6 * ch
                    for qk in range(2):
                        for n in range(3):
                            sp.dma_start(QK[l][qk][h0:h0 + 6, n], parts[:, qk, n, ch, b * S:(b + 1) * S])\
                              .then_inc(sem(f"qk_stored{b}{ch}"), 16)

        QK_STORED = 16 * 2 * 3

        NV = 8 * NH
        ALEAD, BLEAD = 16, 4
        LO_AT = {"p": slice(0, 832), "d": slice(832, S)}

        LO_LAST = {"p": slice(0, 384), "d": slice(384, S)}

        def steps(eng, body):
            body(0, 0)
            with eng.Fori(1, NV // 32 - 1) as i:
                body(i, None)
            body(NV // 32 - 1, NV - 32)

        def key_place(i, x):
            return x + max((x - 10) // 16, 0) if isinstance(i, int) and i == 0 else x + (x - 10) // 16

        def turn_place(i, pair):
            last = isinstance(i, int) and 2 * i + pair == NH // 2 - 1
            return 33 if last else 17 * (pair + 1) + 9

        CX_BANK = (0, 1, 6, 7, 2, 3, 4, 5)

        def turn_cx(pe, j):
            g, k = j // DC, j % DC
            for q in range(4):
                b = 4 * g + q
                src = CX[:, b % 8, b // 8 * D + k * DH:b // 8 * D + (k + 1) * DH]
                last = pe.transpose(PS[0:DH, CX_BANK[j], q * P:(q + 1) * P], src, ident[:, :])
            last.then_inc(sem("cx_turned"), 1)

        def attn_pe(pe, l):
            def scores_q(i, x):
                s, qb = x // 8 % 4, x % 8
                if qb == 0:
                    pe.wait_ge(sem(f"kq_{s}"), 96 * i + 96 * (x // 32 + 1))
                first = isinstance(i, int) and 32 * i + x == 0
                for half in range(2):
                    if qb == 0 and half == 1 and not first:
                        pe.wait_ge(sem("max_split"), 16 * i + 4 * (x // 8) - 2)
                    if not first:
                        pe.wait_ge(sem("max_part"), 64 * i + 2 * x + half - 1)
                    pe.matmul(PS[:, half, :], KQ[1][s][0:KA, qb * P:(qb + 1) * P],
                              KQ[0][s][0:KA, half * 512:(half + 1) * 512], start=True, stop=True).then_inc(sem("sq_done"), 1)

            def turn_max(i, h):
                pe.wait_ge(sem("max_whole"), 4 * i + h + 1)
                pe.transpose(PS[0:8, 1, 0:P], MX[:, h % 2, :], ident[:, :]).then_inc(sem("max_turned"), 1)

            def scores_k(i, x):
                s, kb = x // 8 % 4, x % 8
                if kb == 0:
                    pe.wait_ge(sem(f"mrow_{s}"), 48 * i + 48 * (x // 32 + 1))
                q = key_place(i, x)
                if not (isinstance(i, int) and 34 * i + q < 2):
                    pe.wait_ge(sem("k_taken"), 34 * i + q - 1)
                for half in range(2):
                    last = pe.matmul(PS[:, 2 + 2 * (q % 2) + half, :], KQ[0][s][:, kb * P:(kb + 1) * P],
                                     KQ[1][s][:, half * 512:(half + 1) * 512], start=True, stop=True)
                last.then_inc(sem("sk_done"), 1)

            def values(i, x, between):
                s, kb, pair = x // 8 % 2, x % 8, x // 16
                first, lastt = x % 16 == 0, x % 16 == 15
                if first:
                    pe.wait_ge(sem("vs_ready"), 2 * i + pair + 1)
                    if not (isinstance(i, int) and i == 0 and pair == 0):
                        pe.wait_ge(sem("o_evac"), 2 * i + pair)
                pe.wait_ge(sem("lo_p"), 32 * i + x + 1)
                pe.wait_ge(sem("lo_d"), 32 * i + x + 1)
                lhsT = VS[:, pair, kb, s, :]
                hi = PR[:, x % 8, :].bitcast(BF16).rearrange("p (n two) -> p n two", two=2)
                for q in range(2):
                    pe.matmul(PS[:, 6 + q, :], lhsT, hi[:, q * 512:(q + 1) * 512, 1], start=first, stop=False)
                between()
                for q in range(2):
                    last = pe.matmul(PS[:, 6 + q, :], lhsT, LO[:, x % 8, q * 512:(q + 1) * 512], start=False, stop=lastt)
                last.then_inc(sem("pv_done"), 1)

            def turn_out(i, pair):
                if isinstance(i, int) and 2 * i + pair < 0:
                    return
                q = turn_place(i, pair)
                pe.wait_ge(sem("o_evac"), 2 * i + pair + 1)
                pe.wait_ge(sem("k_taken"), 34 * i + q - 1)
                for k in range(8):
                    last = pe.matmul(PS[:, 2 + 2 * (q % 2), k * NO:(k + 1) * NO], OS[:, pair % 2, k * P:(k + 1) * P], join[:, :],
                                     start=True, stop=True)
                last.then_inc(sem("o_turned"), 1)

            pe.wait_ge(sem("qk_evac"), NJ)
            pe.wait_ge(sem("v_evac"), NB)
            for a in range(ALEAD):
                if a and a % 8 == 0:
                    turn_max(0, a // 8 - 1)
                scores_q(0, a)
                if a >= ALEAD - BLEAD:
                    scores_k(0, a - (ALEAD - BLEAD))

            def body(i, v0):
                for x in range(32):
                    if x % 16 == 6:
                        turn_out(i, x // 16 - 1)
                    if v0 is None or v0 + x + BLEAD < NV:
                        scores_k(i, x + BLEAD)

                    def between():
                        if (v0 is None or v0 + x + ALEAD <= NV) and (x + ALEAD) % 8 == 0:
                            turn_max(i, (x + ALEAD) // 8 - 1)

                    values(i, x, between)
                    if v0 is None or v0 + x + ALEAD < NV:
                        scores_q(i, x + ALEAD)

            steps(pe, body)
            pe.wait_ge(sem("max_split"), 4 * NH)
            for j in range(2):
                turn_cx(pe, j)
            turn_out(NV // 32 - 1, 1)
            for j in range(2, 4):
                turn_cx(pe, j)

        def copy_cx(act, j):
            g, k = j // DC, j % DC
            act.wait_ge(sem("cx_turned"), j + 1)
            act.activation(CXT[:, k, g * G:(g + 1) * G], PS[0:DH, CX_BANK[j], :], ACT.Copy).then_inc(sem("cxT_ready"), 1)

        def attn_act(act, l):
            def evac(i, pair):
                first = isinstance(i, int) and 2 * i + pair < 0
                if first:
                    return
                act.wait_ge(sem("pv_done"), 32 * i + 16 * (pair + 1))
                if not (isinstance(i, int) and 2 * i + pair < 2):
                    act.wait_ge(sem("o_turned"), 2 * i + pair - 1)
                act.activation(OS[:, pair % 2, :].rearrange("p (a b) -> p a b", a=2), PS[:, 6:8, :], ACT.Copy)\
                   .then_inc(sem("o_evac"), 1)

            def copy_values(i, pair):
                for s in range(2):
                    dst = VS[:, pair % 2, :, s, 0:64].rearrange("p k (n c) -> p k n c", n=2)[:, :, :, s * HD:(s + 1) * HD]
                    h = 2 * pair + s
                    if isinstance(i, int):
                        src = VC[:, 4 * i + h]
                    else:
                        src = VC[:, bass.ds(4 * i + h, 1)].rearrange("p o k n c -> p (o k) n c")
                    last = act.activation(dst, src, ACT.Copy)
                last.then_inc(sem("vs_ready"), 1)

            def turned(i, pair):
                if isinstance(i, int) and 2 * i + pair < 0:
                    return
                act.wait_ge(sem("o_turned"), 2 * i + pair + 1)
                if not (isinstance(i, int) and 2 * i + pair < 1):
                    act.wait_ge(sem("norm_done"), 2 * i + pair)
                q = turn_place(i, pair)
                act.activation(OT[:, :, :].rearrange("p k n -> p (k n)"), PS[:, 2 + 2 * (q % 2), 0:8 * NO], ACT.Copy)\
                   .then_inc(sem("k_taken"), 1)

            def body(i, v0):
                for x in range(32):
                    if x % 16 == 10:
                        turned(i, x // 16 - 1)
                    q = key_place(i, x)
                    act.wait_ge(sem("sk_done"), 32 * i + x + 1)
                    if not (isinstance(i, int) and 32 * i + x < 8):
                        act.wait_ge(sem("pv_done"), 32 * i + x - 7)
                    act.activation(PR[:, x % 8, :].rearrange("p (a b) -> p a b", a=2),
                                   PS[:, 2 + 2 * (q % 2):4 + 2 * (q % 2), :], ACT.Exp).then_inc(sem("k_taken"), 1)
                    if x % 16 == 3:
                        evac(i, x // 16 - 1)
                    if x % 16 == 8 and (v0 is None or v0 + x + 8 < NV):
                        if not (isinstance(i, int) and i == 0 and x == 8):
                            act.wait_ge(sem("pv_done"), 32 * i + x - 8)
                        copy_values(i, x // 16 + 1)

            for n in ("00", "01", "10", "11"):
                act.wait_ge(sem("qk_stored" + n), QK_STORED)
            act.wait_ge(sem("v_lo"), NB)
            act.wait_ge(sem("vs_zeroed"), 2)
            copy_values(0, 0)
            steps(act, body)
            evac(NV // 32 - 1, 1)
            copy_cx(act, 0)
            copy_cx(act, 1)
            turned(NV // 32 - 1, 1)
            copy_cx(act, 2)
            copy_cx(act, 3)

        def lo_part(eng, l, i, x, w):
            q = key_place(i, x)
            eng.wait_ge(sem("k_taken"), 34 * i + q + 1)
            if not (isinstance(i, int) and 32 * i + x < 8):
                eng.wait_ge(sem("pv_done"), 32 * i + x - 7)
            hi = PR[:, x % 8, :].bitcast(BF16).rearrange("p (n two) -> p n two", two=2)[:, :, 1]
            last = isinstance(i, int) and 32 * i + x >= NV - ALEAD
            c = (LO_LAST if last else LO_AT)[w]
            eng.tensor_tensor(LO[:, x % 8, c], PR[:, x % 8, c], hi[:, c], ALU.subtract).then_inc(sem(f"lo_{w}"), 1)

        def attn_pool(pool, l):
            def body(i, v0):
                for x in range(32):
                    lo_part(pool, l, i, x, "p")
            steps(pool, body)

        def attn_dve(v, l):
            def reduce_max(i, x):
                for half in range(2):
                    v.wait_ge(sem("sq_done"), 64 * i + 2 * x + half + 1)
                    v.tensor_reduce(MH[:, x // 8 % 4, x % 8, half:half + 1], PS[:, half, :], AX, ALU.max).then_inc(sem("max_part"), 1)
                if x % 8 == 7:
                    v.wait_ge(sem("max_part"), 64 * i + 2 * x + 2)
                    v.tensor_reduce(MX[:, x // 8 % 2, :], MH[:, x // 8 % 4, :, :], AX, ALU.max).then_inc(sem("max_whole"), 1)

            def max_rows(i, h):
                c = Chain(v, sem("max_split"), 16 * i + 4 * h)
                v.wait_ge(sem("max_turned"), 4 * i + h + 1)
                if not (isinstance(i, int) and 4 * i + h < 4):
                    v.wait_ge(sem(f"mrow_{h % 4}"), 48 * i + 48 * (h // 4))
                m = [MP[:, h % 4, n, :] for n in range(3)]
                c(v.tensor_copy(m[0], PS[0:8, 1, 0:P]))
                c(v.tensor_tensor(MR[:, :], PS[0:8, 1, 0:P], m[0], ALU.subtract))
                c(v.tensor_copy(m[1], MR[:, :]))
                c(v.tensor_tensor(m[2], MR[:, :], m[1], ALU.subtract))

            def cx_at(i, pair):
                if isinstance(i, int):
                    return CX[:, :, 32 * (2 * i + pair):32 * (2 * i + pair) + 32]
                return CX[:, :, bass.ds(64 * i + 32 * pair, 32)]

            def normalise(i, pair):
                if isinstance(i, int) and 2 * i + pair < 0:
                    return
                v.wait_ge(sem("k_taken"), 34 * i + turn_place(i, pair) + 1)
                v.reciprocal(RC[:, :, :], OT[:, :, 32:34]).then_inc(sem("rc_ready"), 1)
                v.wait_ge(sem("rc_ready"), 2 * i + pair + 1)
                v.tensor_tensor(cx_at(i, pair).rearrange("p k (h d) -> p k h d", h=2), OT[:, :, 0:32].rearrange("p k (h d) -> p k h d", h=2),
                                RC[:, :, :].unsqueeze(3).broadcast_to([P, 8, 2, HD]), ALU.mult).then_inc(sem("norm_done"), 1)
                v.wait_ge(sem("norm_done"), 2 * i + pair + 1)

            for a in range(ALEAD):
                if a and a % 8 == 0:
                    max_rows(0, a // 8 - 1)
                reduce_max(0, a)
            for x in range(2):
                lo_part(v, l, 0, x, "d")

            def body(i, v0):
                for x in range(32):
                    if v0 is None or v0 + x + ALEAD <= NV:
                        if (x + ALEAD) % 8 == 0:
                            max_rows(i, (x + ALEAD) // 8 - 1)
                    if v0 is None or v0 + x + ALEAD < NV:
                        reduce_max(i, x + ALEAD)
                    if v0 is None or v0 + x + 2 < NV:
                        lo_part(v, l, i, x + 2, "d")
                    if x % 16 == 11:
                        normalise(i, x // 16 - 1)

            steps(v, body)
            normalise(NV // 32 - 1, 1)

        def attn_sp(sp, l):
            def load(i, h):
                for qk in range(2):
                    if isinstance(i, int):
                        src = QK[l][qk][4 * i + h]
                    else:
                        src = QK[l][qk][bass.ds(4 * i + h, 1)].rearrange("o t d q -> (o t) d q")
                    row = 0
                    for n in range(3):
                        t = 3 - n
                        a = src[n:n + 1].broadcast_to([t, HD, S]) if qk else src[0:t]
                        sp.dma_start(KQ[qk][h % 4][row:row + t * HD, :], a).then_inc(sem(f"kq_{h % 4}"), 16)
                        row += t * HD

            def max_row(i, h):
                sp.wait_ge(sem("max_split"), 16 * i + 4 * (h + 1))
                for n in range(3):
                    sp.dma_start(KQ[1][h % 4][KA + n:KA + n + 1, :], MP[:, h % 4, n, :]).then_inc(sem(f"mrow_{h % 4}"), 16)

            sp.wait_ge(sem("qk_stored00"), QK_STORED)
            for h in range(4):
                load(0, h)
            for n in ("01", "10", "11"):
                sp.wait_ge(sem("qk_stored" + n), QK_STORED)
            max_row(0, 0)
            with sp.Fori(0, NH // 4 - 1) as i:
                for h in range(1, 5):
                    max_row(i, h)
                    sp.wait_ge(sem("sk_done"), 32 * i + 8 * h)
                    load(i, h + 3)
            for h in range(1, 4):
                max_row(NH // 4 - 1, h)
            if l == 0:
                sp.wait_ge(sem("zeros_set"), 1)
                for n in range(2):
                    sp.dma_start(XSORT[n].rearrange("(j p) d -> p j d", p=P), zrow[:, :].unsqueeze(1).broadcast_to([P, NT[n] * R // P, D]))\
                      .then_inc(sem("rows_zeroed"), 16)

        def wo_pe(pe, l):
            pe.wait_ge(sem("norm_done"), NH // 2)
            for j in range(4, NG * DC):
                turn_cx(pe, j)
            for b in range(NB):
                pe.wait_ge(sem("cxT_ready"), 2 * (b // 4) + 2)
                pe.wait_ge(sem("cxT_ready"), min(b % 8 + 1, 8))
                if b >= 8:
                    pe.wait_ge(sem("wo_added"), b - 7)
                for k in range(DC):
                    last = pe.matmul(PS[:, CX_BANK[b % 8], 0:D], CXT[:, k, b * P:(b + 1) * P], wo[l][:, k, :], start=k == 0, stop=k == 1)
                last.then_inc(sem("wo_projected"), 1)

        def wo_act(act, l):
            for j in range(4, NG * DC):
                copy_cx(act, j)

        def wo_dve(v, l):
            v.wait_ge(sem("bo_added"), 1)
            for b in range(NB):
                v.wait_ge(sem("wo_projected"), b + 1)
                v.tensor_tensor(H[:, b, :], PS[:, CX_BANK[b % 8], 0:D], H[:, b, :], ALU.add).then_inc(sem("wo_added"), 1)
                if b and l == 0:
                    v.wait_ge(sem("wo_added"), b)
                    stats(v, b - 1)
            if l == 0:
                v.wait_ge(sem("wo_added"), NB)
                stats(v, NB - 1)

        def router_pe(pe, l, n):
            E = (E0, E1)[l]
            for b in range(NB):
                pe.wait_ge(sem("ln_done"), DC * (b // 4 + 1))
                for k in range(DC):
                    last = pe.matmul(PS[:, 0, b * E:(b + 1) * E], XN[:, k, b * P:(b + 1) * P], wr[l][:, k, :], start=k == 0, stop=k == 1)
            last.then_inc(sem("logits"), 1)
            pe.wait_ge(sem("shifted"), 1)
            pe.matmul(PS[:, 1, 0:P], upper[:, :], SELF[:, :], start=True, stop=True)
            pe.matmul(PS[:, 2, 0:P], ones[:, :], SELF[:, :], start=True, stop=True).then_inc(sem("counted"), 1)
            pe.wait_ge(sem("gates"), 1)
            for b in range(NB):
                last = pe.transpose(PS[0:E, 1 + b // 4, b % 4 * P:(b % 4 + 1) * P], GT[:, b, 0:E], ident[:, :])
                if b % 4 == 3:
                    last.then_inc(sem("gates_turned"), 1)
            for b in range(NB):
                pe.wait_ge(sem("gates_rows"), b // 4 + 1)
                if b >= 3:
                    pe.wait_ge(sem("b2_added"), b - 2)
                pe.matmul(PS[:, 5 + b % 3, 0:D], GTT[0:E, b * P:(b + 1) * P], b2[l][:, :], start=True, stop=True)\
                  .then_inc(sem("b2_weighted"), 1)

        def router_act(act, l):
            act.wait_ge(sem("shifted"), 1)
            if l == 0:
                act.activation(EX[:, :, :], L2[:, :, :], ACT.Exp).then_inc(sem("exp_router"), 1)
            else:
                act.activation(t2[:, :], t2[:, :], ACT.Exp).then_inc(sem("exp_router"), 1)
            for g in range(NG):
                act.wait_ge(sem("gates_turned"), g + 1)
                act.activation(GTT[0:(E0, E1)[l], g * G:(g + 1) * G], PS[0:(E0, E1)[l], 1 + g, :], ACT.Copy)\
                   .then_inc(sem("gates_rows"), 1)

        def router_dve(v, l):
            E, K = (E0, E1)[l], TOPK[l]
            KB = K * NB
            c = Chain(v, sem("router_dve"))
            lg, l2, ex, gt = (x[:, :, 0:E] for x in (LG, L2, EX, GT))
            sel = SELF[:, :].rearrange("p (k b e) -> p k b e", k=K, e=E)
            wide = lambda x: x.unsqueeze(2).broadcast_to([P, NB, E])
            rank = order[:, 0:E].unsqueeze(1).broadcast_to([P, NB, E])

            def largest(m, out_sel):
                c(v.tensor_reduce(m, lg, AX, ALU.max))
                c(v.tensor_tensor(out_sel, lg, wide(m), ALU.is_equal))
                c(v.tensor_tensor(out_sel, out_sel, rank, ALU.mult))
                c(v.tensor_reduce(t3[:, :], out_sel, AX, ALU.max))
                c(v.tensor_tensor(out_sel, rank, wide(t3[:, :]), ALU.is_equal))

            v.wait_ge(sem("logits"), 1)
            o = ROW["bs"] if l == 0 else ROW["gb"]
            c(v.tensor_tensor(lg, PS[:, 0, 0:NB * E].rearrange("p (b e) -> p b e", e=E),
                              rows[:, o:o + E].unsqueeze(1).broadcast_to([P, NB, E]), ALU.add))
            largest(t1[:, :], sel[:, 0])
            if l == 0:
                c(v.tensor_tensor(l2, lg, wide(t1[:, :]), ALU.subtract))
            else:
                c(v.scalar_tensor_tensor(lg, sel[:, 0], -3.0e38, lg, ALU.mult, ALU.add))
                largest(t2[:, :], sel[:, 1])
                c(v.tensor_tensor(t2[:, :], t2[:, :], t1[:, :], ALU.subtract))
            v.nop().then_inc(sem("shifted"), 1)

            v.wait_ge(sem("counted"), 1)
            eb = "p (b e) -> p e b"
            cnt, inc, pos = (x[:, :].rearrange("p (e b) -> p e b", e=E) for x in (CNT, INC, POS))
            te = slice(0, E)
            c(v.tensor_copy(cnt, PS[:, 2, 0:P].rearrange(eb, e=E)))
            c(v.tensor_tensor_scan(INC[:, :], smask[:, l, :], CNT[:, :], 0.0, ALU.mult, ALU.add))
            c(v.tensor_scalar(TI[:, te], inc[:, :, KB - 1], float(R - 1), None, ALU.add))
            c(v.tensor_scalar(TI[:, te], TI[:, te], 8, None, ALU.logical_shift_right))
            c(v.tensor_copy(TF[:, te], TI[:, te]))
            c(v.tensor_tensor_scan(TINC[:, te], ones[:, te], TF[:, te], 0.0, ALU.mult, ALU.add))
            c(v.tensor_tensor(TB[:, te], TINC[:, te], TF[:, te], ALU.subtract))
            c(v.tensor_scalar(TB[:, te], TB[:, te], float(R), None, ALU.mult))
            c(v.tensor_tensor(inc, inc, cnt, ALU.subtract))
            c(v.tensor_tensor(inc, inc, TB[:, te].unsqueeze(2).broadcast_to([P, E, KB]), ALU.add))
            c(v.tensor_tensor(pos, PS[:, 1, 0:P].rearrange(eb, e=E), inc, ALU.add))
            c(v.tensor_tensor(pos, pos, SELF[:, :].rearrange(eb, e=E), ALU.mult))
            c(v.tensor_reduce(SLF[:, 0:KB], POS[:, :].rearrange("p (e b) -> p b e", e=E), AX, ALU.add))
            v.tensor_copy(SLOT[:, 0:KB], SLF[:, 0:KB]).then_inc(sem("slots_ready"), 1)
            nt = NT[l]
            c(v.tensor_tensor(GE[:, 0:nt, te], iota[:, 0:nt].unsqueeze(2).broadcast_to([P, nt, E]),
                              TINC[:, te].unsqueeze(1).broadcast_to([P, nt, E]), ALU.is_ge))
            c(v.tensor_reduce(TEF[:, 0:nt], GE[:, 0:nt, te], AX, ALU.add))
            v.tensor_scalar(TE[:, 0:nt], TEF[:, 0:nt], float(E - 1), None, ALU.min).then_inc(sem("tile_experts"), 1)

            v.wait_ge(sem("exp_router"), 1)
            if l == 0:
                c(v.tensor_reduce(t2[:, :], ex, AX, ALU.add))
                c(v.reciprocal(GK[:, 0, :], t2[:, :]))
                v.tensor_tensor(gt, sel[:, 0], wide(GK[:, 0, :]), ALU.mult).then_inc(sem("gates"), 1)
            else:
                c(v.tensor_scalar(t1[:, :], t2[:, :], 1.0, None, ALU.add))
                c(v.reciprocal(GK[:, 0, :], t1[:, :]))
                c(v.tensor_tensor(GK[:, 1, :], t2[:, :], GK[:, 0, :], ALU.mult))
                c(v.tensor_tensor(ex, sel[:, 1], wide(GK[:, 1, :]), ALU.mult))
                c(v.tensor_tensor(l2, sel[:, 0], wide(GK[:, 0, :]), ALU.mult))
                v.tensor_tensor(gt, ex, l2, ALU.add).then_inc(sem("gates"), 1)
            for b in range(NB):
                v.wait_ge(sem("b2_weighted"), b + 1)
                v.tensor_tensor(H[:, b, :], PS[:, 5 + b % 3, 0:D], H[:, b, :], ALU.add).then_inc(sem("b2_added"), 1)

        def router_pool(pool, l):
            pool.wait_ge(sem("slots_ready"), 1)
            pool.wait_ge(sem("rows_zeroed"), 32)
            for n in range(TOPK[l] * NB):
                pool.indirect_dma_start(XSORT[l], bass.IndirectOffsetOnAxis(ap=SLOT[:, n:n + 1], axis=0), XT[:, n % NB, :], None)\
                    .then_inc(sem(f"scattered{l}"), 16)
            pool.wait_ge(sem(f"scattered{l}"), 16 * TOPK[l] * NB)

        def tile_steps(eng, l, body):
            body(0, 0)
            body(0, 1)
            with eng.Fori(1, (NT[l] - 3) // 2) as i:
                body(i, 0)
                body(i, 1)
            for j in range(NT[l] - 3, NT[l]):
                body((NT[l] - 3) // 2, j - (NT[l] - 3))

        def is0(i, x, below):
            return isinstance(i, int) and 2 * i + x < below

        def there(i, x, l):
            return not isinstance(i, int) or 2 * i + x < NT[l]

        def moe_sp(sp, l, W):
            def expert(i, x):
                at = TE[0:1, 2 * i + x:2 * i + x + 1] if isinstance(i, int) else TE[0:1, bass.ds(2 * i + x, 1)]
                return sp.value_load(at, min_val=0, max_val=(E0, E1)[l] - 1)

            def fetch(dst, a, e, name):
                sp.dma_start(dst, a[bass.ds(e, 1)].rearrange("o p n -> (o p) n")).then_inc(sem(name), 16)

            def first_layer(e, s):
                fetch(W1s[:, s, :, :].rearrange("p k n -> p (k n)"), W[0], e, f"mlp_w{s}")
                fetch(B1s[:, s, :], W[2], e, f"mlp_w{s}")

            def second_layer(e, s):
                fetch(W2s[:, s, :, :].rearrange("p k n -> p (k n)"), W[1], e, f"mlp_v{s}")

            sp.wait_ge(sem("tile_experts"), 1)
            for x in range(2):
                e = expert(0, x)
                first_layer(e, x)
                second_layer(e, x)

            def body(i, x):
                if there(i, x + 2, l):
                    e = expert(i, x + 2)
                    sp.wait_ge(sem("mlp_gelu"), 12 * i + 6 * (x + 1))
                    first_layer(e, x % 2)
                    sp.wait_ge(sem("mlp_down"), 4 * i + 2 * (x + 1))
                    second_layer(e, x % 2)
                sp.wait_ge(sem("y_evac"), 4 * i + 2 * (x + 1))
                if isinstance(i, int):
                    j = 2 * i + x
                    dst = YSORT[l][R * j:R * (j + 1), :]
                else:
                    dst = YSORT[l][bass.ds(2 * R * i + R * x, R), :]
                sp.dma_start(dst.rearrange("(r p) d -> p r d", p=P), YB[:, x % 2, :, :]).then_inc(sem(f"y_stored{x % 2}"), 16)

            tile_steps(sp, l, body)

        def moe_pool(pool, l):
            def load(i, x):
                if isinstance(i, int):
                    j = 2 * i + x
                    src = XSORT[l][R * j:R * (j + 1), :]
                else:
                    src = XSORT[l][bass.ds(2 * R * i + R * x, R), :]
                pool.dma_start(XIN[:, x % 2, :, :], src.rearrange("(r p) d -> p r d", p=P)).then_inc(sem(f"x_loaded{l}_{x % 2}"), 16)

            load(0, 0)
            load(0, 1)

            def body(i, x):
                if there(i, x + 2, l):
                    pool.wait_ge(sem("tile_turned"), 2 * i + x + 1)
                    load(i, x + 2)

            tile_steps(pool, l, body)

        def moe_pe(pe, l):
            def turn(i, x):
                s = x % 2
                pe.wait_ge(sem(f"x_loaded{l}_{s}"), 16 * i + 16 * (x // 2 + 1))
                if not is0(i, x, 2):
                    pe.wait_ge(sem("xt_evac"), 2 * i + x - 1)
                for k in range(DC):
                    for r in range(2):
                        last = pe.transpose(PS[0:DH, s, k * R + r * P:k * R + (r + 1) * P], XIN[:, s, r, k * DH:(k + 1) * DH], ident[:, :])
                last.then_inc(sem("tile_turned"), 1)

            def up(i, x):
                s = x % 2
                pe.wait_ge(sem(f"mlp_w{s}"), 32 * i + 32 * (x // 2 + 1))
                pe.wait_ge(sem("xt_evac"), 2 * i + x + 1)
                for f in range(FC):
                    n = 6 * x + f
                    if not (isinstance(i, int) and 12 * i + n < 4):
                        pe.wait_ge(sem("mlp_gelu"), 12 * i + n - 3)
                    for k in range(DC):
                        last = pe.matmul(PS[:, 2 + n % 4, 0:R], W1s[:, s, k, f * P:(f + 1) * P], XTT[:, s, k, :], start=k == 0, stop=k == 1)
                    last.then_inc(sem("mlp_up"), 1)

            def down(i, x):
                s = x % 2
                pe.wait_ge(sem(f"mlp_v{s}"), 16 * i + 16 * (x // 2 + 1))
                pe.wait_ge(sem("mlp_gelu"), 12 * i + 6 * (x + 1))
                for r in range(2):
                    if not is0(i, x, 1):
                        pe.wait_ge(sem("y_evac"), 4 * i + 2 * x + r - 1)
                    for f in range(FC):
                        last = pe.matmul(PS[:, 6 + r, 0:D], HT[:, s, f, r * P:(r + 1) * P], W2s[:, s, f, :], start=f == 0, stop=f == FC - 1)
                    last.then_inc(sem("mlp_down"), 1)

            pe.wait_ge(sem("gates_rows"), NG)
            pe.wait_ge(sem("b2_added"), NB)
            turn(0, 0)
            turn(0, 1)
            up(0, 0)

            def body(i, x):
                if there(i, x + 2, l):
                    turn(i, x + 2)
                if there(i, x + 1, l):
                    up(i, x + 1)
                down(i, x)

            tile_steps(pe, l, body)

        def moe_act(act, l, gain=None, bias=None):
            def evac(i, x):
                s = x % 2
                act.wait_ge(sem("tile_turned"), 2 * i + x + 1)
                if not is0(i, x, 2):
                    act.wait_ge(sem("mlp_up"), 12 * i + 6 * (x - 1))
                dst, src = XTT[:, s, :, :], PS[0:DH, s, :].rearrange("p (k n) -> p k n", k=DC)
                if gain is None:
                    ins = act.activation(dst, src, ACT.Copy)
                else:
                    for k in range(DC):
                        ins = act.activation(dst[:, k, :], src[:, k, :], ACT.Identity, scale=c96[:, C96[gain] + k:C96[gain] + k + 1],
                                             bias=c96[:, C96[bias] + k:C96[bias] + k + 1])
                ins.then_inc(sem("xt_evac"), 1)

            def gelu(i, x):
                s = x % 2
                if not is0(i, x, 2):
                    act.wait_ge(sem("mlp_down"), 4 * i + 2 * (x - 1))
                for f in range(FC):
                    act.wait_ge(sem("mlp_up"), 12 * i + 6 * x + f + 1)
                    act.activation(HT[:, s, f, 0:R], PS[:, 2 + (6 * x + f) % 4, 0:R], ACT.Gelu, bias=B1s[:, s, f:f + 1])\
                       .then_inc(sem("mlp_gelu"), 1)

            evac(0, 0)
            evac(0, 1)
            gelu(0, 0)

            def body(i, x):
                if there(i, x + 2, l):
                    evac(i, x + 2)
                if there(i, x + 1, l):
                    gelu(i, x + 1)

            tile_steps(act, l, body)

        def moe_dve(v, l):
            def body(i, x):
                s = x % 2
                if not is0(i, x, 2):
                    v.wait_ge(sem(f"y_stored{s}"), 16 * i + 16 * (x // 2))
                for r in range(2):
                    v.wait_ge(sem("mlp_down"), 4 * i + 2 * x + r + 1)
                    v.tensor_copy(YB[:, s, r, :], PS[:, 6 + r, 0:D]).then_inc(sem("y_evac"), 1)

            tile_steps(v, l, body)

        def combine_pool(pool, l):
            pool.wait_ge(sem("y_stored0"), 16 * ((NT[l] + 1) // 2))
            pool.wait_ge(sem("y_stored1"), 16 * (NT[l] // 2))
            for n in range(TOPK[l] * NB):
                pool.indirect_dma_start(YGT[:, n, :], None, YSORT[l], bass.IndirectOffsetOnAxis(ap=SLOT[:, n:n + 1], axis=0))\
                    .then_inc(sem(f"y_gathered{l}_{n // 4}"), 16)

        def combine_dve(v, l):
            for n in range(TOPK[l] * NB):
                k, b = n // NB, n % NB
                v.wait_ge(sem(f"y_gathered{l}_{n // 4}"), 64)
                if k:
                    v.wait_ge(sem("combined"), b + 1)
                v.scalar_tensor_tensor(H[:, b, :], YGT[:, n, :], GK[:, k, b:b + 1], H[:, b, :], ALU.mult, ALU.add).then_inc(sem("combined"), 1)
                if l == 0 and b:
                    v.wait_ge(sem("combined"), b)
                    stats(v, b - 1)
            if l == 0:
                v.wait_ge(sem("combined"), NB)
                stats(v, NB - 1)

        def mlp_sp(sp, W):
            w1, w2, bb1 = W
            sp.dma_start(W1s[:, 0, :, :].rearrange("p k n -> p (k n)"), w1[0]).then_inc(sem("mlp_w0"), 16)
            sp.dma_start(W2s[:, 0, :, :].rearrange("p k n -> p (k n)"), w2[0]).then_inc(sem("mlp_w0"), 16)
            sp.dma_start(B1s[:, 0, :], bb1[0]).then_inc(sem("mlp_w0"), 16)

        def mlp_pe(pe):
            def up(g):
                for f in range(FC):
                    n = FC * g + f
                    pe.wait_ge(sem("x_evac"), max(2 * g + 2, min(n, 3) + 1))
                    if n >= 4:
                        pe.wait_ge(sem("mlp_gelu"), n - 3)
                    for k in range(DC):
                        last = pe.matmul(PS[:, n % 4, :], W1s[:, 0, k, f * P:(f + 1) * P], XN[:, k, g * G:(g + 1) * G],
                                         start=k == 0, stop=k == 1)
                    last.then_inc(sem("mlp_up"), 1)

            def down(g):
                pe.wait_ge(sem("x_evac"), NG * DC)
                pe.wait_ge(sem("mlp_gelu"), FC * (g + 1))
                for q in range(4):
                    b = 4 * g + q
                    if b >= 4:
                        pe.wait_ge(sem("mlp_added"), b - 3)
                    for f in range(FC):
                        last = pe.matmul(PS[:, 4 + q, 0:D], HT[:, g % 2, f, q * P:(q + 1) * P], W2s[:, 0, f, :],
                                         start=f == 0, stop=f == FC - 1)
                    last.then_inc(sem("mlp_down"), 1)

            pe.wait_ge(sem("mlp_w0"), 48)
            up(0)
            for g in range(NG):
                if g < NG - 1:
                    up(g + 1)
                down(g)

        def mlp_act(act):
            for g in range(NG):
                if g >= 2:
                    act.wait_ge(sem("mlp_down"), 4 * (g - 1))
                for f in range(FC):
                    n = FC * g + f
                    act.wait_ge(sem("mlp_up"), n + 1)
                    act.activation(HT[:, g % 2, f, :], PS[:, n % 4, :], ACT.Gelu, bias=B1s[:, 0, f:f + 1]).then_inc(sem("mlp_gelu"), 1)

        def mlp_dve(v):
            v.wait_ge(sem("mlp_b2_added"), 1)
            for b in range(NB):
                v.wait_ge(sem("mlp_down"), b + 1)
                v.tensor_tensor(H[:, b, :], PS[:, 4 + b % 4, 0:D], H[:, b, :], ALU.add).then_inc(sem("mlp_added"), 1)
                if b:
                    v.wait_ge(sem("mlp_added"), b)
                stats(v, b - 1)
            v.wait_ge(sem("mlp_added"), NB)
            stats(v, NB - 1)

        def add_row(pool, row, name, read, count):
            o = ROW[row]
            pool.wait_ge(sem(read), count)
            pool.tensor_tensor(H[:, :, :], H[:, :, :], rows[:, o:o + D].unsqueeze(1).broadcast_to([P, NB, D]), ALU.add)\
                .then_inc(sem(name), 1)

        SCAN = dram("scan_rows", [4, B, NS, S], F32)

        def mamba_pe(pe):
            n = 0
            for g in range(NG):
                for c in range(IC + 1):
                    M = P if c < IC else NS
                    pe.wait_ge(sem("ln_done"), max(2 * g + 2, min(n, 3) + 1))
                    if n >= 4:
                        pe.wait_ge(sem("xz_evac"), n - 3)
                    for k in range(DC):
                        last = pe.matmul(PS[0:M, n % 4, :], w_in[:, k, c * P:c * P + M], XN[:, k, g * G:(g + 1) * G],
                                         start=k == 0, stop=k == 1)
                    last.then_inc(sem("xz_projected"), 1)
                    n += 1
            for g in range(NG):
                pe.wait_ge(sem("silu_done"), 3 * B if g >= 2 else 3)
                for k in range(IC):
                    last = pe.matmul(PS[0:72, 4 + g, :], w_x[:, k, :], XS[:, k, g * G:(g + 1) * G], start=k == 0, stop=k == IC - 1)
                last.then_inc(sem("dbc_projected"), 1)
            pe.wait_ge(sem("weighted_states"), 1)
            for g in range(NG):
                pe.matmul(PS[0:NS, g, :], ssum[:, g // 2, :], UU[:, g % 2 * G:(g % 2 + 1) * G], start=True, stop=True)\
                  .then_inc(sem("ys_summed"), 1)
            for b in range(NB):
                pe.wait_ge(sem("ys_gated"), b // 4 + 1)
                if b >= 4:
                    pe.wait_ge(sem("mamba_added"), b - 3)
                pe.matmul(PS[:, 4 + b % 4, 0:D], YG[:, b * P:(b + 1) * P], w_out[:, :], start=True, stop=True)\
                  .then_inc(sem("mamba_projected"), 1)

        def mamba_act(act):
            n = 0
            act.wait_ge(sem("pads_zeroed"), 1)
            for g in range(NG):
                b, o = g // 2, g % 2 * G
                for c in range(IC + 1):
                    act.wait_ge(sem("xz_projected"), n + 1)
                    if c < IC:
                        ins = act.activation(XC[:, c, b, 3 + o:3 + o + G], PS[:, n % 4, :], ACT.Identity,
                                             bias=c128[:, C128["b_in"] + c:C128["b_in"] + c + 1])
                    else:
                        ins = act.activation(ZT[:, g * G:(g + 1) * G], PS[0:NS, n % 4, :], ACT.Identity, bias=b_z[:, 0:1])
                    ins.then_inc(sem("xz_evac"), 1)
                    n += 1
                if g % 2:
                    act.wait_ge(sem("xz_evac"), n)
                    for c in range(IC):
                        act.activation(XV[:, c, b * S:(b + 1) * S], XC[:, c, b, 0:S], ACT.Identity, scale=conv_w(0, c),
                                       bias=c128[:, C128["conv_b"] + c:C128["conv_b"] + c + 1]).then_inc(sem("first_tap"), 1)
            for b in range(B):
                for c in range(IC):
                    act.wait_ge(sem("conv_done"), 3 * b + c + 1)
                    act.activation(XS[:, c, b * S:(b + 1) * S], XV[:, c, b * S:(b + 1) * S], ACT.Silu).then_inc(sem("silu_done"), 1)
            act.activation(ZS[:, :], ZT[:, :], ACT.Silu).then_inc(sem("z_silu"), 1)
            for b in range(B):
                act.wait_ge(sem("dbc_evac"), 2 * (b + 1))
                act.activation(RT[0:NS, b * S:(b + 1) * S], RT[0:NS, b * S:(b + 1) * S], ACT.Sigmoid, scale=-1.0).then_inc(sem("decay_ready"), 1)
                act.wait_ge(sem("decay_ready"), b + 1)
                act.dma_start(SCAN[0, b], RT[0:NS, b * S:(b + 1) * S]).then_inc(sem("decay_stored"), 16)
            act.wait_ge(sem("decay_stored"), 16 * B)
            spread(act, 0, "decay_loaded")

        def spread(eng, q, name):
            for b in range(B):
                src = SCAN[q, b]
                if q < 3:
                    src = src.unsqueeze(0).broadcast_to([NS, NS, S])
                else:
                    src = src.unsqueeze(1).broadcast_to([NS, NS, S])
                eng.dma_start(REP[q][b * 64:(b + 1) * 64, :], src).then_inc(sem(name), 16)

        def mamba_sp(sp):
            sp.wait_ge(sem("silu_done"), 4)
            for b in range(B):
                sp.dma_start(SCAN[3, b], XS[0:NS, 0, b * S:(b + 1) * S]).then_inc(sem("x_stored"), 16)
            sp.wait_ge(sem("x_stored"), 16 * B)
            spread(sp, 3, "inputs_loaded")
            for b in range(B):
                sp.wait_ge(sem("dbc_evac"), 2 * (b + 1))
                for q in (1, 2):
                    sp.dma_start(SCAN[q, b], RT[32 * q:32 * q + NS, b * S:(b + 1) * S]).then_inc(sem("bc_stored"), 16)
            sp.wait_ge(sem("bc_stored"), 16 * 2 * B)
            spread(sp, 1, "inputs_loaded")
            spread(sp, 2, "c_loaded")

        def conv_w(j, ch):
            return c128[:, C128["conv_w"] + 3 * j + ch:C128["conv_w"] + 3 * j + ch + 1]

        def mamba_dve(v):
            v.memset(XC[:, :, :, 0:3], 0.0).then_inc(sem("pads_zeroed"), 1)
            c = Chain(v, sem("mamba_dve"))
            for b in range(B):
                v.wait_ge(sem("xz_evac"), 8 * (b + 1))
                v.wait_ge(sem("first_tap"), IC * (b + 1))
                for j in range(1, 4):
                    for ch in range(IC):
                        o, x = XV[:, ch, b * S:(b + 1) * S], XC[:, ch, b, j:j + S]
                        ins = v.scalar_tensor_tensor(o, x, conv_w(j, ch), o, ALU.mult, ALU.add)
                        if j == 3:
                            ins.then_inc(sem("conv_done"), 1)
                        elif ch == IC - 1:
                            c(ins)
            for g in range(NG):
                v.wait_ge(sem("dbc_projected"), g + 1)
                v.tensor_scalar(RT[:, g * G:(g + 1) * G], PS[0:72, 4 + g, :], b_x[:, 0:1], None, ALU.add).then_inc(sem("dbc_evac"), 1)
            v.wait_ge(sem("inputs_loaded"), 16 * 2 * B)
            c(v.tensor_tensor(UU[:, :], REP[1][:, :], REP[3][:, :], ALU.mult))
            v.wait_ge(sem("decay_loaded"), 16 * B)
            c(v.tensor_tensor_scan(HH[:, :], REP[0][:, :], UU[:, :], 0.0, ALU.mult, ALU.add))
            v.wait_ge(sem("c_loaded"), 16 * B)
            v.tensor_tensor(UU[:, :], HH[:, :], REP[2][:, :], ALU.mult).then_inc(sem("weighted_states"), 1)
            v.wait_ge(sem("z_silu"), 1)
            for g in range(NG):
                v.wait_ge(sem("ys_summed"), g + 1)
                v.tensor_tensor(YG[:, g * G:(g + 1) * G], PS[0:NS, g, :], ZS[:, g * G:(g + 1) * G], ALU.mult).then_inc(sem("ys_gated"), 1)
            v.wait_ge(sem("b_out_added"), 1)
            for b in range(NB):
                v.wait_ge(sem("mamba_projected"), b + 1)
                v.tensor_tensor(H[:, b, :], PS[:, 4 + b % 4, 0:D], H[:, b, :], ALU.add).then_inc(sem("mamba_added"), 1)
                if b:
                    v.wait_ge(sem("mamba_added"), b)
                    stats(v, b - 1)
            v.wait_ge(sem("mamba_added"), NB)
            stats(v, NB - 1)

        def store_sp(sp):
            for g in range(NG):
                sp.wait_ge(sem("combined"), NB + 4 * (g + 1))
                sp.dma_start(out[g * G:(g + 1) * G].rearrange("(b p) d -> p b d", p=P), H[:, 4 * g:4 * g + 4, :]).then_inc(sem("stored"), 16)
            sp.wait_ge(sem("stored"), 16 * NG)

        MEET = None

        def plan(name, eng):
            k = 0
            for n, ph in enumerate(PHASES):
                if ph is MEET:
                    k += 1
                    barrier(eng, k)
                    continue
                if name in ph:
                    ph[name](eng)
                if n < len(PHASES) - 1 and PHASES[n + 1] is not MEET:
                    eng.drain()

        H_KEPT = dram("h_kept", [P, NB * D], F32)
        HK = at([P, NB, D], F32, 4096)

        def keep_sp(sp):
            sp.dma_start(H_KEPT, H[:, :, :].rearrange("p b d -> p (b d)")).then_inc(sem("h_kept"), 16)
            sp.wait_ge(sem("h_kept"), 16)

        def norm_dve(v):
            c = Chain(v, sem("norm_in_place"))
            v.wait_ge(sem("blocks_seen"), NB * BEFORE["again"])
            for b in range(NB):
                last = v.bn_aggr(MV[:, b, :], ST[:, b, :])
            last.then_inc(sem("norm_var"), 1)
            v.wait_ge(sem("norm_root"), 1)
            c(v.reciprocal(RI[:, :], RS[:, :]))
            v.wait_ge(sem("h_kept"), 16)
            for b in range(NB):
                v.tensor_scalar(H[:, b, :], H[:, b, :], MV[:, b, 0:1], RI[:, b:b + 1], ALU.subtract, ALU.mult)\
                 .then_inc(sem("H_normed"), 1)
                if b:
                    v.wait_ge(sem("H_normed"), b)
                stats(v, b - 1)
            v.wait_ge(sem("H_normed"), NB)
            stats(v, NB - 1)

        def norm_act(act):
            act.wait_ge(sem("norm_var"), 1)
            act.activation(RS[:, :], MV[:, :, 1], ACT.Sqrt, bias=epsc[:, 0:1]).then_inc(sem("norm_root"), 1)

        def last_sp(sp):
            sp.dma_start(HK[:, :, :].rearrange("p b d -> p (b d)"), H_KEPT).then_inc(sem("h_back"), 16)

        def last_dve(v):
            v.wait_ge(sem("h_back"), 16)
            v.tensor_tensor(H[:, :, :], H[:, :, :], HK[:, :, :], ALU.add)

        def turn_pe(pe):
            for j in range(NG * DC):
                g, k = j // DC, j % DC
                for q in range(4):
                    b = 4 * g + q
                    last = pe.transpose(PS[0:DH, j, q * P:(q + 1) * P], H[:, b, k * DH:(k + 1) * DH], ident[:, :])
                last.then_inc(sem("x_turned"), 1)

        def turn_act(act):
            for j in range(NG * DC):
                g, k = j // DC, j % DC
                act.wait_ge(sem("x_turned"), j + 1)
                act.activation(XN[:, k, g * G:(g + 1) * G], PS[0:DH, j, :], ACT.Copy).then_inc(sem("x_evac"), 1)

        def ln(n, gain=None, bias=None):
            return dict(pe=lambda e: ln_pe(e, n), act=lambda e: ln_act(e, n, gain, bias), dve=lambda e: ln_dve(e, n))

        def router(l, n):
            return dict(pe=lambda e: router_pe(e, l, n), act=lambda e: router_act(e, l), dve=lambda e: router_dve(e, l),
                        pool=lambda e: router_pool(e, l))

        def experts(l, nm, gain=None, bias=None):
            return [dict(pe=lambda e: moe_pe(e, l), act=lambda e: moe_act(e, l, gain, bias), dve=lambda e: moe_dve(e, l),
                         pool=lambda e: moe_pool(e, l), sp=lambda e: moe_sp(e, l, [A[f"{nm}_{k}"] for k in ("w1", "w2", "b1")])),
                    dict(pool=lambda e: combine_pool(e, l), dve=lambda e: combine_dve(e, l))]

        def attention(l, n=0, gain=None, bias=None):
            return [
                ln(n, gain, bias),
                dict(pe=lambda e: qkv_pe(e, l, n), act=lambda e: qkv_act(e, l), dve=lambda e: qkv_dve(e, l),
                     pool=lambda e: qkv_pool(e, l), sp=lambda e: qkv_sp(e, l)),
                dict(pe=lambda e: attn_pe(e, l), act=lambda e: attn_act(e, l), dve=lambda e: attn_dve(e, l),
                     pool=lambda e: attn_pool(e, l), sp=lambda e: attn_sp(e, l)),
                dict(pe=lambda e: wo_pe(e, l), act=lambda e: wo_act(e, l), dve=lambda e: wo_dve(e, l)),
            ]

        moe1, combine1 = experts(1, "moe1", "ln2_g", "ln2_b")
        PHASES = [
            dict(sp=embed_sp, dve=embed_dve, pool=embed_pool, pe=embed_pe, act=embed_act),
            *attention(0),
            *clear(1), ln(1), router(0, 1),
            *experts(0, "moe0"),
            *clear(2), ln(2),
            dict(pe=mamba_pe, act=mamba_act, sp=mamba_sp, dve=mamba_dve, pool=lambda e: add_row(e, "b_out", "b_out_added", "ln_scaled", NB)),
            *clear(3), dict(sp=keep_sp, dve=norm_dve, act=norm_act), *attention(1, 3, "ln1_g", "ln1_b"),
            *clear(4), dict(pe=turn_pe, act=turn_act),
            dict(pe=mlp_pe, act=mlp_act, dve=mlp_dve,
                 pool=lambda e: add_row(e, "mlp_b2", "mlp_b2_added", "x_turned", NG * DC),
                 sp=lambda e: mlp_sp(e, [A[f"mlp_{k}"] for k in ("w1", "w2", "b1")])),
            *clear(5), ln(4, "ln2_g", "ln2_b"), router(1, 4),
            moe1, dict(sp=last_sp, dve=last_dve), combine1,
        ]

        @block.sync
        def _(sp):
            plan("sp", sp)
            store_sp(sp)

        @block.gpsimd
        def _(pool):
            plan("pool", pool)

        @block.scalar
        def _(act):
            plan("act", act)

        @block.tensor
        def _(pe):
            plan("pe", pe)

        @block.vector
        def _(v):
            plan("dve", v)


def kernel(**inputs):
    import numpy as np
    import concourse.bacc as bacc
    from concourse.bass_utils import run_bass_kernel_spmd as run

    w = {k: np.asarray(v) for k, v in inputs.items()}

    def chunk(a, n):
        return np.ascontiguousarray(a.reshape(-1, n, a.shape[-1]).transpose(1, 0, 2))

    def col(a, n):
        return a.reshape(-1, n).T

    v96 = {"bq0": w["L0_attn_bq"], "bk0": w["L0_attn_bk"], "ln1_g": w["L1_ffn_ln1_g"], "ln1_b": w["L1_ffn_ln1_b"],
           "bq1": w["L1_ffn_in_b"][0:D], "bk1": w["L1_ffn_in_b"][D:2 * D], "ln2_g": w["L1_ffn_ln2_g"], "ln2_b": w["L1_ffn_ln2_b"]}
    v128 = [w["L1_attn_b_in"][0:DI], w["L1_attn_conv_b"], np.ascontiguousarray(w["L1_attn_conv_w"][:, 0, :].T), w["L1_ffn_mlp_b1"]]

    row = np.concatenate([w["L0_attn_bv"].reshape(-1), w["L1_ffn_in_b"][2 * D:], w["L0_attn_bo"], w["L1_ffn_out_b"],
                          w["L1_attn_b_out"], w["L1_ffn_mlp_b2"], w["L0_tok_norm_w"], w["L0_ffn_bs"], w["L1_ffn_gate_b"]])
    arrays = {
        "x": np.ascontiguousarray(w["x"].reshape(NB, P).T),
        "coords": w["L0_tok_basin_coords"],
        "c96": np.ascontiguousarray(np.concatenate([col(v96[k], DH) for k in C96], 1)),
        "c128": np.ascontiguousarray(np.concatenate([col(v, P) for v in v128], 1)),
        "rows": np.ascontiguousarray(np.broadcast_to(row, (P, NROW))),
        "ident": np.eye(P, dtype=np.float32),
        "projT": np.ascontiguousarray(w["L0_tok_proj_w"].T),
        "wqkv0": chunk(np.concatenate([w[f"L0_attn_W{n}"].reshape(D, D) for n in "qkv"], 1), DH),
        "wo0": chunk(w["L0_attn_Wo"].reshape(D, D), DH),
        "wqkv1": chunk(np.ascontiguousarray(w["L1_ffn_in_w"].T), DH),
        "wo1": chunk(np.ascontiguousarray(w["L1_ffn_out_w"].T), DH),
    }
    def experts(nm, w1, b1, w2):
        E = w1.shape[0]
        arrays[f"{nm}_w1"] = np.ascontiguousarray(w1.reshape(E, DC, DH, FF).transpose(0, 2, 1, 3).reshape(E, DH, DC * FF))
        arrays[f"{nm}_w2"] = np.ascontiguousarray(w2.reshape(E, FC, P, D).transpose(0, 2, 1, 3).reshape(E, P, FC * D))
        arrays[f"{nm}_b1"] = np.ascontiguousarray(b1.reshape(E, FC, P).transpose(0, 2, 1))

    experts("moe0", w["L0_ffn_W1"], w["L0_ffn_b1"], w["L0_ffn_W2"])
    experts("moe1", w["L1_ffn_exp_w1"], w["L1_ffn_exp_b1"], w["L1_ffn_exp_w2"])
    experts("mlp", w["L1_ffn_mlp_w1"][None], w["L1_ffn_mlp_b1"][None], w["L1_ffn_mlp_w2"][None])
    arrays["wr0"] = chunk(w["L0_ffn_Ws"], DH)
    arrays["wr1"] = chunk(np.ascontiguousarray(w["L1_ffn_gate_w"].T), DH)
    arrays["b20"] = w["L0_ffn_b2"]
    arrays["b21"] = w["L1_ffn_exp_b2"]
    join = np.zeros((P, NO), np.float32)
    for n in range(32):
        join[n, n] = join[32 + n, n] = 1.0
    join[64, 32] = join[80, 33] = 1.0
    arrays["join"] = join
    arrays["upper"] = np.triu(np.ones((P, P), np.float32), 1)
    arrays["ones"] = np.ones((P, P), np.float32)
    smask = np.ones((P, 2, P), np.float32)
    for l, E in enumerate((E0, E1)):
        smask[:, l, ::P // E] = 0.0
    arrays["smask"] = smask
    arrays["iota"] = np.ascontiguousarray(np.broadcast_to(np.arange(max(NT), dtype=np.float32), (P, max(NT))))
    arrays["order"] = np.ascontiguousarray(np.broadcast_to(np.arange(E0, 0, -1, dtype=np.float32), (P, E0)))
    arrays["w_in"] = chunk(w["L1_attn_W_in"][:, 0:DI + NS], DH)
    w_x = np.zeros((DI, 72), np.float32)
    b_x = np.zeros((72, 1), np.float32)
    w_x[:, 0:NS] = w["L1_attn_W_dt"][:, 0:NS]
    b_x[0:NS, 0] = w["L1_attn_b_dt"][0:NS]
    for q in range(2):
        w_x[:, 32 * (q + 1):32 * (q + 1) + NS] = w["L1_attn_W_x"][:, (2 + q) * NS:(3 + q) * NS]
        b_x[32 * (q + 1):32 * (q + 1) + NS, 0] = w["L1_attn_b_x"][(2 + q) * NS:(3 + q) * NS]
    arrays["w_x"] = chunk(w_x, P)
    arrays["b_x"] = b_x
    arrays["b_z"] = np.ascontiguousarray(w["L1_attn_b_in"][DI:DI + NS, None])
    arrays["w_out"] = np.ascontiguousarray(w["L1_attn_W_out"][0:NS])
    ssum = np.zeros((P, 2, NS), np.float32)
    for p in range(P):
        ssum[p, p // 64, p % 64 // NS] = 1.0
    arrays["ssum"] = ssum
    nc = bacc.Bacc("TRN2", target_bir_lowering=False, num_devices=1)
    A = {k: nc.dram_tensor(f"in_{k}", a.shape, mybir.dt.from_np(a.dtype), kind="ExternalInput").ap() for k, a in arrays.items()}
    out = nc.dram_tensor("out", (T, D), F32, kind="ExternalOutput").ap()
    build(nc, A, out)
    r = run(nc, [{f"in_{k}": a for k, a in arrays.items()}], core_ids=[0])
    y = r.results[0]["out"]
    return y.reshape(B, S, D)
```
